# Optimizing a Trainium2 kernel written in Bass

```python
import numpy as np
import jax
import jax.numpy as jnp

def _softmax(x, axis=-1):
    return jax.nn.softmax(x, axis=axis)

def _gelu(x):
    return jax.nn.gelu(x, approximate=True)

def _silu(x):
    return jax.nn.silu(x)

def _sigmoid(x):
    return jax.nn.sigmoid(x)

def _layernorm(x, axis=-1, eps=1e-05):
    m = jnp.mean(x, axis=axis, keepdims=True)
    v = jnp.var(x, axis=axis, keepdims=True)
    return (x - m) / jnp.sqrt(v + eps)

def _scatter_add(tgt, idx, src, axis=0):
    return tgt.at[idx].add(src)

def _segment_sum(src, seg, n):
    return jax.ops.segment_sum(src, seg, n)
kernel_name = 'mk_cond_seq_d4_seqx_r8_fef06b'

def setup_inputs(seed: int=0):
    np.random.seed(seed)
    _w = jnp.asarray

    def _rec_inputs():
        import jax
        import jax.numpy as jnp
        _rk = jax.random.key(seed)
        x = 7.22e-05 + 1 * jax.random.normal(jax.random.fold_in(_rk, 1), (64, 32, 128), jnp.float32)
        _lenS = 32 - jax.random.randint(jax.random.fold_in(_rk, 7), (64,), 0, max(1, 32 // 4) + 1, jnp.int32)
        _lenS2 = 32 - jax.random.randint(jax.random.fold_in(_rk, 8), (64,), 0, max(1, 32 // 4) + 1, jnp.int32)
        condB_gatescore = jax.random.uniform(jax.random.fold_in(_rk, 11), (64,), jnp.float32, 0.0, 0.581427)
        itok_B_34_63 = jax.random.randint(jax.random.fold_in(_rk, 13), (64,), 34, 64, jnp.int32)
        fside_Bx16xSxS_0 = -1.47943e-05 + 1.00017 * jax.random.normal(jax.random.fold_in(_rk, 14), (64, 16, 32, 32), jnp.float32)
        condB_theta = jax.random.uniform(jax.random.fold_in(_rk, 15), (64,), jnp.float32, 0.0, 0.983423)
        condB_phi = jax.random.uniform(jax.random.fold_in(_rk, 16), (64,), jnp.float32, 0.0, 0.961312)
        itok_B_0_15 = jax.random.randint(jax.random.fold_in(_rk, 17), (64,), 0, 16, jnp.int32)
        _validS = jnp.arange(32)[None, :] < _lenS[:, None]
        _validS2 = jnp.arange(32)[None, :] < _lenS2[:, None]
        _causal = jnp.tril(jnp.ones((32, 32), dtype=bool))
        mask_Bx1xSxS_bk0 = jnp.logical_not(jnp.broadcast_to(_validS[:, None, None, :], (64, 1, 32, 32)))
        return (x, condB_gatescore, itok_B_34_63, fside_Bx16xSxS_0, condB_theta, condB_phi, itok_B_0_15, mask_Bx1xSxS_bk0)
    x, condB_gatescore, itok_B_34_63, fside_Bx16xSxS_0, condB_theta, condB_phi, itok_B_0_15, mask_Bx1xSxS_bk0 = _rec_inputs()

    def _L0_cond_setup():
        import jax, jax.numpy as jnp
        import numpy as np
        D_MODEL = 128
        N_HEADS = 16
        D_HEAD = D_MODEL // N_HEADS
        D_FF = 512
        EPS = 1e-05

        def layernorm(x, gamma, beta):
            mu = jnp.mean(x, axis=-1, keepdims=True)
            var = jnp.var(x, axis=-1, keepdims=True)
            return (x - mu) * jax.lax.rsqrt(var + EPS) * gamma + beta
        key = jax.random.key(seed)
        ks = jax.random.split(key, 16)
        B, T = (4, 256)
        s = 1.0 / np.sqrt(D_MODEL)
        sf = 1.0 / np.sqrt(D_FF)
        return {'x': jax.random.normal(ks[0], (B, T, D_MODEL), jnp.float32), 'gate_score': jax.random.uniform(ks[1], (B,), jnp.float32), 'Wq': jax.random.normal(ks[2], (D_MODEL, D_MODEL), jnp.float32) * s, 'bq': jnp.zeros((D_MODEL,), jnp.float32), 'Wk': jax.random.normal(ks[3], (D_MODEL, D_MODEL), jnp.float32) * s, 'bk': jnp.zeros((D_MODEL,), jnp.float32), 'Wv': jax.random.normal(ks[4], (D_MODEL, D_MODEL), jnp.float32) * s, 'bv': jnp.zeros((D_MODEL,), jnp.float32), 'Wo': jax.random.normal(ks[5], (D_MODEL, D_MODEL), jnp.float32) * s, 'bo': jnp.zeros((D_MODEL,), jnp.float32), 'W1': jax.random.normal(ks[6], (D_MODEL, D_FF), jnp.float32) * s, 'b1': jnp.zeros((D_FF,), jnp.float32), 'W2': jax.random.normal(ks[7], (D_FF, D_MODEL), jnp.float32) * sf, 'b2': jnp.zeros((D_MODEL,), jnp.float32), 'gamma1': jnp.ones((D_MODEL,), jnp.float32), 'beta1': jnp.zeros((D_MODEL,), jnp.float32), 'gamma2': jnp.ones((D_MODEL,), jnp.float32), 'beta2': jnp.zeros((D_MODEL,), jnp.float32)}
    _L0_cond_all = _L0_cond_setup()
    _L0_cond_in = {k: v for k, v in _L0_cond_all.items() if k in ('Wq', 'bq', 'Wk', 'bk', 'Wv', 'bv', 'Wo', 'bo', 'W1', 'b1', 'W2', 'b2', 'gamma1', 'beta1', 'gamma2', 'beta2')}
    del _L0_cond_all

    def _L1_cond_setup():
        import jax, jax.numpy as jnp
        import numpy as np
        import math
        D_MODEL = 128
        N_HEAD = 16
        HEAD_DIM = D_MODEL // N_HEAD
        D_FF = 512
        NUM_STEPS = 100.0
        RESCALE = 4000.0
        EPS = 1e-05

        def _sin_emb(t):
            half = D_MODEL // 2
            x = t.astype(jnp.float32) / NUM_STEPS * RESCALE
            freqs = jnp.exp(jnp.arange(half, dtype=jnp.float32) * (-math.log(10000.0) / (half - 1)))
            e = x[:, None] * freqs[None, :]
            return jnp.concatenate([jnp.sin(e), jnp.cos(e)], axis=-1)

        def _ln(x):
            m = jnp.mean(x, axis=-1, keepdims=True)
            v = jnp.var(x, axis=-1, keepdims=True)
            return (x - m) / jnp.sqrt(v + EPS)

        def _gelu2(x):
            return x * jax.nn.sigmoid(1.702 * x)
        key = jax.random.key(seed)
        ks = jax.random.split(key, 24)
        B, S, D, F = (4, 64, D_MODEL, D_FF)
        std = 0.02
        inp = {'src': jax.random.normal(ks[0], (B, S, D), dtype=jnp.float32), 'src_mask': jax.random.randint(ks[1], (B, 1, S, S), 0, 2).astype(bool), 'timestep': jax.random.randint(ks[2], (B,), 0, 100, dtype=jnp.int32), 'attention_bias': jax.random.normal(ks[3], (B, N_HEAD, S, S), dtype=jnp.float32), 'W_ada': jax.random.normal(ks[4], (D, 2 * D), dtype=jnp.float32) * std, 'b_ada': jnp.zeros((2 * D,), dtype=jnp.float32), 'Wq': jax.random.normal(ks[5], (D, D), dtype=jnp.float32) * std, 'bq': jnp.zeros((D,), dtype=jnp.float32), 'Wk': jax.random.normal(ks[6], (D, D), dtype=jnp.float32) * std, 'bk': jnp.zeros((D,), dtype=jnp.float32), 'Wv': jax.random.normal(ks[7], (D, D), dtype=jnp.float32) * std, 'bv': jnp.zeros((D,), dtype=jnp.float32), 'Wo': jax.random.normal(ks[8], (D, D), dtype=jnp.float32) * std, 'bo': jnp.zeros((D,), dtype=jnp.float32), 'W1': jax.random.normal(ks[9], (D, F), dtype=jnp.float32) * std, 'b1': jnp.zeros((F,), dtype=jnp.float32), 'W2': jax.random.normal(ks[10], (F, D), dtype=jnp.float32) * std, 'b2': jnp.zeros((D,), dtype=jnp.float32), 'g2': jnp.ones((D,), dtype=jnp.float32), 'beta2': jnp.zeros((D,), dtype=jnp.float32)}
        return inp
    _L1_cond_all = _L1_cond_setup()
    _L1_cond_in = {k: v for k, v in _L1_cond_all.items() if k in ('W_ada', 'b_ada', 'Wq', 'bq', 'Wk', 'bk', 'Wv', 'bv', 'Wo', 'bo', 'W1', 'b1', 'W2', 'b2', 'g2', 'beta2')}
    del _L1_cond_all

    def _L2_cond_setup():
        import jax, jax.numpy as jnp
        import numpy as np
        key = jax.random.key(seed)
        k1, k2, k3 = jax.random.split(key, 3)
        B, N, D = (16, 512, 128)
        embeddings = jax.random.normal(k1, (B, N, D), dtype=jnp.float32)
        theta = jax.random.uniform(k2, (B,), dtype=jnp.float32)
        phi = jax.random.uniform(k3, (B,), dtype=jnp.float32)
        return {'embeddings': embeddings, 'theta': theta, 'phi': phi}
    _L2_cond_all = _L2_cond_setup()
    _L2_cond_in = {k: v for k, v in _L2_cond_all.items() if k in ()}
    del _L2_cond_all

    def _L3_cond_setup():
        import jax, jax.numpy as jnp
        import numpy as np
        B, S, D = (32, 128, 128)
        A = 32
        E = 16
        LN_EPS = 1e-05
        key = jax.random.key(seed)
        ks = jax.random.split(key, 10)
        s = lambda fan_in: 1.0 / np.sqrt(fan_in)
        return {'hidden_states': jax.random.normal(ks[0], (B, S, D), dtype=jnp.float32), 'domain_id': jax.random.randint(ks[1], (B,), 0, E, dtype=jnp.int64), 'down_W': jax.random.uniform(ks[2], (A, D), jnp.float32, -s(D), s(D)), 'down_b': jax.random.uniform(ks[3], (A,), jnp.float32, -s(D), s(D)), 'up_W': jax.random.uniform(ks[4], (D, A), jnp.float32, -s(A), s(A)), 'up_b': jax.random.uniform(ks[5], (D,), jnp.float32, -s(A), s(A)), 'expert_W': jax.random.uniform(ks[6], (E, A, A), jnp.float32, -s(A), s(A)), 'expert_b': jax.random.uniform(ks[7], (E, A), jnp.float32, -s(A), s(A)), 'domain_emb': jax.random.normal(ks[8], (E, A), dtype=jnp.float32), 'ln_gamma': jnp.ones((D,), jnp.float32), 'ln_beta': jnp.zeros((D,), jnp.float32)}
    _L3_cond_all = _L3_cond_setup()
    _L3_cond_in = {k: v for k, v in _L3_cond_all.items() if k in ('down_W', 'down_b', 'up_W', 'up_b', 'expert_W', 'expert_b', 'domain_emb', 'ln_gamma', 'ln_beta')}
    del _L3_cond_all
    return {'x': x, 'condB_gatescore': condB_gatescore, 'itok_B_34_63': itok_B_34_63, 'fside_Bx16xSxS_0': fside_Bx16xSxS_0, 'condB_theta': condB_theta, 'condB_phi': condB_phi, 'itok_B_0_15': itok_B_0_15, 'mask_Bx1xSxS_bk0': mask_Bx1xSxS_bk0, 'L0_cond_Wq': _L0_cond_in['Wq'], 'L0_cond_bq': _L0_cond_in['bq'], 'L0_cond_Wk': _L0_cond_in['Wk'], 'L0_cond_bk': _L0_cond_in['bk'], 'L0_cond_Wv': _L0_cond_in['Wv'], 'L0_cond_bv': _L0_cond_in['bv'], 'L0_cond_Wo': _L0_cond_in['Wo'], 'L0_cond_bo': _L0_cond_in['bo'], 'L0_cond_W1': _L0_cond_in['W1'], 'L0_cond_b1': _L0_cond_in['b1'], 'L0_cond_W2': _L0_cond_in['W2'], 'L0_cond_b2': _L0_cond_in['b2'], 'L0_cond_gamma1': _L0_cond_in['gamma1'], 'L0_cond_beta1': _L0_cond_in['beta1'], 'L0_cond_gamma2': _L0_cond_in['gamma2'], 'L0_cond_beta2': _L0_cond_in['beta2'], 'L1_cond_W_ada': _L1_cond_in['W_ada'], 'L1_cond_b_ada': _L1_cond_in['b_ada'], 'L1_cond_Wq': _L1_cond_in['Wq'], 'L1_cond_bq': _L1_cond_in['bq'], 'L1_cond_Wk': _L1_cond_in['Wk'], 'L1_cond_bk': _L1_cond_in['bk'], 'L1_cond_Wv': _L1_cond_in['Wv'], 'L1_cond_bv': _L1_cond_in['bv'], 'L1_cond_Wo': _L1_cond_in['Wo'], 'L1_cond_bo': _L1_cond_in['bo'], 'L1_cond_W1': _L1_cond_in['W1'], 'L1_cond_b1': _L1_cond_in['b1'], 'L1_cond_W2': _L1_cond_in['W2'], 'L1_cond_b2': _L1_cond_in['b2'], 'L1_cond_g2': _L1_cond_in['g2'], 'L1_cond_beta2': _L1_cond_in['beta2'], 'L3_cond_down_W': _L3_cond_in['down_W'], 'L3_cond_down_b': _L3_cond_in['down_b'], 'L3_cond_up_W': _L3_cond_in['up_W'], 'L3_cond_up_b': _L3_cond_in['up_b'], 'L3_cond_expert_W': _L3_cond_in['expert_W'], 'L3_cond_expert_b': _L3_cond_in['expert_b'], 'L3_cond_domain_emb': _L3_cond_in['domain_emb'], 'L3_cond_ln_gamma': _L3_cond_in['ln_gamma'], 'L3_cond_ln_beta': _L3_cond_in['ln_beta']}

def reference(x, condB_gatescore, itok_B_34_63, fside_Bx16xSxS_0, condB_theta, condB_phi, itok_B_0_15, mask_Bx1xSxS_bk0, L0_cond_Wq, L0_cond_bq, L0_cond_Wk, L0_cond_bk, L0_cond_Wv, L0_cond_bv, L0_cond_Wo, L0_cond_bo, L0_cond_W1, L0_cond_b1, L0_cond_W2, L0_cond_b2, L0_cond_gamma1, L0_cond_beta1, L0_cond_gamma2, L0_cond_beta2, L1_cond_W_ada, L1_cond_b_ada, L1_cond_Wq, L1_cond_bq, L1_cond_Wk, L1_cond_bk, L1_cond_Wv, L1_cond_bv, L1_cond_Wo, L1_cond_bo, L1_cond_W1, L1_cond_b1, L1_cond_W2, L1_cond_b2, L1_cond_g2, L1_cond_beta2, L3_cond_down_W, L3_cond_down_b, L3_cond_up_W, L3_cond_up_b, L3_cond_expert_W, L3_cond_expert_b, L3_cond_domain_emb, L3_cond_ln_gamma, L3_cond_ln_beta):
    import jax
    import jax.numpy as jnp

    def _L0_cond_ref(x, gate_score, Wq, bq, Wk, bk, Wv, bv, Wo, bo, W1, b1, W2, b2, gamma1, beta1, gamma2, beta2):
        import jax, jax.numpy as jnp
        import numpy as np
        D_MODEL = 128
        N_HEADS = 16
        D_HEAD = D_MODEL // N_HEADS
        D_FF = 512
        EPS = 1e-05

        def layernorm(x, gamma, beta):
            mu = jnp.mean(x, axis=-1, keepdims=True)
            var = jnp.var(x, axis=-1, keepdims=True)
            return (x - mu) * jax.lax.rsqrt(var + EPS) * gamma + beta
        B, T, C = x.shape
        h = layernorm(x, gamma1, beta1)
        Q = (h @ Wq + bq).reshape(B, T, N_HEADS, D_HEAD).transpose(0, 2, 1, 3)
        K = (h @ Wk + bk).reshape(B, T, N_HEADS, D_HEAD).transpose(0, 2, 1, 3)
        V = (h @ Wv + bv).reshape(B, T, N_HEADS, D_HEAD).transpose(0, 2, 1, 3)
        scores = jnp.einsum('bhqd,bhkd->bhqk', Q, K) / np.sqrt(D_HEAD)
        causal = jnp.tril(jnp.ones((T, T), dtype=bool))
        scores = jnp.where(causal, scores, -jnp.inf)
        attn = jax.nn.softmax(scores, axis=-1)
        ctx = jnp.einsum('bhqk,bhkd->bhqd', attn, V)
        ctx = ctx.transpose(0, 2, 1, 3).reshape(B, T, C)
        attn_out = ctx @ Wo + bo
        x1 = x + attn_out
        h2 = layernorm(x1, gamma2, beta2)
        ff = jax.nn.gelu(h2 @ W1 + b1, approximate=False) @ W2 + b2
        x2 = x1 + ff
        g = gate_score[:, None, None]
        return x + g * (x2 - x)

    def _L1_cond_ref(src, src_mask, timestep, attention_bias, W_ada, b_ada, Wq, bq, Wk, bk, Wv, bv, Wo, bo, W1, b1, W2, b2, g2, beta2):
        import jax, jax.numpy as jnp
        import numpy as np
        import math
        D_MODEL = 128
        N_HEAD = 16
        HEAD_DIM = D_MODEL // N_HEAD
        D_FF = 512
        NUM_STEPS = 100.0
        RESCALE = 4000.0
        EPS = 1e-05

        def _sin_emb(t):
            half = D_MODEL // 2
            x = t.astype(jnp.float32) / NUM_STEPS * RESCALE
            freqs = jnp.exp(jnp.arange(half, dtype=jnp.float32) * (-math.log(10000.0) / (half - 1)))
            e = x[:, None] * freqs[None, :]
            return jnp.concatenate([jnp.sin(e), jnp.cos(e)], axis=-1)

        def _ln(x):
            m = jnp.mean(x, axis=-1, keepdims=True)
            v = jnp.var(x, axis=-1, keepdims=True)
            return (x - m) / jnp.sqrt(v + EPS)

        def _gelu2(x):
            return x * jax.nn.sigmoid(1.702 * x)
        B, S, D = src.shape
        emb = jax.nn.silu(_sin_emb(timestep)) @ W_ada + b_ada
        scale, shift = jnp.split(emb[:, None, :], 2, axis=-1)
        x = _ln(src) * (1.0 + scale) + shift
        q = (x @ Wq + bq).reshape(B, S, N_HEAD, HEAD_DIM).transpose(0, 2, 1, 3)
        k = (x @ Wk + bk).reshape(B, S, N_HEAD, HEAD_DIM).transpose(0, 2, 1, 3)
        v = (x @ Wv + bv).reshape(B, S, N_HEAD, HEAD_DIM).transpose(0, 2, 1, 3)
        scores = jnp.einsum('bhqd,bhkd->bhqk', q / math.sqrt(HEAD_DIM), k)
        scores = scores + attention_bias
        scores = jnp.where(src_mask, -jnp.inf, scores.astype(jnp.float32))
        probs = jax.nn.softmax(scores, axis=-1).astype(v.dtype)
        ctx = jnp.einsum('bhqk,bhkd->bhqd', probs, v)
        ctx = ctx.transpose(0, 2, 1, 3).reshape(B, S, D)
        x = x + (ctx @ Wo + bo)
        h = _ln(x) * g2 + beta2
        ff = _gelu2(h @ W1 + b1) @ W2 + b2
        return x + ff

    def _L2_cond_ref(embeddings, theta, phi):
        import jax, jax.numpy as jnp
        import numpy as np
        B, N, D = embeddings.shape
        e = embeddings.reshape(B, N, D // 4, 4)
        ct = jnp.cos(theta)[:, None, None]
        st = jnp.sin(theta)[:, None, None]
        cp = jnp.cos(phi)[:, None, None]
        sp = jnp.sin(phi)[:, None, None]
        x0, x1, x2, x3 = (e[..., 0], e[..., 1], e[..., 2], e[..., 3])
        out = jnp.stack([x0 * ct + x1 * st, -x0 * st + x1 * ct, x2 * cp + x3 * sp, -x2 * sp + x3 * cp], axis=-1)
        return out.reshape(B, N, D)

    def _L3_cond_ref(hidden_states, domain_id, down_W, down_b, up_W, up_b, expert_W, expert_b, domain_emb, ln_gamma, ln_beta):
        import jax, jax.numpy as jnp
        import numpy as np
        B, S, D = (32, 128, 128)
        A = 32
        E = 16
        LN_EPS = 1e-05
        residual = hidden_states
        hidden = jnp.einsum('bsd,ad->bsa', hidden_states, down_W) + down_b
        hidden = jax.nn.gelu(hidden, approximate=False)
        valid = (domain_id >= 0) & (domain_id < E)
        idx = jnp.clip(domain_id, 0, E - 1)
        Wsel = expert_W[idx]
        bsel = expert_b[idx]
        expert_out = jnp.einsum('bsa,boa->bso', hidden, Wsel) + bsel[:, None, :]
        domain_output = jnp.where(valid[:, None, None], expert_out, hidden)
        hidden = domain_output + domain_emb[idx][:, None, :]
        hidden = jnp.einsum('bsa,da->bsd', hidden, up_W) + up_b
        x = hidden + residual
        mu = jnp.mean(x, axis=-1, keepdims=True)
        var = jnp.mean(jnp.square(x - mu), axis=-1, keepdims=True)
        return (x - mu) * jax.lax.rsqrt(var + LN_EPS) * ln_gamma + ln_beta
    x = _L0_cond_ref(x, condB_gatescore, L0_cond_Wq, L0_cond_bq, L0_cond_Wk, L0_cond_bk, L0_cond_Wv, L0_cond_bv, L0_cond_Wo, L0_cond_bo, L0_cond_W1, L0_cond_b1, L0_cond_W2, L0_cond_b2, L0_cond_gamma1, L0_cond_beta1, L0_cond_gamma2, L0_cond_beta2)
    x = _L1_cond_ref(x, mask_Bx1xSxS_bk0, itok_B_34_63, fside_Bx16xSxS_0, L1_cond_W_ada, L1_cond_b_ada, L1_cond_Wq, L1_cond_bq, L1_cond_Wk, L1_cond_bk, L1_cond_Wv, L1_cond_bv, L1_cond_Wo, L1_cond_bo, L1_cond_W1, L1_cond_b1, L1_cond_W2, L1_cond_b2, L1_cond_g2, L1_cond_beta2)
    x = _L2_cond_ref(x, condB_theta, condB_phi)
    x = _L3_cond_ref(x, itok_B_0_15, L3_cond_down_W, L3_cond_down_b, L3_cond_up_W, L3_cond_up_b, L3_cond_expert_W, L3_cond_expert_b, L3_cond_domain_emb, L3_cond_ln_gamma, L3_cond_ln_beta)
    return x

_drawn_inputs = setup_inputs


def setup_inputs(seed=0):
    import zlib

    import numpy as np

    out = dict(_drawn_inputs(seed))
    spreads = {'L0_cond_bq': (0.0, 0.8),
     'L0_cond_bk': (0.0, 2.0),
     'L0_cond_bv': (0.0, 0.1),
     'L0_cond_bo': (0.0, 0.274),
     'L0_cond_b1': (0.0, 0.426),
     'L0_cond_b2': (0.0, 0.308),
     'L0_cond_gamma1': (1.0, 0.2),
     'L0_cond_beta1': (0.0, 0.1),
     'L0_cond_gamma2': (1.0, 0.2),
     'L0_cond_beta2': (0.0, 0.406),
     'L1_cond_b_ada': (0.0, 0.1),
     'L1_cond_bq': (0.0, 0.8),
     'L1_cond_bk': (0.0, 2.0),
     'L1_cond_bv': (0.0, 0.401),
     'L1_cond_bo': (0.0, 0.1),
     'L1_cond_b1': (0.0, 0.421),
     'L1_cond_b2': (0.0, 0.1),
     'L1_cond_g2': (1.0, 0.6),
     'L1_cond_beta2': (0.0, 0.8),
     'L3_cond_ln_gamma': (1.0, 0.2),
     'L3_cond_ln_beta': (0.0, 0.1)}
    factors = {'fside_Bx16xSxS_0': 6.022,
     'L1_cond_Wq': 8.0,
     'L1_cond_Wk': 8.0,
     'L1_cond_Wv': 3.744,
     'L3_cond_down_b': 5.919}
    for name, (base, spread) in spreads.items():
        noise = np.random.default_rng([zlib.crc32(name.encode()), seed]).standard_normal(out[name].shape)
        drawn = base * np.exp(spread * noise) if base else spread * noise
        out[name] = jnp.asarray(drawn.astype(out[name].dtype))
    for name, factor in factors.items():
        out[name] = (out[name] * factor).astype(out[name].dtype)
    return out
```

```python
from contextlib import ExitStack

import numpy as np

import concourse.bass as bass
from concourse import mybir

F32 = mybir.dt.float32
BF16 = mybir.dt.bfloat16
I32 = mybir.dt.int32
U32 = mybir.dt.uint32
U8 = mybir.dt.uint8
ALU = mybir.AluOpType
ACT = mybir.ActivationFunctionType
AX = mybir.AxisListType.X

B, S, D = 64, 32, 128
H, DH = 16, 8
DFF = 512
E, A = 16, 32
P = 128
R = 4
TILES = B * S // P
T = 4
CH = TILES // T
CB = T * R
CT = T * P
FC = DFF // P
EPS = 1e-5
NEG = -1e30
TWO_PI = 6.283185307179586
PI_A = 6.28125
PI_B = 0.0019350051879882812
PI_C = TWO_PI - PI_A - PI_B
ROUND = 12582912.0
PI_MAX = 3.1415925

C_IDENT, C_BLOCK, C_CAUSAL, C_EYE, C_HEAD, C_FREQ, C_OUT, C_SIN, C_COSM, C_COSA = (
    0, 128, 256, 288, 320, 324, 325, 326, 327, 328)
N_CONST = 329
W_Q, W_K, W_V, W_O, W_1, W_2 = 0, 128, 256, 384, 512, 1024
R_BO0, R_B20, R_BO1, R_B21, R_UP, R_LNG, R_LNB = (128 * n for n in range(7))
K_BQ, K_BK, K_BV, K_G2, K_BETA2, K_B1 = 0, 1, 2, 3, 4, 5
K_STREAM = 9
K_G1, K_BETA1, K_ADA, K_DOWN = 18, 19, 20, 22
N_COLS = 23


class Norm:

    def __init__(self, sb, sem, name):
        self.stats = sb(name + "_stats", [P, T, 6], F32)
        self.mv = sb(name + "_mv", [P, T, 2], F32)
        self.ve = sb(name + "_ve", [P, T], F32)
        self.rstd = sb(name + "_rstd", [P, T], F32)
        self.xh = sb(name + "_xh", [P, T, D], F32)
        self.mv_done = sem(name + "_mv_done")
        self.ve_done = sem(name + "_ve_done")
        self.rstd_done = sem(name + "_rstd_done")
        self.xh_done = sem(name + "_xh_done")
        self.turned = sem(name + "_turned")


class Stream:

    def __init__(self, sb, ps, sem, name, col):
        self.name = name
        self.col = col
        self.w = sb(name + "_w", [P, 4 * D + 2 * DFF], F32)
        self.ln1 = Norm(sb, sem, name + "_ln1")
        self.ln2 = Norm(sb, sem, name + "_ln2")
        self.hT = sb(name + "_hT", [P, CT], F32)
        self.h2T = self.hT
        self.Qm = sb(name + "_Qm", [P, CB, R, S], F32)
        self.Km = sb(name + "_Km", [P, CB, R, S], F32)
        self.Vm = sb(name + "_Vm", [P, CB, D], F32)
        self.bqm = sb(name + "_bqm", [P, R], F32)
        self.bvb = sb(name + "_bvb", [P, D], F32)
        self.bo = sb(name + "_bo", [P, D], F32)
        self.mx = sb(name + "_mx", [P, 2, 16], F32)
        self.sm = sb(name + "_sm", [P, 2, 16], F32)
        self.rc = sb(name + "_rc", [P, 2, 16], F32)
        self.Dm = sb(name + "_Dm", [P, 2, CT], F32)
        self.Ex = sb(name + "_Ex", [P, 2, CT], F32)
        self.Pn = sb(name + "_Pn", [P, 2, CT], F32)
        self.PT = sb(name + "_PT", [P, 2, CT], F32)
        self.ctxT = sb(name + "_ctxT", [P, CT], F32)
        self.x1 = sb(name + "_x1", [P, T, D], F32)
        self.rest = sb(name + "_rest", [P, T, D], F32)
        self.fT = self.Qm[:].rearrange("p n r q -> p (n r q)").rearrange("p (c n) -> p c n", c=FC)
        self.P0 = ps(name + "_P0", [P, CT], F32)
        self.P1 = ps(name + "_P1", [P, CT], F32)
        self.S2 = [ps(name + f"_S{n}", [P, CT], F32) for n in range(2)]
        self.loaded = sem(name + "_w_loaded")
        self.bqm_done = sem(name + "_bqm_done")
        self.bvb_done = sem(name + "_bvb_done")
        self.bo_mm = sem(name + "_bo_mm")
        self.bo_done = sem(name + "_bo_done")
        self.zeroed = sem(name + "_zeroed")
        self.hT_done = sem(name + "_hT_done")
        self.q_mm = sem(name + "_q_mm")
        self.k_mm = sem(name + "_k_mm")
        self.v_mm = sem(name + "_v_mm")
        self.qm_done = sem(name + "_qm_done")
        self.km_done = sem(name + "_km_done")
        self.vm_act = sem(name + "_vm_act")
        self.vm_dve = sem(name + "_vm_dve")
        self.sc_mm = sem(name + "_sc_mm")
        self.mx_done = sem(name + "_mx_done")
        self.s_free = sem(name + "_s_free")
        self.sub_done = self.s_free if name == "a" else sem(name + "_sub_done")
        self.ex_done = sem(name + "_ex_done")
        self.sm_done = sem(name + "_sm_done")
        self.rc_done = sem(name + "_rc_done")
        self.pn_done = sem(name + "_pn_done")
        self.pt_done = sem(name + "_pt_done")
        self.pv_mm = sem(name + "_pv_mm")
        self.ctx_done = sem(name + "_ctx_done")
        self.o_mm = sem(name + "_o_mm")
        self.x1_done = sem(name + "_x1_done")
        self.rest_done = sem(name + "_rest_done")
        self.h2T_done = sem(name + "_h2T_done")
        self.f_mm = sem(name + "_f_mm")
        self.f_done = sem(name + "_f_done")
        self.y_mm = sem(name + "_y_mm")
        self.y_done = sem(name + "_y_done")


def wait(eng, sem, value):
    if isinstance(value, int) and value <= 0:
        return
    eng.wait_ge(sem, value)


def two_ago(n, t):
    return n if t == 0 else n - 1


def cond_seq_kernel(nc, x_in, bias_in, mask_in, w0_in, w1_in, wx_in, rows_in, cols_in, toks_in,
                    ids_in, etab_in, const_in, out):
    with ExitStack() as ctx:
        def sb(name, shape, dt):
            return ctx.enter_context(nc.sbuf_tensor(name, shape, dt))

        def ps(name, shape, dt):
            return ctx.enter_context(nc.psum_tensor(name, shape, dt))

        def sem(name):
            return ctx.enter_context(nc.semaphore(name))

        a = Stream(sb, ps, sem, "a", 0)
        b = Stream(sb, ps, sem, "b", K_STREAM)
        ln3 = Norm(sb, sem, "ln3")

        const = sb("const", [P, N_CONST], F32)
        cols = sb("cols", [P, N_COLS], F32)
        rows = sb("rows", [P, 7 * D], F32)
        wx = sb("wx", [P, 4 * D], F32)
        toks = sb("toks", [P, 2 * TILES], F32)
        ids = sb("ids", [P, TILES + B], I32)
        xg = sb("xg", [P, CT + T], F32)
        x = xg[:, 0:CT].rearrange("p (t d) -> p t d", d=D)
        gate = xg[:, CT:]
        gate_kept = sb("gate_kept", [P, T], F32)
        bias = sb("bias", [P, T, CT], F32)
        mask4 = sb("mask4", [P, B * S // 4], I32)
        maskb = sb("maskb", [P, B, S], BF16)
        identb = sb("identb", [P, P], BF16)
        causalb = sb("causalb", [P, S], BF16)
        mhalf = sb("mhalf", [P, T], F32)
        eps = sb("eps", [P, T], F32)
        ident = const[:, C_IDENT:C_IDENT + P]
        block_mask = const[:, C_BLOCK:C_BLOCK + P]
        head_mask = const[:, C_HEAD:C_HEAD + R]
        NA = 2 * TILES + B
        ang = sb("ang", [P, NA], F32)
        ang_k = sb("ang_k", [P, 2, NA], F32)
        ang_r = sb("ang_r", [P, 4, NA], F32)
        arg = sb("arg", [P, 2 * 2 * TILES + B], F32)
        trig = sb("trig", [P, 2 * 2 * TILES + B], F32)
        tf = sb("tf", [P, 8, B], F32)
        emb_abs = sb("emb_abs", [P, 2, B], F32)
        emb = sb("emb", [P, B], F32)
        T_SCALE, T_SHIFT, T_COS, T_SIN, T_BIAS, T_W = 0, CB, 2 * CB, 2 * CB + 4 * T, 2 * CB + 6 * T, 2 * CB + 7 * T
        N_TAB = T_W + T * A
        tabs = sb("tabs", [P, CH, N_TAB], F32)
        tab = sb("tab", [P, N_TAB], F32)
        idf = sb("idf", [P, 5, TILES], F32)
        idx = sb("idx", [P, TILES], U32)
        got = sb("got", [P, TILES, A + 2], F32)
        wsel = sb("wsel", [P, 3, TILES, A], F32)
        bsel = sb("bsel", [P, TILES], F32)
        wblk = sb("wblk", [P, T, P], F32)
        xn = sb("xn", [P, T, D], F32)
        xb = sb("xb", [P, T, D], F32)
        aw = sb("aw", [P, 3, T, D], F32)
        xm = sb("xm", [P, CT], F32)
        xr = sb("xr", [P, T, D], F32)
        rc4 = sb("rc4", [P, T, D], F32)
        rs4 = sb("rs4", [P, 2, CT // 2], F32)
        y = sb("y", [P, T, D], F32)
        yb = sb("yb", [P, T, D], F32)
        yT = xm
        hid = sb("hid", [P, CT], F32)
        em = sb("em", [P, T, P], F32)
        z = sb("z", [P, T, D], F32)
        og = sb("og", [P, T, D], F32)
        ob = sb("ob", [P, T, D], F32)

        ld_const = sem("ld_const")
        ld_x = sem("ld_x")
        ld_ids = sem("ld_ids")
        ld_rows = sem("ld_rows")
        ld_toks = sem("ld_toks")
        ld_wx = sem("ld_wx")
        ld_mask = sem("ld_mask")
        ld_bias = [sem(f"ld_bias{t}") for t in range(T)]
        consts_b = sem("consts_b")
        maskb_done = sem("maskb_done")
        mhalf_done = sem("mhalf_done")
        chain = sem("chain")
        arg_done = sem("arg_done")
        trig_done = sem("trig_done")
        emb_done = sem("emb_done")
        tables_done = sem("tables_done")
        ada_mm = sem("ada_mm")
        ada_done = sem("ada_done")
        idx_done = sem("idx_done")
        gathered = sem("gathered")
        tab_done = sem("tab_done")
        gate_done = sem("gate_done")
        xb_done = sem("xb_done")
        aw_done = sem("aw_done")
        xm_done = sem("xm_done")
        rc4_done = sem("rc4_done")
        rs4_done = sem("rs4_done")
        rot_done = sem("rot_done")
        yb_done = sem("yb_done")
        y_turned = sem("y_turned")
        yT_done = sem("yT_done")
        down_mm = sem("down_mm")
        hid_done = sem("hid_done")
        wblk_done = sem("wblk_done")
        ex_mm = sem("ex_mm")
        em_done = sem("em_done")
        up_mm = sem("up_mm")
        z_done = sem("z_done")
        og_done = sem("og_done")
        ob_done = sem("ob_done")
        stored = sem("stored")

        def over_tiles(row):
            return row.rearrange("p (o d) -> p o d", o=1).to_broadcast([P, T, D])

        def spread(col, n, k):
            return col.rearrange("p (n o) -> p n o", o=1).to_broadcast([P, n, k])

        def groups(ap):
            return ap.rearrange("p (n k) -> p n k", k=S)

        def pairs(buf):
            v = buf[:].rearrange("p t (q e) -> p (t q) e", e=2)
            return v[:, :, 0], v[:, :, 1]

        block = ctx.enter_context(nc.Block())

        @block.sync
        def _(sp):
            sp.dma_start(xg[:], x_in[:, 0:CT + T]).then_inc(ld_x, 16)
            sp.dma_start(const[:], const_in).then_inc(ld_const, 16)
            sp.dma_start(a.w[:], w0_in).then_inc(a.loaded, 16)
            sp.dma_start(rows[:], rows_in).then_inc(ld_rows, 16)
            sp.dma_start(mask4[:], mask_in).then_inc(ld_mask, 16)
            sp.dma_start(b.w[:], w1_in).then_inc(b.loaded, 16)
            for t in range(T):
                sp.dma_start(bias[:, t, :], bias_in[:, t * CT:(t + 1) * CT]).then_inc(ld_bias[t], 16)
            with sp.Fori(1, CH) as i:
                sp.wait_ge(aw_done, 4 * i)
                sp.wait_ge(gate_done, i)
                sp.dma_start(xg[:], x_in[:, bass.ds(i * (CT + T), CT + T)]).then_inc(ld_x, 16)
                for t in range(T):
                    sp.wait_ge(b.s_free, (i - 1) * T + t + 1)
                    sp.dma_start(bias[:, t, :], bias_in[:, bass.ds((i * T + t) * CT, CT)]).then_inc(ld_bias[t], 16)
                sp.wait_ge(ob_done, i)
                sp.dma_start(out[:, bass.ds((i - 1) * CT, CT)], ob[:].rearrange("p t d -> p (t d)")).then_inc(stored, 16)
            sp.wait_ge(ob_done, CH)
            sp.dma_start(out[:, (CH - 1) * CT:], ob[:].rearrange("p t d -> p (t d)")).then_inc(stored, 16)
            sp.wait_ge(stored, 16 * CH)

        @block.tensor
        def _(pe):
            def turn(ln, src, bank, i):
                for t in range(T):
                    last = pe.transpose(bank[:, t * P:(t + 1) * P], src[:, t, :], ident)
                last.then_inc(ln, 1)

            def turn1(s, i):
                wait(pe, s.ln1.xh_done, i + 1)
                turn(s.ln1.turned, s.ln1.xh, s.P0, i)

            def project(s, i, p1_free):
                pe.wait_ge(s.hT_done, i + 1)
                wait(pe, p1_free, i)
                pe.matmul(s.P1[:], s.w[:, W_Q:W_Q + D], s.hT[:], start=True, stop=True).then_inc(s.q_mm, 1)
                pe.matmul(s.P0[:], s.w[:, W_K:W_K + D], s.hT[:], start=True, stop=True).then_inc(s.k_mm, 1)
                pe.wait_ge(s.qm_done, i + 1)
                for t in range(T):
                    last = pe.matmul(s.P1[:, t * P:(t + 1) * P], s.hT[:, t * P:(t + 1) * P],
                                     s.w[:, W_V:W_V + D], start=True, stop=True)
                last.then_inc(s.v_mm, 1)

            def scores(s, i, t):
                if t == 0:
                    pe.wait_ge(s.km_done, i + 1)
                if t == 0:
                    wait(pe, s.f_done, i * FC)
                if t >= 2:
                    pe.wait_ge(s.s_free, i * T + t - 1)
                bank = s.S2[t % 2]
                if s is a:
                    masks = causalb[:].rearrange("p (o k) -> p o k", o=1).to_broadcast([P, CB, S])
                else:
                    masks = maskb[:, bass.ds(i * CB + t * R, R), :].rearrange(
                        "p (n o) k -> p n o k", o=1).to_broadcast([P, R, R, S])
                pe.matmul(bank[:], identb[:], masks, start=True, stop=False)
                for j in range(R):
                    n = t * R + j
                    last = pe.matmul(bank[:, j * P:(j + 1) * P], s.Qm[:, n, :, :], s.Km[:, n, :, :],
                                     start=False, stop=(j == R - 1))
                last.then_inc(s.sc_mm, 1)

            def values(s, i, t):
                if t == 0:
                    pe.wait_ge(s.vm_act, i + 1)
                    pe.wait_ge(s.vm_dve, i + 1)
                pe.wait_ge(s.pt_done, i * T + t + 1)
                for j in range(R):
                    n = t * R + j
                    for g in range(R):
                        last = pe.matmul(s.P0[32 * g:32 * g + 32, n * S:(n + 1) * S],
                                         s.Vm[:, n, 32 * g:32 * g + 32],
                                         s.PT[:, t % 2, (j * R + g) * S:(j * R + g + 1) * S],
                                         start=True, stop=True, tile_position=(0, 32 * g))
                last.then_inc(s.pv_mm, 1)

            def attend_out(s, i):
                pe.wait_ge(s.ctx_done, i + 1)
                for t in range(T):
                    tile = slice(t * P, (t + 1) * P)
                    last = pe.matmul(s.P1[:, tile], s.ctxT[:, tile], s.w[:, W_O:W_O + D],
                                     start=True, stop=(s is a))
                    if s is b:
                        last = pe.matmul(s.P1[:, tile], s.hT[:, tile], ident, start=False, stop=True)
                last.then_inc(s.o_mm, 1)

            def turn2(s, i):
                pe.wait_ge(s.ln2.xh_done, i + 1)
                turn(s.ln2.turned, s.ln2.xh, s.P0, i)

            def hidden(s, i, c):
                if c == 0:
                    pe.wait_ge(s.h2T_done, i + 1)
                if c >= 2:
                    pe.wait_ge(s.f_done, i * FC + c - 1)
                pe.matmul(s.S2[c % 2][:], s.w[:, W_1 + c * P:W_1 + (c + 1) * P], s.h2T[:],
                          start=True, stop=True).then_inc(s.f_mm, 1)

            def hidden_out(s, i):
                pe.wait_ge(s.f_done, (i + 1) * FC)
                pe.wait_ge(s.x1_done, i + 1)
                for t in range(T):
                    for c in range(FC):
                        last = pe.matmul(s.P1[:, t * P:(t + 1) * P], s.fT[:, c, t * P:(t + 1) * P],
                                         s.w[:, W_2 + c * D:W_2 + (c + 1) * D],
                                         start=(c == 0), stop=(c == FC - 1))
                last.then_inc(s.y_mm, 1)

            def adapter_down(i):
                pe.wait_ge(rot_done, i + 1)
                turn(y_turned, y, b.P0, i)
                pe.wait_ge(yT_done, i + 1)
                pe.matmul(b.P1[:], wx[:, 2 * D:3 * D], yT[:], start=True, stop=True).then_inc(down_mm, 1)

            def adapter_expert(i):
                pe.wait_ge(hid_done, i + 1)
                pe.wait_ge(wblk_done, i + 1)
                for t in range(T):
                    last = pe.matmul(b.P0[:, t * P:(t + 1) * P], wblk[:, t, :], hid[:, t * P:(t + 1) * P],
                                     start=True, stop=True)
                last.then_inc(ex_mm, 1)

            def adapter_up(i):
                pe.wait_ge(em_done, i + 1)
                for t in range(T):
                    last = pe.matmul(b.P1[:, t * P:(t + 1) * P], em[:, t, :], wx[:, 3 * D:4 * D],
                                     start=True, stop=True)
                last.then_inc(up_mm, 1)

            def turn1_a(i):
                wait(pe, a.h2T_done, i)
                turn1(a, i)

            def turn1_b(i):
                wait(pe, em_done, i)
                turn1(b, i)

            def fold_bv(s):
                pe.wait_ge(s.loaded, 16)
                pe.wait_ge(s.bvb_done, 1)
                pe.matmul(s.S2[0][:, 0:D], s.bvb[:], s.w[:, W_O:W_O + D], start=True, stop=True).then_inc(s.bo_mm, 1)

            pe.wait_ge(ld_const, 32)
            pe.wait_ge(consts_b, 1)
            fold_bv(a)
            turn1_a(0)
            project(a, 0, a.y_done)
            pe.wait_ge(a.bo_done, 1)
            for t in range(T + 2):
                if t < T:
                    scores(a, 0, t)
                if t >= 2:
                    values(a, 0, t - 2)
            fold_bv(b)
            pe.wait_ge(ld_wx, 16)
            pe.wait_ge(emb_done, 1)
            pe.matmul(b.S2[1][:, 0:B], wx[:, 0:D], emb[:], start=True, stop=True)
            pe.matmul(b.S2[1][:, B:2 * B], wx[:, D:2 * D], emb[:], start=True, stop=True).then_inc(ada_mm, 1)
            attend_out(a, 0)
            turn2(a, 0)
            for c in range(FC):
                hidden(a, 0, c)
            hidden_out(a, 0)
            pe.wait_ge(b.bo_done, 1)
            pe.wait_ge(ada_done, 1)
            pe.wait_ge(maskb_done, 1)

            def both(i):
                turn1_b(i - 1)
                turn1_a(i)
                project(b, i - 1, z_done)
                project(a, i, a.y_done)
                for t in range(T + 2):
                    if t < T:
                        scores(b, i - 1, t)
                        scores(a, i, t)
                    if t >= 2:
                        values(b, i - 1, t - 2)
                        values(a, i, t - 2)
                attend_out(b, i - 1)
                attend_out(a, i)
                turn2(b, i - 1)
                turn2(a, i)
                for c in range(FC):
                    hidden(b, i - 1, c)
                hidden_out(b, i - 1)
                for c in range(FC):
                    hidden(a, i, c)
                adapter_down(i - 1)
                hidden_out(a, i)
                adapter_expert(i - 1)
                adapter_up(i - 1)

            both(1)
            with pe.Fori(2, CH) as i:
                both(i)

            i = CH - 1
            turn1_b(i)
            project(b, i, z_done)
            for t in range(T + 2):
                if t < T:
                    scores(b, i, t)
                if t >= 2:
                    values(b, i, t - 2)
            attend_out(b, i)
            turn2(b, i)
            for c in range(FC):
                hidden(b, i, c)
            hidden_out(b, i)
            adapter_down(i)
            adapter_expert(i)
            adapter_up(i)

        @block.scalar
        def _(act):
            act.dma_start(cols[:], cols_in).then_inc(ld_const, 16)
            act.dma_start(ids[:], ids_in).then_inc(ld_ids, 16)
            act.dma_start(toks[:], toks_in).then_inc(ld_toks, 16)
            act.dma_start(wx[:], wx_in).then_inc(ld_wx, 16)

            def norm_out(s, i):
                act.wait_ge(s.ln1.turned, i + 1)
                nc.scalar.activation(s.hT[:], s.P0[:], ACT.Identity, bias=cols[:, K_BETA1:K_BETA1 + 1],
                                     scale=cols[:, K_G1:K_G1 + 1]).then_inc(s.hT_done, 1)

            def queries(s, i):
                act.wait_ge(s.q_mm, i + 1)
                for r in range(R):
                    last = nc.scalar.activation(s.Qm[:, :, r, :], groups(s.P1[:]), ACT.Identity,
                                                bias=s.bqm[:, r:r + 1], scale=head_mask[:, r:r + 1])
                last.then_inc(s.qm_done, 1)

            def values_spread(s, i):
                act.wait_ge(s.v_mm, i + 1)
                for j in range(2):
                    src = s.P1[32 * j:32 * j + 32, :].rearrange("p (t g r d) -> p t g r d", t=T, g=R, r=R)
                    for r in range(R):
                        dst = s.Vm[32 * r:32 * r + 32, :, :].rearrange(
                            "p (t j) (g r d) -> p t j g r d", j=R, g=R, r=R)
                        last = nc.scalar.activation(dst[:, :, j, :, r, :], src[:, :, :, r, :], ACT.Copy)
                last.then_inc(s.vm_act, 1)

            def exps(s, i, t):
                act.wait_ge(s.sub_done, i * T + t + 1)
                wait(act, s.pn_done, two_ago(i * T + t, t))
                nc.scalar.activation(s.Ex[:, t % 2, :], s.Dm[:, t % 2, :], ACT.Exp).then_inc(s.ex_done, 1)

            def context(s, i):
                act.wait_ge(s.pv_mm, (i + 1) * T)
                nc.scalar.activation(s.ctxT[:], s.P0[:], ACT.Copy).then_inc(s.ctx_done, 1)

            def norm2_out(s, i):
                act.wait_ge(s.ln2.turned, i + 1)
                nc.scalar.activation(s.h2T[:], s.P0[:], ACT.Identity,
                                     bias=cols[:, s.col + K_BETA2:s.col + K_BETA2 + 1],
                                     scale=cols[:, s.col + K_G2:s.col + K_G2 + 1]).then_inc(s.h2T_done, 1)

            def gelu(s, i, c):
                act.wait_ge(s.f_mm, i * FC + c + 1)
                nc.scalar.activation(s.fT[:, c, :], s.S2[c % 2][:],
                                     ACT.Gelu if s is a else ACT.Gelu_apprx_sigmoid,
                                     bias=cols[:, s.col + K_B1 + c:s.col + K_B1 + c + 1]).then_inc(s.f_done, 1)

            def adapter_in(i):
                act.wait_ge(y_turned, i + 1)
                nc.scalar.activation(yT[:], b.P0[:], ACT.Copy).then_inc(yT_done, 1)

            def adapter_gelu(i):
                act.wait_ge(down_mm, i + 1)
                nc.scalar.activation(hid[:], b.P1[:], ACT.Gelu,
                                     bias=cols[:, K_DOWN:K_DOWN + 1]).then_inc(hid_done, 1)

            act.wait_ge(ld_const, 32)
            norm_out(a, 0)
            act.wait_ge(a.bqm_done, 1)
            queries(a, 0)
            act.wait_ge(a.zeroed, 1)
            values_spread(a, 0)
            for t in range(T):
                exps(a, 0, t)
            act.wait_ge(arg_done, 1)
            nc.scalar.activation(trig[:], arg[:], ACT.Sin).then_inc(trig_done, 1)
            act.wait_ge(trig_done, 1)
            nc.scalar.activation(emb[:], trig[:, 4 * TILES:], ACT.Silu).then_inc(emb_done, 1)
            context(a, 0)
            norm2_out(a, 0)
            for c in range(FC):
                gelu(a, 0, c)
            act.wait_ge(b.bqm_done, 1)
            act.wait_ge(b.zeroed, 1)

            def both(i):
                norm_out(a, i)
                queries(b, i - 1)
                queries(a, i)
                values_spread(b, i - 1)
                values_spread(a, i)
                for t in range(T):
                    exps(b, i - 1, t)
                    exps(a, i, t)
                context(b, i - 1)
                context(a, i)
                norm2_out(b, i - 1)
                norm2_out(a, i)
                for c in range(FC):
                    gelu(b, i - 1, c)
                for c in range(FC):
                    gelu(a, i, c)
                adapter_in(i - 1)
                adapter_gelu(i - 1)

            both(1)
            with act.Fori(2, CH) as i:
                both(i)

            i = CH - 1
            queries(b, i)
            values_spread(b, i)
            for t in range(T):
                exps(b, i, t)
            context(b, i)
            norm2_out(b, i)
            for c in range(FC):
                gelu(b, i, c)
            adapter_in(i)
            adapter_gelu(i)

        @block.vector
        def _(dve):
            steps = [0]

            def link(ins):
                steps[0] += 1
                ins.then_inc(chain, 1)
                dve.wait_ge(chain, steps[0])

            def norm_stats(ln, src, i):
                for t in range(T):
                    nc.vector.bn_stats(ln.stats[:, t, :], src(t))
                dve.drain()
                for t in range(T):
                    last = nc.vector.bn_aggr(ln.mv[:, t, :], ln.stats[:, t, :])
                last.then_inc(ln.mv_done, 1)

            def norm_apply(ln, src, i):
                dve.wait_ge(ln.rstd_done, i + 1)
                for t in range(T):
                    last = nc.vector.tensor_scalar(ln.xh[:, t, :], src(t), ln.mv[:, t, 0:1],
                                                   ln.rstd[:, t:t + 1], ALU.subtract, ALU.mult)
                last.then_inc(ln.xh_done, 1)

            def tile_of(buf):
                return lambda t: buf[:, t, :]

            def keys(s, i):
                dve.wait_ge(s.k_mm, i + 1)
                for g in range(R):
                    q = slice(32 * g, 32 * g + 32)
                    last = nc.vector.tensor_scalar(s.Km[q, :, g, :], groups(s.P0[q, :]),
                                                   cols[q, s.col + K_BK:s.col + K_BK + 1], None, ALU.add)
                last.then_inc(s.km_done, 1)

            def values_spread(s, i):
                dve.wait_ge(s.v_mm, i + 1)
                for j in range(2, R):
                    src = s.P1[32 * j:32 * j + 32, :].rearrange("p (t g r d) -> p t g r d", t=T, g=R, r=R)
                    for r in range(R):
                        dst = s.Vm[32 * r:32 * r + 32, :, :].rearrange(
                            "p (t j) (g r d) -> p t j g r d", j=R, g=R, r=R)
                        last = nc.vector.tensor_copy(dst[:, :, j, :, r, :], src[:, :, :, r, :])
                last.then_inc(s.vm_dve, 1)

            def row_max(s, i, t):
                n = i * T + t
                k = t % 2
                dve.wait_ge(s.sc_mm, n + 1)
                if s is a:
                    nc.vector.tensor_reduce(s.mx[:, k, :], groups(s.S2[k][:]), AX, ALU.max).then_inc(s.mx_done, 1)
                    dve.wait_ge(s.mx_done, n + 1)
                    wait(dve, s.ex_done, two_ago(n, t))
                    nc.vector.tensor_tensor(groups(s.Dm[:, k, :]), groups(s.S2[k][:]), spread(s.mx[:, k, :], CB, S),
                                            ALU.subtract).then_inc(s.s_free, 1)
                else:
                    dve.wait_ge(ld_bias[t], (i + 1) * 16)
                    wait(dve, s.ex_done, two_ago(n, t))
                    nc.vector.tensor_tensor(s.Dm[:, k, :], s.S2[k][:], bias[:, t, :], ALU.add).then_inc(s.s_free, 1)
                    dve.wait_ge(s.s_free, n + 1)
                    nc.vector.tensor_reduce(s.mx[:, k, :], groups(s.Dm[:, k, :]), AX, ALU.max).then_inc(s.mx_done, 1)

            def row_sum(s, i, t):
                n = i * T + t
                k = t % 2
                dve.wait_ge(s.ex_done, n + 1)
                nc.vector.tensor_reduce(s.sm[:, k, :], groups(s.Ex[:, k, :]), AX, ALU.add).then_inc(s.sm_done, 1)
                dve.wait_ge(s.sm_done, n + 1)
                wait(dve, s.pn_done, two_ago(n, t))
                nc.vector.reciprocal(s.rc[:, k, :], s.sm[:, k, :]).then_inc(s.rc_done, 1)

            def turn_probs(s, i, t):
                n = i * T + t
                k = t % 2
                dve.wait_ge(s.pn_done, n + 1)
                wait(dve, s.pv_mm, two_ago(n, t))
                nc.vector.transpose(s.PT[:, k, :], s.Pn[:, k, :]).then_inc(s.pt_done, 1)

            def after_attention(s, i):
                dve.wait_ge(s.o_mm, i + 1)
                p1 = s.P1[:].rearrange("p (t d) -> p t d", d=D)
                if s is a:
                    dve.wait_ge(xb_done, i + 1)
                    wait(dve, aw_done, 4 * i)
                    nc.vector.tensor_tensor(s.x1[:], p1, xb[:], ALU.add).then_inc(s.x1_done, 1)
                else:
                    wait(dve, s.rest_done, i)
                    nc.vector.tensor_tensor(s.x1[:], p1, over_tiles(s.bo[:]), ALU.add).then_inc(s.x1_done, 1)

            def block_out_a(i):
                dve.wait_ge(gate_done, i + 1)
                dve.wait_ge(a.y_mm, i + 1)
                dve.wait_ge(aw_done, 4 * i + 4)
                for t in range(T):
                    last = nc.vector.scalar_tensor_tensor(
                        xn[:, t, :], a.P1[:, t * P:(t + 1) * P], gate_kept[:, t:t + 1],
                        aw[:, 0, t, :], ALU.mult, ALU.add)
                last.then_inc(a.y_done, 1)

            def chunk_tables(i):
                wait(dve, rs4_done, 2 * i)
                nc.vector.tensor_copy(tab[:], tabs[:, bass.ds(i, 1), :].rearrange("p o n -> p (o n)")).then_inc(tab_done, 1)
                dve.wait_ge(tab_done, i + 1)

            def modulate(i):
                dve.wait_ge(b.ln1.turned, i + 1)
                nc.vector.tensor_tensor(groups(xm[:]), groups(b.P0[:]),
                                        spread(tab[:, T_SCALE:T_SCALE + CB], CB, S), ALU.mult).then_inc(xm_done, 1)

            def block_out_b(i):
                dve.wait_ge(b.y_mm, i + 1)
                dve.wait_ge(b.rest_done, i + 1)
                nc.vector.tensor_tensor(xr[:], b.P1[:].rearrange("p (t d) -> p t d", d=D), b.rest[:],
                                        ALU.add).then_inc(b.y_done, 1)
                dve.wait_ge(b.y_done, i + 1)
                c4 = tab[:, T_COS:T_COS + 4 * T].rearrange("p (t o w) -> p t o w", o=1, w=4)
                nc.vector.tensor_tensor(xr_quads(rc4), xr_quads(xr), c4.to_broadcast([P, T, D // 4, 4]),
                                        ALU.mult).then_inc(rc4_done, 1)
                dve.wait_ge(rc4_done, i + 1)
                dve.wait_ge(rs4_done, 2 * i + 2)
                wait(dve, yb_done, i)
                even, odd = pairs(y)
                c_even, c_odd = pairs(rc4)
                nc.vector.tensor_tensor(even, c_even, rs4[:, 0, :], ALU.add)
                nc.vector.tensor_tensor(odd, c_odd, rs4[:, 1, :], ALU.subtract).then_inc(rot_done, 1)

            def xr_quads(buf):
                return buf[:].rearrange("p t (q w) -> p t q w", w=4)

            def expert_bias(i):
                dve.wait_ge(ex_mm, i + 1)
                for t in range(T):
                    last = nc.vector.scalar_tensor_tensor(
                        em[:, t, :], b.P0[:, t * P:(t + 1) * P], tab[:, T_BIAS + t:T_BIAS + t + 1],
                        block_mask, ALU.add, ALU.mult)
                last.then_inc(em_done, 1)

            def adapter_out(i):
                dve.wait_ge(up_mm, i + 1)
                dve.wait_ge(yb_done, i + 1)
                nc.vector.tensor_tensor(z[:], b.P1[:].rearrange("p (t d) -> p t d", d=D), yb[:],
                                        ALU.add).then_inc(z_done, 1)

            def norm3(i):
                dve.wait_ge(z_done, i + 1)
                norm_stats(ln3, tile_of(z), i)
                wait(dve, og_done, i)
                norm_apply(ln3, tile_of(z), i)

            def fold_bo(s, row):
                dve.wait_ge(s.bo_mm, 1)
                nc.vector.tensor_tensor(s.bo[:], s.S2[0][:, 0:D], rows[:, row:row + D], ALU.add).then_inc(s.bo_done, 1)

            def stats1_a(i):
                dve.wait_ge(ld_x, 16 * (i + 1))
                nc.vector.tensor_copy(gate_kept[:], gate).then_inc(gate_done, 1)
                norm_stats(a.ln1, tile_of(x), i)

            def norm1_a(i):
                stats1_a(i)
                norm_apply(a.ln1, tile_of(x), i)

            def softmax_step(s, i, t):
                if t < T:
                    row_max(s, i, t)

            dve.wait_ge(ld_const, 32)
            nc.vector.tensor_copy(identb[:], ident)
            nc.vector.tensor_copy(causalb[:], const[:, C_CAUSAL:C_CAUSAL + S]).then_inc(consts_b, 1)
            for s in (a, b):
                nc.vector.tensor_scalar(s.bqm[:], head_mask, cols[:, s.col + K_BQ:s.col + K_BQ + 1], None,
                                        ALU.mult).then_inc(s.bqm_done, 1)
                nc.vector.tensor_scalar(s.bvb[:], ident, 0.0, cols[:, s.col + K_BV:s.col + K_BV + 1],
                                        ALU.mult, ALU.add).then_inc(s.bvb_done, 1)
            norm1_a(0)
            dve.wait_ge(ld_rows, 16)
            fold_bo(a, R_BO0)
            dve.wait_ge(a.zeroed, 1)
            keys(a, 0)
            values_spread(a, 0)

            dve.wait_ge(ld_ids, 16)
            dve.wait_ge(ld_toks, 16)
            link(nc.vector.tensor_copy(tf[:, 0, :], ids[:, TILES:]))
            link(nc.vector.tensor_scalar(tf[:, 1, :], tf[:, 0, :], 0.01, None, ALU.mult))
            link(nc.vector.tensor_scalar(tf[:, 2, :], tf[:, 1, :], 4097.0, None, ALU.mult))
            link(nc.vector.tensor_tensor(tf[:, 3, :], tf[:, 2, :], tf[:, 1, :], ALU.subtract))
            link(nc.vector.tensor_tensor(tf[:, 4, :], tf[:, 2, :], tf[:, 3, :], ALU.subtract))
            link(nc.vector.tensor_tensor(tf[:, 5, :], tf[:, 1, :], tf[:, 4, :], ALU.subtract))
            link(nc.vector.scalar_tensor_tensor(tf[:, 6, :], tf[:, 4, :], -100.0, tf[:, 0, :], ALU.mult, ALU.add))
            link(nc.vector.scalar_tensor_tensor(tf[:, 7, :], tf[:, 5, :], -100.0, tf[:, 6, :], ALU.mult, ALU.add))
            link(nc.vector.scalar_tensor_tensor(tf[:, 2, :], tf[:, 7, :], 0.01, tf[:, 1, :], ALU.mult, ALU.add))
            link(nc.vector.tensor_scalar(tf[:, 3, :], tf[:, 2, :], 4000.0, None, ALU.mult))
            nc.vector.tensor_copy(ang[:, 0:2 * TILES], toks[:])
            link(nc.vector.tensor_scalar(ang[:, 2 * TILES:], tf[:, 3, :], const[:, C_FREQ:C_FREQ + 1], None, ALU.mult))
            link(nc.vector.tensor_scalar(ang_k[:, 0, :], ang[:], 1.0 / TWO_PI, ROUND, ALU.mult, ALU.add))
            link(nc.vector.tensor_scalar(ang_k[:, 1, :], ang_k[:, 0, :], -ROUND, None, ALU.add))
            link(nc.vector.scalar_tensor_tensor(ang_r[:, 0, :], ang_k[:, 1, :], -PI_A, ang[:], ALU.mult, ALU.add))
            link(nc.vector.scalar_tensor_tensor(ang_r[:, 1, :], ang_k[:, 1, :], -PI_B, ang_r[:, 0, :], ALU.mult, ALU.add))
            link(nc.vector.scalar_tensor_tensor(ang_r[:, 2, :], ang_k[:, 1, :], -PI_C, ang_r[:, 1, :], ALU.mult, ALU.add))
            link(nc.vector.tensor_scalar(ang_r[:, 3, :], ang_r[:, 2, :], -PI_MAX, PI_MAX, ALU.max, ALU.min))
            nc.vector.tensor_scalar(arg[:, 0:2 * TILES], ang_r[:, 3, 0:2 * TILES], 1.0, None, ALU.mult)
            link(nc.vector.scalar_tensor_tensor(ang_r[:, 0, :], ang_r[:, 3, :], -1.0, ang_r[:, 3, :], ALU.mult, ALU.max))
            nc.vector.tensor_scalar(arg[:, 2 * TILES:4 * TILES], ang_r[:, 0, 0:2 * TILES], -1.0, TWO_PI / 4,
                                    ALU.mult, ALU.add)
            link(nc.vector.tensor_scalar(emb_abs[:, 0, :], ang_r[:, 0, 2 * TILES:], const[:, C_COSM:C_COSM + 1],
                                         const[:, C_COSA:C_COSA + 1], ALU.mult, ALU.add))
            nc.vector.scalar_tensor_tensor(arg[:, 4 * TILES:], ang_r[:, 3, 2 * TILES:], const[:, C_SIN:C_SIN + 1],
                                           emb_abs[:, 0, :], ALU.mult, ALU.add).then_inc(arg_done, 1)
            link(nc.vector.tensor_copy(idf[:, 0, :], ids[:, 0:TILES]))
            link(nc.vector.tensor_scalar(idf[:, 1, :], idf[:, 0, :], 0.0, float(E - 1), ALU.max, ALU.min))
            nc.vector.tensor_scalar(idx[:], idf[:, 1, :], float(A), const[:, C_OUT:C_OUT + 1],
                                    ALU.mult, ALU.add).then_inc(idx_done, 1)
            link(nc.vector.tensor_tensor(idf[:, 2, :], idf[:, 1, :], idf[:, 0, :], ALU.is_equal))
            link(nc.vector.tensor_scalar(idf[:, 3, :], idf[:, 2, :], -1.0, 1.0, ALU.mult, ALU.add))

            def attention_a(i):
                for t in range(T + 2):
                    if t < T:
                        row_max(a, i, t)
                    if t >= 1 and t - 1 < T:
                        row_sum(a, i, t - 1)
                    if t >= 2:
                        turn_probs(a, i, t - 2)

            attention_a(0)
            after_attention(a, 0)
            dve.wait_ge(a.x1_done, 1)
            norm_stats(a.ln2, tile_of(a.x1), 0)
            norm_apply(a.ln2, tile_of(a.x1), 0)

            dve.wait_ge(trig_done, 1)
            sines = trig[:, 0:2 * TILES].rearrange("p (w t) -> p t w", w=2)
            cosines = trig[:, 2 * TILES:4 * TILES].rearrange("p (w t o) -> p t w o", w=2, o=1)
            for c in range(CH):
                tiles = slice(c * T, (c + 1) * T)
                nc.vector.tensor_copy(tabs[:, c, T_SIN:T_SIN + 2 * T].rearrange("p (t w) -> p t w", w=2), sines[:, tiles, :])
                nc.vector.tensor_copy(
                    tabs[:, c, T_COS:T_COS + 4 * T].rearrange("p (t w e) -> p t w e", w=2, e=2),
                    cosines[:, tiles, :, :].to_broadcast([P, T, 2, 2]))
            fold_bo(b, R_BO1)
            dve.wait_ge(ada_mm, 1)
            chunks = b.S2[1][:, 0:2 * B].rearrange("p (w c n) -> p w c n", w=2, c=CH)
            nc.vector.tensor_scalar(tabs[:, :, T_SCALE:T_SCALE + CB], chunks[:, 0], cols[:, K_ADA:K_ADA + 1], 1.0, ALU.add, ALU.add)
            nc.vector.tensor_scalar(tabs[:, :, T_SHIFT:T_SHIFT + CB], chunks[:, 1], cols[:, K_ADA + 1:K_ADA + 2], None,
                                    ALU.add).then_inc(ada_done, 1)
            dve.wait_ge(gathered, 16 * TILES)
            nc.vector.tensor_tensor(wsel[:, 0, :, :], got[:, :, 0:A], spread(idf[:, 2, :], TILES, A), ALU.mult)
            nc.vector.tensor_tensor(bsel[:], got[:, :, A], idf[:, 2, :], ALU.mult)
            eye = const[:, C_EYE:C_EYE + A].rearrange("p (o a) -> p o a", o=1).to_broadcast([P, TILES, A])
            link(nc.vector.tensor_tensor(wsel[:, 1, :, :], eye, spread(idf[:, 3, :], TILES, A), ALU.mult))
            nc.vector.tensor_tensor(tabs[:, :, T_BIAS:T_BIAS + T], bsel[:].rearrange("p (c t) -> p c t", c=CH),
                                    got[:, :, A + 1].rearrange("p (c t) -> p c t", c=CH), ALU.add)
            link(nc.vector.tensor_tensor(wsel[:, 2, :, :], wsel[:, 0, :, :], wsel[:, 1, :, :], ALU.add))
            for c in range(CH):
                last = nc.vector.transpose(tabs[:, c, T_W:], wsel[:, 2, c * T:(c + 1) * T, :].rearrange("p t a -> p (t a)"))
            last.then_inc(tables_done, 1)
            block_out_a(0)
            dve.wait_ge(tables_done, 1)
            dve.wait_ge(b.zeroed, 1)

            def both(i):
                chunk_tables(i - 1)
                dve.wait_ge(a.y_done, i)
                norm_stats(b.ln1, tile_of(xn), i - 1)
                stats1_a(i)
                norm_apply(b.ln1, tile_of(xn), i - 1)
                norm_apply(a.ln1, tile_of(x), i)
                modulate(i - 1)
                keys(b, i - 1)
                keys(a, i)
                values_spread(b, i - 1)
                values_spread(a, i)
                for t in range(T + 2):
                    if t < T:
                        row_max(b, i - 1, t)
                        row_max(a, i, t)
                    if t >= 1 and t - 1 < T:
                        row_sum(b, i - 1, t - 1)
                        row_sum(a, i, t - 1)
                    if t >= 2:
                        turn_probs(b, i - 1, t - 2)
                        turn_probs(a, i, t - 2)
                after_attention(b, i - 1)
                dve.wait_ge(b.x1_done, i)
                norm_stats(b.ln2, tile_of(b.x1), i - 1)
                after_attention(a, i)
                norm_apply(b.ln2, tile_of(b.x1), i - 1)
                dve.wait_ge(a.x1_done, i + 1)
                norm_stats(a.ln2, tile_of(a.x1), i)
                norm_apply(a.ln2, tile_of(a.x1), i)
                block_out_b(i - 1)
                expert_bias(i - 1)
                block_out_a(i)
                adapter_out(i - 1)
                norm3(i - 1)

            both(1)
            with dve.Fori(2, CH) as i:
                both(i)

            i = CH - 1
            chunk_tables(i)
            dve.wait_ge(a.y_done, i + 1)
            norm_stats(b.ln1, tile_of(xn), i)
            norm_apply(b.ln1, tile_of(xn), i)
            modulate(i)
            keys(b, i)
            values_spread(b, i)
            for t in range(T + 2):
                if t < T:
                    row_max(b, i, t)
                if t >= 1 and t - 1 < T:
                    row_sum(b, i, t - 1)
                if t >= 2:
                    turn_probs(b, i, t - 2)
            after_attention(b, i)
            dve.wait_ge(b.x1_done, i + 1)
            norm_stats(b.ln2, tile_of(b.x1), i)
            norm_apply(b.ln2, tile_of(b.x1), i)
            block_out_b(i)
            expert_bias(i)
            adapter_out(i)
            norm3(i)

        @block.gpsimd
        def _(pool):
            def norm_rstd(ln, i):
                pool.wait_ge(ln.mv_done, i + 1)
                nc.gpsimd.tensor_tensor(ln.ve[:], ln.mv[:, :, 1], eps[:], ALU.add).then_inc(ln.ve_done, 1)
                pool.wait_ge(ln.ve_done, i + 1)
                nc.gpsimd.tensor_tensor(ln.rstd[:], ln.ve[:], mhalf[:], ALU.pow).then_inc(ln.rstd_done, 1)

            def probabilities(s, i, t):
                n = i * T + t
                k = t % 2
                pool.wait_ge(s.rc_done, n + 1)
                wait(pool, s.pt_done, two_ago(n, t))
                nc.gpsimd.tensor_tensor(groups(s.Pn[:, k, :]), groups(s.Ex[:, k, :]), spread(s.rc[:, k, :], CB, S),
                                        ALU.mult).then_inc(s.pn_done, 1)

            def subtract_max(i, t):
                k = t % 2
                pool.wait_ge(b.mx_done, i * T + t + 1)
                nc.gpsimd.tensor_tensor(groups(b.Dm[:, k, :]), groups(b.Dm[:, k, :]), spread(b.mx[:, k, :], CB, S),
                                        ALU.subtract).then_inc(b.sub_done, 1)

            def residual_a(i):
                wait(pool, a.x1_done, i)
                pool.wait_ge(ld_x, 16 * (i + 1))
                nc.gpsimd.tensor_tensor(xb[:], x, over_tiles(a.bo[:]), ALU.add).then_inc(xb_done, 1)

            def rest_a(i):
                pool.wait_ge(a.x1_done, i + 1)
                nc.gpsimd.tensor_tensor(aw[:, 1, :, :], a.x1[:], over_tiles(rows[:, R_B20:R_B20 + D]),
                                        ALU.add).then_inc(aw_done, 1)
                pool.wait_ge(aw_done, 4 * i + 1)
                nc.gpsimd.tensor_tensor(aw[:, 2, :, :], aw[:, 1, :, :], x, ALU.subtract).then_inc(aw_done, 1)
                pool.wait_ge(aw_done, 4 * i + 2)
                nc.gpsimd.tensor_tensor(aw[:, 1, :, :], aw[:, 2, :, :], spread(gate, T, D),
                                        ALU.mult).then_inc(aw_done, 1)
                pool.wait_ge(aw_done, 4 * i + 3)
                wait(pool, a.y_done, i)
                nc.gpsimd.tensor_tensor(aw[:, 0, :, :], aw[:, 1, :, :], x, ALU.add).then_inc(aw_done, 1)

            def add_shift(i):
                pool.wait_ge(tab_done, i + 1)
                pool.wait_ge(xm_done, i + 1)
                nc.gpsimd.tensor_tensor(groups(b.hT[:]), groups(xm[:]),
                                        spread(tab[:, T_SHIFT:T_SHIFT + CB], CB, S), ALU.add).then_inc(b.hT_done, 1)

            def rest_b(i):
                pool.wait_ge(b.x1_done, i + 1)
                wait(pool, b.y_done, i)
                nc.gpsimd.tensor_tensor(b.rest[:], b.x1[:], over_tiles(rows[:, R_B21:R_B21 + D]),
                                        ALU.add).then_inc(b.rest_done, 1)

            def rotate(i):
                pool.wait_ge(b.y_done, i + 1)
                v = xr[:].rearrange("p t (q w e) -> p t q w e", w=2, e=2)
                s2 = tab[:, T_SIN:T_SIN + 2 * T].rearrange("p (t o w) -> p t o w", o=1, w=2).to_broadcast([P, T, D // 4, 2])
                for e in range(2):
                    o = rs4[:, e, :].rearrange("p (t q w) -> p t q w", t=T, w=2)
                    nc.gpsimd.tensor_tensor(o, v[:, :, :, :, 1 - e], s2, ALU.mult).then_inc(rs4_done, 1)

            def residual_y(i):
                pool.wait_ge(rot_done, i + 1)
                wait(pool, z_done, i)
                nc.gpsimd.tensor_tensor(yb[:], y[:], over_tiles(rows[:, R_UP:R_UP + D]), ALU.add).then_inc(yb_done, 1)

            def expert_blocks(i):
                wait(pool, ex_mm, i)
                w = tab[:, T_W:T_W + T * A].rearrange("p (t o a) -> p t o a", o=1, a=A).to_broadcast([P, T, R, A])
                m = block_mask.rearrange("p (o j a) -> p o j a", o=1, a=A).to_broadcast([P, T, R, A])
                nc.gpsimd.tensor_tensor(wblk[:].rearrange("p t (j a) -> p t j a", a=A), w, m,
                                        ALU.mult).then_inc(wblk_done, 1)

            def norm3_out(i):
                pool.wait_ge(ln3.xh_done, i + 1)
                nc.gpsimd.tensor_tensor(og[:], ln3.xh[:], over_tiles(rows[:, R_LNG:R_LNG + D]), ALU.mult).then_inc(og_done, 1)
                pool.wait_ge(og_done, i + 1)
                wait(pool, stored, 16 * i)
                nc.gpsimd.tensor_tensor(ob[:], og[:], over_tiles(rows[:, R_LNB:R_LNB + D]), ALU.add).then_inc(ob_done, 1)

            nc.gpsimd.memset(eps[:], EPS)
            nc.gpsimd.memset(mhalf[:], -0.5).then_inc(mhalf_done, 1)
            pool.wait_ge(mhalf_done, 1)
            norm_rstd(a.ln1, 0)
            nc.gpsimd.memset(a.Km[:], 0.0)
            nc.gpsimd.memset(a.Vm[:], 0.0).then_inc(a.zeroed, 1)
            pool.wait_ge(a.bo_done, 1)
            residual_a(0)
            for t in range(T):
                probabilities(a, 0, t)
            pool.wait_ge(idx_done, 1)
            for t in range(TILES):
                nc.gpsimd.indirect_dma_start(got[:, t, :], None, etab_in,
                                             bass.IndirectOffsetOnAxis(ap=idx[:, t:t + 1], axis=0)).then_inc(gathered, 16)
            norm_rstd(a.ln2, 0)
            rest_a(0)
            nc.gpsimd.memset(b.Km[:], 0.0)
            nc.gpsimd.memset(b.Vm[:], 0.0).then_inc(b.zeroed, 1)
            pool.wait_ge(ld_mask, 16)
            nc.gpsimd.tensor_scalar(maskb[:].rearrange("p n k -> p (n k)"), mask4[:].bitcast(U8), NEG, None,
                                    ALU.mult).then_inc(maskb_done, 1)

            def both(i):
                norm_rstd(b.ln1, i - 1)
                norm_rstd(a.ln1, i)
                add_shift(i - 1)
                residual_a(i)
                expert_blocks(i - 1)
                for t in range(T + 1):
                    if t < T:
                        subtract_max(i - 1, t)
                    if t >= 1:
                        probabilities(b, i - 1, t - 1)
                        probabilities(a, i, t - 1)
                norm_rstd(b.ln2, i - 1)
                norm_rstd(a.ln2, i)
                rest_b(i - 1)
                rest_a(i)
                rotate(i - 1)
                residual_y(i - 1)
                norm_rstd(ln3, i - 1)
                norm3_out(i - 1)

            both(1)
            with pool.Fori(2, CH) as i:
                both(i)

            i = CH - 1
            norm_rstd(b.ln1, i)
            add_shift(i)
            expert_blocks(i)
            for t in range(T + 1):
                if t < T:
                    subtract_max(i, t)
                if t >= 1:
                    probabilities(b, i, t - 1)
            norm_rstd(b.ln2, i)
            rest_b(i)
            rotate(i)
            residual_y(i)
            norm_rstd(ln3, i)
            norm3_out(i)


def constants():
    c = np.zeros((P, N_CONST), np.float32)
    p = np.arange(P)
    c[:, C_IDENT:C_IDENT + P] = np.eye(P)
    c[:, C_BLOCK:C_BLOCK + P] = p[:, None] // S == p[None, :] // S
    c[:, C_CAUSAL:C_CAUSAL + S] = np.where(np.arange(S)[None, :] > (p % S)[:, None], NEG, 0.0)
    c[:, C_EYE:C_EYE + A] = (p % A)[:, None] == np.arange(A)[None, :]
    c[:, C_HEAD:C_HEAD + R] = ((p // DH % R)[:, None] == np.arange(R)[None, :]) / np.sqrt(DH)
    half = D // 2
    freq = np.exp(np.arange(half, dtype=np.float32) * np.float32(-np.log(10000.0) / (half - 1)))
    c[:, C_FREQ] = np.concatenate([freq, freq])
    c[:, C_OUT] = p % A
    c[:, C_SIN] = p < half
    c[:, C_COSM] = -(p >= half).astype(np.float32)
    c[:, C_COSA] = (p >= half) * (np.pi / 2)
    return c


def kernel(**inputs):
    import concourse.bacc as bacc
    from concourse.bass_utils import run_bass_kernel_spmd

    v = {k: np.asarray(a) for k, a in inputs.items()}

    def block_weights(n):
        w2 = v[n + "W2"].reshape(FC, P, D).transpose(1, 0, 2).reshape(P, FC * D)
        return np.concatenate([v[n + "Wq"], v[n + "Wk"], v[n + "Wv"], v[n + "Wo"], v[n + "W1"], w2], axis=1)

    def block_columns(n, g, be):
        return [v[n + "bq"], v[n + "bk"], v[n + "bv"], v[n + g], v[n + be], *v[n + "b1"].reshape(FC, P)]

    def beside(rows):
        return np.broadcast_to(np.concatenate(rows)[None, :], (P, sum(len(r) for r in rows)))

    def of_token(a):
        return np.repeat(a.reshape(TILES, R), S, axis=1).T

    arrays = {
        "x_in": np.concatenate([v["x"].reshape(CH, T, P, D).transpose(2, 0, 1, 3).reshape(P, CH, CT),
                                of_token(v["condB_gatescore"]).reshape(P, CH, T)], axis=2).reshape(P, CH * (CT + T)),
        "bias_in": v["fside_Bx16xSxS_0"].reshape(B, R, R, S, S).transpose(2, 3, 0, 1, 4).reshape(P, B * R * S),
        "mask_in": np.tile(v["mask_Bx1xSxS_bk0"].reshape(B, S, S).transpose(1, 0, 2).reshape(S, B * S),
                           (R, 1)).view(np.int32),
        "w0_in": block_weights("L0_cond_"),
        "w1_in": block_weights("L1_cond_"),
        "wx_in": np.concatenate([v["L1_cond_W_ada"], np.tile(v["L3_cond_down_W"].T, (1, R)),
                                 np.tile(v["L3_cond_up_W"].T, (R, 1))], axis=1),
        "rows_in": beside([v["L0_cond_bo"], v["L0_cond_b2"], v["L1_cond_bo"], v["L1_cond_b2"],
                           v["L3_cond_up_b"], v["L3_cond_ln_gamma"], v["L3_cond_ln_beta"]]),
        "cols_in": np.stack(block_columns("L0_cond_", "gamma2", "beta2") + block_columns("L1_cond_", "g2", "beta2")
                            + [v["L0_cond_gamma1"], v["L0_cond_beta1"], *v["L1_cond_b_ada"].reshape(2, D),
                               np.tile(v["L3_cond_down_b"], R)], axis=1),
        "toks_in": np.concatenate([of_token(v["condB_theta"]), of_token(v["condB_phi"])], axis=1),
        "ids_in": np.concatenate([of_token(v["itok_B_0_15"]),
                                  np.broadcast_to(v["itok_B_34_63"][None, :], (P, B))], axis=1),
        "etab_in": np.concatenate([v["L3_cond_expert_W"].reshape(E * A, A), v["L3_cond_expert_b"].reshape(E * A, 1),
                                   v["L3_cond_domain_emb"].reshape(E * A, 1)], axis=1),
        "const_in": constants(),
    }
    arrays = {k: np.ascontiguousarray(a) for k, a in arrays.items()}
    nc = bacc.Bacc("TRN2", target_bir_lowering=False, num_devices=1)
    args = [nc.dram_tensor(k, a.shape, mybir.dt.from_np(a.dtype), kind="ExternalInput").ap()
            for k, a in arrays.items()]
    out = nc.dram_tensor("out", (P, TILES * D), F32, kind="ExternalOutput").ap()
    cond_seq_kernel(nc, *args, out)
    r = run_bass_kernel_spmd(nc, [arrays], core_ids=[0])
    got = r.results[0]["out"].reshape(P, TILES, D).transpose(1, 0, 2).reshape(B, S, D)
    return np.ascontiguousarray(got)
```

```python
from contextlib import ExitStack

import numpy as np

import concourse.bass as bass
from concourse import mybir

F32 = mybir.dt.float32
BF16 = mybir.dt.bfloat16
I32 = mybir.dt.int32
U32 = mybir.dt.uint32
U8 = mybir.dt.uint8
ALU = mybir.AluOpType
ACT = mybir.ActivationFunctionType
AX = mybir.AxisListType.X

B, S, D = 64, 32, 128
H, DH = 16, 8
DFF = 512
E, A = 16, 32
P = 128
R = 4
TILES = B * S // P
T = 4
CH = TILES // T
CB = T * R
CT = T * P
NC = CH // 2
TW = R * P
FC = DFF // P
EPS = 1e-5
NEG = -1e30
TWO_PI = 6.283185307179586
PI_A = 6.28125
PI_B = 0.0019350051879882812
PI_C = TWO_PI - PI_A - PI_B
ROUND = 12582912.0
PI_MAX = 3.1415925

T_SCALE, T_SHIFT, T_COS, T_SIN, T_BIAS, T_W = 0, CB, 2 * CB, 2 * CB + 4 * T, 2 * CB + 6 * T, 2 * CB + 7 * T
N_TAB = T_W + T * A

C_IDENT, C_BLOCK, C_CAUSAL, C_EYE, C_HEAD, C_FREQ, C_OUT, C_SIN, C_COSM, C_COSA = (
    0, 128, 256, 288, 320, 324, 325, 326, 327, 328)
N_CONST = 329
W_Q, W_K, W_V, W_O, W_1, W_2 = 0, 128, 256, 384, 512, 1024
R_BO0, R_B20, R_BO1, R_B21, R_UP, R_LNG, R_LNB = (128 * n for n in range(7))
K_BQ, K_BK, K_BV, K_G2, K_BETA2, K_B1 = 0, 1, 2, 3, 4, 5
K_STREAM = 9
K_G1, K_BETA1, K_ADA, K_DOWN = 18, 19, 20, 22
N_COLS = 23


class Stream:

    def __init__(self, sb, ps, sem, name, number):
        self.number = number
        self.stats = sb(name + "_stats", [P, T, 6], F32)
        self.mv = sb(name + "_mv", [P, T, 2], F32)
        self.ve = sb(name + "_ve", [P, T], F32)
        self.rstd = sb(name + "_rstd", [P, T], F32)
        self.xh = sb(name + "_xh", [P, T, D], F32)
        self.xg = sb(name + "_xg", [P, CT + T], F32)
        self.x = self.xg[:, 0:CT].rearrange("p (t d) -> p t d", d=D)
        self.gate = self.xg[:, CT:]
        self.gate_kept = sb(name + "_gate_kept", [P, T], F32)
        self.xb = sb(name + "_xb", [P, T, D], F32)
        self.hT = sb(name + "_hT", [P, CT], F32)
        self.Qm = sb(name + "_Qm", [P, CB, R, S], F32)
        self.Km = sb(name + "_Km", [P, CB, R, S], F32)
        self.Vm = sb(name + "_Vm", [P, CB, D], F32)
        self.mx = sb(name + "_mx", [P, 2, 16], F32)
        self.sm = sb(name + "_sm", [P, 2, 16], F32)
        self.rc = sb(name + "_rc", [P, 2, 16], F32)
        self.Dm = sb(name + "_Dm", [P, 2, TW], F32)
        self.Ex = sb(name + "_Ex", [P, 2, TW], F32)
        self.Pn = sb(name + "_Pn", [P, 2, TW], F32)
        self.PT = sb(name + "_PT", [P, 2, TW], F32)
        self.ctxT = sb(name + "_ctxT", [P, CT], F32)
        self.x1 = sb(name + "_x1", [P, T, D], F32)
        self.rest = sb(name + "_rest", [P, T, D], F32)
        self.fT = self.Qm[:].rearrange("p n r q -> p (n r q)").rearrange("p (c n) -> p c n", c=FC)
        self.xo = sb(name + "_xo", [P, T, D], F32)
        self.tab = sb(name + "_tab", [P, N_TAB], F32)
        self.xm = sb(name + "_xm", [P, CT], F32)
        self.yT = self.xm
        self.rc4 = sb(name + "_rc4", [P, T, D], F32)
        self.rs4 = sb(name + "_rs4", [P, 2, CT // 2], F32)
        self.y = self.x1
        self.yb = sb(name + "_yb", [P, T, D], F32)
        self.wblk = sb(name + "_wblk", [P, T, P], F32)
        self.hid = sb(name + "_hid", [P, CT], F32)
        self.em = sb(name + "_em", [P, T, P], F32)
        self.z = sb(name + "_z", [P, T, D], F32)
        self.og = self.yb
        self.ob = sb(name + "_ob", [P, T, D], F32)
        self.P0 = ps(name + "_P0", [P, 512], F32)[:, 0:CT]
        self.P1 = ps(name + "_P1", [P, 512], F32)[:, 0:CT]
        self.S2 = [ps(name + f"_S{n}", [P, 512], F32) for n in range(2)]

        self.ld_x = sem(name + "_ld_x")
        self.zeroed = sem(name + "_zeroed")
        self.gate_done = sem(name + "_gate_done")
        self.mv_done = sem(name + "_mv_done")
        self.ve_done = sem(name + "_ve_done")
        self.rstd_done = sem(name + "_rstd_done")
        self.xh_done = sem(name + "_xh_done")
        self.turned = sem(name + "_turned")
        self.xb_done = sem(name + "_xb_done")
        self.tab_done = sem(name + "_tab_done")
        self.xm_done = sem(name + "_xm_done")
        self.hT_done = sem(name + "_hT_done")
        self.q_mm = sem(name + "_q_mm")
        self.k_mm = sem(name + "_k_mm")
        self.v_mm = sem(name + "_v_mm")
        self.qm_done = sem(name + "_qm_done")
        self.km_done = sem(name + "_km_done")
        self.vm_act = sem(name + "_vm_act")
        self.vm_dve = sem(name + "_vm_dve")
        self.sc_mm = sem(name + "_sc_mm")
        self.s_free = sem(name + "_s_free")
        self.mx_done = sem(name + "_mx_done")
        self.sub_done = sem(name + "_sub_done")
        self.ex_done = sem(name + "_ex_done")
        self.sm_done = sem(name + "_sm_done")
        self.rc_done = sem(name + "_rc_done")
        self.pn_done = sem(name + "_pn_done")
        self.pt_done = sem(name + "_pt_done")
        self.pv_mm = sem(name + "_pv_mm")
        self.ctx_done = sem(name + "_ctx_done")
        self.o_mm = sem(name + "_o_mm")
        self.x1_done = sem(name + "_x1_done")
        self.rest0_done = sem(name + "_rest0_done")
        self.rest1_done = sem(name + "_rest1_done")
        self.h2T_done = sem(name + "_h2T_done")
        self.f_mm = sem(name + "_f_mm")
        self.f_done = sem(name + "_f_done")
        self.y_mm = sem(name + "_y_mm")
        self.xo_done = sem(name + "_xo_done")
        self.rc4_done = sem(name + "_rc4_done")
        self.rs4_done = sem(name + "_rs4_done")
        self.rot_done = sem(name + "_rot_done")
        self.yb_done = sem(name + "_yb_done")
        self.y_turned = sem(name + "_y_turned")
        self.yT_done = sem(name + "_yT_done")
        self.down_mm = sem(name + "_down_mm")
        self.hid_done = sem(name + "_hid_done")
        self.wblk_done = sem(name + "_wblk_done")
        self.ex_mm = sem(name + "_ex_mm")
        self.em_done = sem(name + "_em_done")
        self.up_mm = sem(name + "_up_mm")
        self.z_done = sem(name + "_z_done")
        self.og_done = sem(name + "_og_done")
        self.ob_done = sem(name + "_ob_done")
        self.stored = sem(name + "_stored")


class Block:

    def __init__(self, sb, sem, name, col):
        self.col = col
        self.w = sb(name + "_w", [P, 4 * D + 2 * DFF], F32)
        self.bqm = sb(name + "_bqm", [P, R], F32)
        self.bvb = sb(name + "_bvb", [P, D], F32)
        self.bo = sb(name + "_bo", [P, D], F32)
        self.loaded = sem(name + "_loaded")
        self.bqm_done = sem(name + "_bqm_done")
        self.bvb_done = sem(name + "_bvb_done")
        self.bo_mm = sem(name + "_bo_mm")
        self.bo_done = sem(name + "_bo_done")


def wait(eng, sem, value):
    if isinstance(value, int) and value <= 0:
        return
    eng.wait_ge(sem, value)


def two_ago(n, t):
    return n if t == 0 else n - 1


def run(joint, Fori, even, odd):
    def round_of(c, before):
        joint((even, c, 0), before)
        joint((odd, c, 0), (even, c, 0))
        joint((even, c, 1), (odd, c, 0))
        joint((odd, c, 1), (even, c, 1))

    round_of(0, None)
    with Fori(1, NC) as c:
        round_of(c, (odd, c - 1, 1))
    joint(None, (odd, NC - 1, 1))


def cond_seq_kernel(nc, x_in, bias_in, mask_in, w0_in, w1_in, wx_in, rows_in, cols_in, toks_in,
                    ids_in, etab_in, const_in, out):
    with ExitStack() as ctx:
        def sb(name, shape, dt):
            return ctx.enter_context(nc.sbuf_tensor(name, shape, dt))

        def ps(name, shape, dt):
            return ctx.enter_context(nc.psum_tensor(name, shape, dt))

        def sem(name):
            return ctx.enter_context(nc.semaphore(name))

        even = Stream(sb, ps, sem, "even", 0)
        odd = Stream(sb, ps, sem, "odd", 1)
        blocks = (Block(sb, sem, "l0", 0), Block(sb, sem, "l1", K_STREAM))

        const = sb("const", [P, N_CONST], F32)
        cols = sb("cols", [P, N_COLS], F32)
        rows = sb("rows", [P, 7 * D], F32)
        wx = sb("wx", [P, 4 * D], F32)
        toks = sb("toks", [P, 2 * TILES], F32)
        ids = sb("ids", [P, TILES + B], I32)
        bias = sb("bias", [P, T, TW], F32)
        mask4 = sb("mask4", [P, B * S // 4], I32)
        maskb = sb("maskb", [P, B, S], BF16)
        identb = sb("identb", [P, P], BF16)
        causalb = sb("causalb", [P, S], BF16)
        mhalf = sb("mhalf", [P, T], F32)
        eps = sb("eps", [P, T], F32)
        ident = const[:, C_IDENT:C_IDENT + P]
        block_mask = const[:, C_BLOCK:C_BLOCK + P]
        head_mask = const[:, C_HEAD:C_HEAD + R]
        NA = 2 * TILES + B
        ang = sb("ang", [P, NA], F32)
        ang_k = sb("ang_k", [P, 2, NA], F32)
        ang_r = sb("ang_r", [P, 4, NA], F32)
        arg = sb("arg", [P, 2 * 2 * TILES + B], F32)
        trig = sb("trig", [P, 2 * 2 * TILES + B], F32)
        tf = sb("tf", [P, 8, B], F32)
        emb_abs = sb("emb_abs", [P, B], F32)
        emb = sb("emb", [P, B], F32)
        tabs = sb("tabs", [P, CH, N_TAB], F32)
        idf = sb("idf", [P, 4, TILES], F32)
        idx = sb("idx", [P, TILES], U32)
        got = sb("got", [P, TILES, A + 2], F32)
        wsel = sb("wsel", [P, 2, TILES, A], F32)
        bsel = sb("bsel", [P, TILES], F32)

        ld_const = sem("ld_const")
        ld_ids = sem("ld_ids")
        ld_rows = sem("ld_rows")
        ld_toks = sem("ld_toks")
        ld_wx = sem("ld_wx")
        ld_mask = sem("ld_mask")
        ld_bias = [sem(f"ld_bias{t}") for t in range(T)]
        consts_b = sem("consts_b")
        maskb_done = sem("maskb_done")
        mhalf_done = sem("mhalf_done")
        chain = sem("chain")
        arg_done = sem("arg_done")
        trig_done = sem("trig_done")
        emb_done = sem("emb_done")
        ada_mm = sem("ada_mm")
        ada_done = sem("ada_done")
        tables_done = sem("tables_done")
        idx_done = sem("idx_done")
        gathered = sem("gathered")

        def over_tiles(row):
            return row.rearrange("p (o d) -> p o d", o=1).to_broadcast([P, T, D])

        def spread(col, n, k):
            return col.rearrange("p (n o) -> p n o", o=1).to_broadcast([P, n, k])

        def groups(ap):
            return ap.rearrange("p (n k) -> p n k", k=S)

        def tiled(ap):
            return ap.rearrange("p (t d) -> p t d", d=D)

        def pairs(buf):
            v = buf[:].rearrange("p t (q e) -> p (t q) e", e=2)
            return v[:, :, 0], v[:, :, 1]

        block = ctx.enter_context(nc.Block())

        @block.sync
        def _(sp):
            def load_x(s, c):
                wait(sp, s.rest0_done, 4 * c)
                wait(sp, s.gate_done, c)
                sp.dma_start(s.xg[:], x_in[:, bass.ds((2 * c + s.number) * (CT + T), CT + T)]).then_inc(s.ld_x, 16)

            def load_bias(s, c, first=False):
                for t in range(T):
                    if s is odd:
                        sp.wait_ge(even.s_free, (2 * c + 1) * T + t + 1)
                    elif not first:
                        sp.wait_ge(odd.s_free, (2 * c - 1) * T + t + 1)
                    at = ((2 * c + s.number) * T + t) * TW
                    sp.dma_start(bias[:, t, :], bias_in[:, bass.ds(at, TW)]).then_inc(ld_bias[t], 16)

            def store(s, c):
                sp.wait_ge(s.ob_done, c + 1)
                sp.dma_start(out[:, bass.ds((2 * c + s.number) * CT, CT)],
                             s.ob[:].rearrange("p t d -> p (t d)")).then_inc(s.stored, 16)

            load_x(even, 0)
            sp.dma_start(const[:], const_in).then_inc(ld_const, 16)
            sp.dma_start(blocks[0].w[:], w0_in).then_inc(blocks[0].loaded, 16)
            sp.dma_start(rows[:], rows_in).then_inc(ld_rows, 16)
            load_x(odd, 0)
            sp.dma_start(mask4[:], mask_in).then_inc(ld_mask, 16)
            sp.dma_start(blocks[1].w[:], w1_in).then_inc(blocks[1].loaded, 16)
            load_bias(even, 0, first=True)
            load_bias(odd, 0)
            with sp.Fori(1, NC) as c:
                load_x(even, c)
                load_x(odd, c)
                load_bias(even, c)
                store(even, c - 1)
                store(odd, c - 1)
                load_bias(odd, c)
            store(even, NC - 1)
            store(odd, NC - 1)
            sp.wait_ge(even.stored, 16 * NC)
            sp.wait_ge(odd.stored, 16 * NC)

        @block.tensor
        def _(pe):
            def turn(src, bank, done):
                for t in range(T):
                    last = pe.transpose(bank[:, t * P:(t + 1) * P], src[:, t, :], ident)
                last.then_inc(done, 1)

            def turn1(s, c, l):
                if l == 0:
                    wait(pe, s.em_done, c)
                else:
                    pe.wait_ge(s.h2T_done, 2 * c + 1)
                pe.wait_ge(s.xh_done, 5 * c + 2 * l + 1)
                turn(s.xh, s.P0, s.turned)

            def project(s, c, l):
                p = 2 * c + l
                w = blocks[l].w
                if l == 0:
                    wait(pe, s.z_done, c)
                else:
                    pe.wait_ge(s.xo_done, p)
                pe.wait_ge(s.hT_done, p + 1)
                pe.matmul(s.P1, w[:, W_Q:W_Q + D], s.hT[:], start=True, stop=True).then_inc(s.q_mm, 1)
                pe.matmul(s.P0, w[:, W_K:W_K + D], s.hT[:], start=True, stop=True).then_inc(s.k_mm, 1)

            def project_values(s, c, l):
                pe.wait_ge(s.qm_done, 2 * c + l + 1)
                for t in range(T):
                    last = pe.matmul(s.P1[:, t * P:(t + 1) * P], s.hT[:, t * P:(t + 1) * P],
                                     blocks[l].w[:, W_V:W_V + D], start=True, stop=True)
                last.then_inc(s.v_mm, 1)

            def scores(s, c, l, t):
                p = 2 * c + l
                if t == 0:
                    wait(pe, s.f_done, p * FC)
                    pe.wait_ge(s.km_done, p + 1)
                if t >= 2:
                    pe.wait_ge(s.s_free, p * T + t - 1)
                bank = s.S2[t % 2]
                if l == 0:
                    masks = causalb[:].rearrange("p (o k) -> p o k", o=1).to_broadcast([P, R * R, S])
                else:
                    masks = maskb[:, bass.ds((2 * c + s.number) * CB + t * R, R), :].rearrange(
                        "p (n o) k -> p n o k", o=1).to_broadcast([P, R, R, S])
                pe.matmul(bank[:], identb[:], masks, start=True, stop=False)
                for j in range(R):
                    n = t * R + j
                    last = pe.matmul(bank[:, j * P:(j + 1) * P], s.Qm[:, n, :, :], s.Km[:, n, :, :],
                                     start=False, stop=(j == R - 1))
                last.then_inc(s.sc_mm, 1)

            def values(s, c, l, t):
                p = 2 * c + l
                if t == 0:
                    pe.wait_ge(s.vm_act, p + 1)
                    pe.wait_ge(s.vm_dve, p + 1)
                pe.wait_ge(s.pt_done, p * T + t + 1)
                for j in range(R):
                    n = t * R + j
                    for g in range(R):
                        last = pe.matmul(s.P0[32 * g:32 * g + 32, n * S:(n + 1) * S],
                                         s.Vm[:, n, 32 * g:32 * g + 32],
                                         s.PT[:, t % 2, (j * R + g) * S:(j * R + g + 1) * S],
                                         start=True, stop=True, tile_position=(0, 32 * g))
                last.then_inc(s.pv_mm, 1)

            def attention_out(s, c, l):
                pe.wait_ge(s.ctx_done, 2 * c + l + 1)
                for t in range(T):
                    tile = slice(t * P, (t + 1) * P)
                    last = pe.matmul(s.P1[:, tile], s.ctxT[:, tile], blocks[l].w[:, W_O:W_O + D],
                                     start=True, stop=(l == 0))
                    if l == 1:
                        last = pe.matmul(s.P1[:, tile], s.hT[:, tile], ident, start=False, stop=True)
                last.then_inc(s.o_mm, 1)

            def turn2(s, c, l):
                pe.wait_ge(s.xh_done, 5 * c + 2 * l + 2)
                turn(s.xh, s.P0, s.turned)

            def hidden(s, c, l, k):
                p = 2 * c + l
                if k == 0:
                    pe.wait_ge(s.h2T_done, p + 1)
                if k >= 2:
                    pe.wait_ge(s.f_done, p * FC + k - 1)
                pe.matmul(s.S2[k % 2][:, 0:CT], blocks[l].w[:, W_1 + k * P:W_1 + (k + 1) * P], s.hT[:],
                          start=True, stop=True).then_inc(s.f_mm, 1)

            def hidden_out(s, c, l):
                p = 2 * c + l
                pe.wait_ge(s.f_done, (p + 1) * FC)
                pe.wait_ge(s.x1_done, p + 1)
                for t in range(T):
                    for k in range(FC):
                        last = pe.matmul(s.P1[:, t * P:(t + 1) * P], s.fT[:, k, t * P:(t + 1) * P],
                                         blocks[l].w[:, W_2 + k * D:W_2 + (k + 1) * D],
                                         start=(k == 0), stop=(k == FC - 1))
                last.then_inc(s.y_mm, 1)

            def adapter_turn(s, c):
                pe.wait_ge(s.rot_done, c + 1)
                turn(s.y, s.P0, s.y_turned)

            def adapter_down(s, c):
                pe.wait_ge(s.yT_done, c + 1)
                pe.matmul(s.P1, wx[:, 2 * D:3 * D], s.yT[:], start=True, stop=True).then_inc(s.down_mm, 1)

            def adapter_expert(s, c):
                pe.wait_ge(s.hid_done, c + 1)
                pe.wait_ge(s.wblk_done, c + 1)
                for t in range(T):
                    last = pe.matmul(s.P0[:, t * P:(t + 1) * P], s.wblk[:, t, :], s.hid[:, t * P:(t + 1) * P],
                                     start=True, stop=True)
                last.then_inc(s.ex_mm, 1)

            def adapter_up(s, c):
                pe.wait_ge(s.em_done, c + 1)
                for t in range(T):
                    last = pe.matmul(s.P1[:, t * P:(t + 1) * P], s.em[:, t, :], wx[:, 3 * D:4 * D],
                                     start=True, stop=True)
                last.then_inc(s.up_mm, 1)

            def fold_bv(b, bank):
                pe.wait_ge(b.loaded, 16)
                pe.wait_ge(b.bvb_done, 1)
                pe.matmul(bank[:, 0:D], b.bvb[:], b.w[:, W_O:W_O + D], start=True, stop=True).then_inc(b.bo_mm, 1)

            def joint(att, hid):
                if hid:
                    attention_out(*hid)
                if att:
                    turn1(*att)
                if hid:
                    turn2(*hid)
                if att:
                    project(*att)
                if hid:
                    hidden(*hid, 0)
                    hidden(*hid, 1)
                if att:
                    project_values(*att)
                if hid:
                    hidden(*hid, 2)
                    hidden(*hid, 3)
                if att:
                    scores(*att, 0)
                    scores(*att, 1)
                if hid:
                    hidden_out(*hid)
                l3 = hid and hid[2] == 1
                for t in range(2, T + 3):
                    if att and t < T:
                        scores(*att, t)
                    if att and t >= 3:
                        values(*att, t - 3)
                    if l3 and t == 3:
                        adapter_turn(*hid[:2])
                        adapter_down(*hid[:2])
                    if l3 and t == T + 1:
                        adapter_expert(*hid[:2])
                if l3:
                    adapter_up(*hid[:2])

            pe.wait_ge(ld_const, 32)
            pe.wait_ge(consts_b, 1)
            fold_bv(blocks[0], odd.S2[0])
            fold_bv(blocks[1], odd.S2[1])
            pe.wait_ge(ld_wx, 16)
            pe.wait_ge(emb_done, 1)
            ada = odd.P1[:, 0:2 * B]
            pe.matmul(ada[:, 0:B], wx[:, 0:D], emb[:], start=True, stop=True)
            pe.matmul(ada[:, B:2 * B], wx[:, D:2 * D], emb[:], start=True, stop=True).then_inc(ada_mm, 1)
            pe.wait_ge(blocks[0].bo_done, 1)
            pe.wait_ge(blocks[1].bo_done, 1)
            pe.wait_ge(ada_done, 1)
            pe.wait_ge(maskb_done, 1)
            run(joint, pe.Fori, even, odd)

        @block.scalar
        def _(act):
            act.dma_start(cols[:], cols_in).then_inc(ld_const, 16)
            act.dma_start(ids[:], ids_in).then_inc(ld_ids, 16)
            act.dma_start(toks[:], toks_in).then_inc(ld_toks, 16)
            act.dma_start(wx[:], wx_in).then_inc(ld_wx, 16)

            def norm_out(s, c, l):
                if l == 0:
                    act.wait_ge(s.turned, 4 * c + 1)
                    nc.scalar.activation(s.hT[:], s.P0, ACT.Identity, bias=cols[:, K_BETA1:K_BETA1 + 1],
                                         scale=cols[:, K_G1:K_G1 + 1]).then_inc(s.hT_done, 1)

            def queries(s, c, l):
                act.wait_ge(s.q_mm, 2 * c + l + 1)
                for r in range(R):
                    last = nc.scalar.activation(s.Qm[:, :, r, :], groups(s.P1), ACT.Identity,
                                                bias=blocks[l].bqm[:, r:r + 1], scale=head_mask[:, r:r + 1])
                last.then_inc(s.qm_done, 1)

            def keys(s, c, l):
                k = blocks[l].col + K_BK
                act.wait_ge(s.k_mm, 2 * c + l + 1)
                for g in range(R):
                    q = slice(32 * g, 32 * g + 32)
                    last = nc.scalar.activation(s.Km[q, :, g, :], groups(s.P0[q, :]), ACT.Identity,
                                                bias=cols[q, k:k + 1])
                last.then_inc(s.km_done, 1)

            def values_spread(s, c, l):
                act.wait_ge(s.v_mm, 2 * c + l + 1)
                for j in range(2):
                    src = s.P1[32 * j:32 * j + 32, :].rearrange("p (t g r d) -> p t g r d", t=T, g=R, r=R)
                    for r in range(R):
                        dst = s.Vm[32 * r:32 * r + 32, :, :].rearrange(
                            "p (t j) (g r d) -> p t j g r d", j=R, g=R, r=R)
                        last = nc.scalar.activation(dst[:, :, j, :, r, :], src[:, :, :, r, :], ACT.Copy)
                last.then_inc(s.vm_act, 1)

            def exps(s, c, l, t):
                n = (2 * c + l) * T + t
                if l == 0:
                    act.wait_ge(s.s_free, n + 1)
                else:
                    act.wait_ge(s.sub_done, c * T + t + 1)
                wait(act, s.pn_done, two_ago(n, t))
                nc.scalar.activation(s.Ex[:, t % 2, :], s.Dm[:, t % 2, :], ACT.Exp).then_inc(s.ex_done, 1)

            def context(s, c, l):
                p = 2 * c + l
                act.wait_ge(s.pv_mm, (p + 1) * T)
                nc.scalar.activation(s.ctxT[:], s.P0, ACT.Copy).then_inc(s.ctx_done, 1)

            def norm2_out(s, c, l):
                col = blocks[l].col
                act.wait_ge(s.turned, 4 * c + 2 * l + 2)
                nc.scalar.activation(s.hT[:], s.P0, ACT.Identity, bias=cols[:, col + K_BETA2:col + K_BETA2 + 1],
                                     scale=cols[:, col + K_G2:col + K_G2 + 1]).then_inc(s.h2T_done, 1)

            def gelu(s, c, l, k):
                at = blocks[l].col + K_B1 + k
                act.wait_ge(s.f_mm, (2 * c + l) * FC + k + 1)
                nc.scalar.activation(s.fT[:, k, :], s.S2[k % 2][:, 0:CT], ACT.Gelu if l == 0 else ACT.Gelu_apprx_sigmoid,
                                     bias=cols[:, at:at + 1]).then_inc(s.f_done, 1)

            def adapter_in(s, c):
                act.wait_ge(s.y_turned, c + 1)
                nc.scalar.activation(s.yT[:], s.P0, ACT.Copy).then_inc(s.yT_done, 1)

            def adapter_gelu(s, c):
                act.wait_ge(s.down_mm, c + 1)
                nc.scalar.activation(s.hid[:], s.P1, ACT.Gelu, bias=cols[:, K_DOWN:K_DOWN + 1]).then_inc(s.hid_done, 1)

            def joint(att, hid):
                if att:
                    norm_out(*att)
                if hid:
                    norm2_out(*hid)
                if att:
                    queries(*att)
                if hid:
                    gelu(*hid, 0)
                    gelu(*hid, 1)
                if att:
                    keys(*att)
                if hid:
                    gelu(*hid, 2)
                    gelu(*hid, 3)
                if att:
                    values_spread(*att)
                l3 = hid and hid[2] == 1
                for t in range(T):
                    if l3 and t == T - 1:
                        adapter_in(*hid[:2])
                    if att:
                        exps(*att, t)
                if l3:
                    adapter_gelu(*hid[:2])
                if att:
                    context(*att)

            act.wait_ge(ld_const, 32)
            act.wait_ge(arg_done, 1)
            nc.scalar.activation(trig[:], arg[:], ACT.Sin).then_inc(trig_done, 1)
            act.wait_ge(trig_done, 1)
            nc.scalar.activation(emb[:], trig[:, 4 * TILES:], ACT.Silu).then_inc(emb_done, 1)
            for b in blocks:
                act.wait_ge(b.bqm_done, 1)
            act.wait_ge(even.zeroed, 1)
            act.wait_ge(odd.zeroed, 1)
            run(joint, act.Fori, even, odd)

        @block.vector
        def _(dve):
            steps = [0]

            def link(ins):
                steps[0] += 1
                ins.then_inc(chain, 1)
                dve.wait_ge(chain, steps[0])

            def norm_stats(s, src):
                for t in range(T):
                    nc.vector.bn_stats(s.stats[:, t, :], src[:, t, :])
                dve.drain()
                for t in range(T):
                    last = nc.vector.bn_aggr(s.mv[:, t, :], s.stats[:, t, :])
                last.then_inc(s.mv_done, 1)

            def norm_apply(s, src, k):
                dve.wait_ge(s.rstd_done, k + 1)
                for t in range(T):
                    last = nc.vector.tensor_scalar(s.xh[:, t, :], src[:, t, :], s.mv[:, t, 0:1],
                                                   s.rstd[:, t:t + 1], ALU.subtract, ALU.mult)
                last.then_inc(s.xh_done, 1)

            def stats1(s, c, l):
                if l == 0:
                    dve.wait_ge(s.ld_x, 16 * (c + 1))
                    nc.vector.tensor_copy(s.gate_kept[:], s.gate).then_inc(s.gate_done, 1)
                    norm_stats(s, s.x)
                else:
                    dve.wait_ge(s.xo_done, 2 * c + 1)
                    norm_stats(s, s.xo)

            def apply1(s, c, l):
                wait(dve, s.og_done, c)
                norm_apply(s, s.xo if l else s.x, 5 * c + 2 * l)

            def modulate(s, c, l):
                if l == 0:
                    return
                wait(dve, s.rs4_done, 2 * c)
                nc.vector.tensor_copy(s.tab[:], tabs[:, bass.ds(2 * c + s.number, 1), :].rearrange(
                    "p o n -> p (o n)")).then_inc(s.tab_done, 1)
                dve.wait_ge(s.tab_done, c + 1)
                dve.wait_ge(s.turned, 4 * c + 3)
                nc.vector.tensor_tensor(groups(s.xm[:]), groups(s.P0), spread(s.tab[:, T_SCALE:T_SCALE + CB], CB, S),
                                        ALU.mult).then_inc(s.xm_done, 1)

            def values_spread(s, c, l):
                dve.wait_ge(s.v_mm, 2 * c + l + 1)
                for j in range(2, R):
                    src = s.P1[32 * j:32 * j + 32, :].rearrange("p (t g r d) -> p t g r d", t=T, g=R, r=R)
                    for r in range(R):
                        dst = s.Vm[32 * r:32 * r + 32, :, :].rearrange(
                            "p (t j) (g r d) -> p t j g r d", j=R, g=R, r=R)
                        last = nc.vector.tensor_copy(dst[:, :, j, :, r, :], src[:, :, :, r, :])
                last.then_inc(s.vm_dve, 1)

            def row_max(s, c, l, t):
                n = (2 * c + l) * T + t
                k = t % 2
                dve.wait_ge(s.sc_mm, n + 1)
                if l == 0:
                    nc.vector.tensor_reduce(s.mx[:, k, :], groups(s.S2[k][:]), AX, ALU.max).then_inc(s.mx_done, 1)
                    dve.wait_ge(s.mx_done, n + 1)
                    wait(dve, s.ex_done, two_ago(n, t))
                    nc.vector.tensor_tensor(groups(s.Dm[:, k, :]), groups(s.S2[k][:]), spread(s.mx[:, k, :], R * R, S),
                                            ALU.subtract).then_inc(s.s_free, 1)
                else:
                    dve.wait_ge(ld_bias[t], (2 * c + s.number + 1) * 16)
                    wait(dve, s.ex_done, two_ago(n, t))
                    nc.vector.tensor_tensor(s.Dm[:, k, :], s.S2[k][:], bias[:, t, :], ALU.add).then_inc(s.s_free, 1)
                    dve.wait_ge(s.s_free, n + 1)
                    nc.vector.tensor_reduce(s.mx[:, k, :], groups(s.Dm[:, k, :]), AX, ALU.max).then_inc(s.mx_done, 1)

            def row_sum(s, c, l, t):
                n = (2 * c + l) * T + t
                k = t % 2
                dve.wait_ge(s.ex_done, n + 1)
                nc.vector.tensor_reduce(s.sm[:, k, :], groups(s.Ex[:, k, :]), AX, ALU.add).then_inc(s.sm_done, 1)
                dve.wait_ge(s.sm_done, n + 1)
                wait(dve, s.pn_done, two_ago(n, t))
                nc.vector.reciprocal(s.rc[:, k, :], s.sm[:, k, :]).then_inc(s.rc_done, 1)

            def turn_probs(s, c, l, t):
                n = (2 * c + l) * T + t
                k = t % 2
                dve.wait_ge(s.pn_done, n + 1)
                wait(dve, s.pv_mm, two_ago(n, t))
                nc.vector.transpose(s.PT[:, k, :], s.Pn[:, k, :]).then_inc(s.pt_done, 1)

            def after_attention(s, c, l):
                dve.wait_ge(s.o_mm, 2 * c + l + 1)
                if l == 0:
                    dve.wait_ge(s.xb_done, c + 1)
                    wait(dve, s.rest1_done, c)
                    nc.vector.tensor_tensor(s.x1[:], tiled(s.P1), s.xb[:], ALU.add).then_inc(s.x1_done, 1)
                else:
                    dve.wait_ge(s.rest0_done, 4 * c + 4)
                    nc.vector.tensor_tensor(s.x1[:], tiled(s.P1), over_tiles(blocks[1].bo[:]),
                                            ALU.add).then_inc(s.x1_done, 1)
                dve.wait_ge(s.x1_done, 2 * c + l + 1)
                norm_stats(s, s.x1)

            def apply2(s, c, l):
                norm_apply(s, s.x1, 5 * c + 2 * l + 1)

            def block_out(s, c, l):
                dve.wait_ge(s.y_mm, 2 * c + l + 1)
                if l == 0:
                    dve.wait_ge(s.gate_done, c + 1)
                    dve.wait_ge(s.rest0_done, 4 * c + 4)
                    wait(dve, s.rs4_done, 2 * c)
                    for t in range(T):
                        last = nc.vector.scalar_tensor_tensor(
                            s.xo[:, t, :], s.P1[:, t * P:(t + 1) * P], s.gate_kept[:, t:t + 1],
                            s.rest[:, t, :], ALU.mult, ALU.add)
                    last.then_inc(s.xo_done, 1)
                else:
                    dve.wait_ge(s.rest1_done, c + 1)
                    nc.vector.tensor_tensor(s.xo[:], tiled(s.P1), s.rest[:], ALU.add).then_inc(s.xo_done, 1)
                    dve.wait_ge(s.xo_done, 2 * c + 2)
                    c4 = s.tab[:, T_COS:T_COS + 4 * T].rearrange("p (t o w) -> p t o w", o=1, w=4)
                    nc.vector.tensor_tensor(quads(s.rc4), quads(s.xo), c4.to_broadcast([P, T, D // 4, 4]),
                                            ALU.mult).then_inc(s.rc4_done, 1)

            def quads(buf):
                return buf[:].rearrange("p t (q w) -> p t q w", w=4)

            def rotate(s, c):
                dve.wait_ge(s.rc4_done, c + 1)
                dve.wait_ge(s.rs4_done, 2 * c + 2)
                wait(dve, s.yb_done, c)
                y_even, y_odd = pairs(s.y)
                c_even, c_odd = pairs(s.rc4)
                nc.vector.tensor_tensor(y_even, c_even, s.rs4[:, 0, :], ALU.add)
                nc.vector.tensor_tensor(y_odd, c_odd, s.rs4[:, 1, :], ALU.subtract).then_inc(s.rot_done, 1)

            def expert_bias(s, c):
                dve.wait_ge(s.ex_mm, c + 1)
                for t in range(T):
                    last = nc.vector.scalar_tensor_tensor(
                        s.em[:, t, :], s.P0[:, t * P:(t + 1) * P], s.tab[:, T_BIAS + t:T_BIAS + t + 1],
                        block_mask, ALU.add, ALU.mult)
                last.then_inc(s.em_done, 1)

            def adapter_out(s, c):
                dve.wait_ge(s.up_mm, c + 1)
                dve.wait_ge(s.yb_done, c + 1)
                nc.vector.tensor_tensor(s.z[:], tiled(s.P1), s.yb[:], ALU.add).then_inc(s.z_done, 1)
                dve.wait_ge(s.z_done, c + 1)
                norm_stats(s, s.z)
                norm_apply(s, s.z, 5 * c + 4)

            def fold_bo(b, bank, row):
                dve.wait_ge(b.bo_mm, 1)
                nc.vector.tensor_tensor(b.bo[:], bank[:, 0:D], rows[:, row:row + D], ALU.add).then_inc(b.bo_done, 1)

            def joint(att, hid):
                if att:
                    stats1(*att)
                if hid:
                    after_attention(*hid)
                if att:
                    apply1(*att)
                if hid:
                    apply2(*hid)
                if att:
                    modulate(*att)
                    values_spread(*att)
                l3 = hid and hid[2] == 1
                for t in range(T + 2):
                    if att and t < T:
                        row_max(*att, t)
                    if att and 1 <= t <= T:
                        row_sum(*att, t - 1)
                    if att and t >= 2:
                        turn_probs(*att, t - 2)
                    if hid and t == 1:
                        block_out(*hid)
                    if l3 and t == 2:
                        rotate(*hid[:2])
                if l3:
                    expert_bias(*hid[:2])
                    adapter_out(*hid[:2])

            dve.wait_ge(ld_const, 32)
            nc.vector.tensor_copy(identb[:], ident)
            nc.vector.tensor_copy(causalb[:], const[:, C_CAUSAL:C_CAUSAL + S]).then_inc(consts_b, 1)
            for b in blocks:
                nc.vector.tensor_scalar(b.bqm[:], head_mask, cols[:, b.col + K_BQ:b.col + K_BQ + 1], None,
                                        ALU.mult).then_inc(b.bqm_done, 1)
                nc.vector.tensor_scalar(b.bvb[:], ident, 0.0, cols[:, b.col + K_BV:b.col + K_BV + 1],
                                        ALU.mult, ALU.add).then_inc(b.bvb_done, 1)
            dve.wait_ge(ld_ids, 16)
            dve.wait_ge(ld_toks, 16)
            link(nc.vector.tensor_copy(tf[:, 0, :], ids[:, TILES:]))
            link(nc.vector.tensor_scalar(tf[:, 1, :], tf[:, 0, :], 0.01, None, ALU.mult))
            link(nc.vector.tensor_scalar(tf[:, 2, :], tf[:, 1, :], 4097.0, None, ALU.mult))
            link(nc.vector.tensor_tensor(tf[:, 3, :], tf[:, 2, :], tf[:, 1, :], ALU.subtract))
            link(nc.vector.tensor_tensor(tf[:, 4, :], tf[:, 2, :], tf[:, 3, :], ALU.subtract))
            link(nc.vector.tensor_tensor(tf[:, 5, :], tf[:, 1, :], tf[:, 4, :], ALU.subtract))
            link(nc.vector.scalar_tensor_tensor(tf[:, 6, :], tf[:, 4, :], -100.0, tf[:, 0, :], ALU.mult, ALU.add))
            link(nc.vector.scalar_tensor_tensor(tf[:, 7, :], tf[:, 5, :], -100.0, tf[:, 6, :], ALU.mult, ALU.add))
            link(nc.vector.scalar_tensor_tensor(tf[:, 2, :], tf[:, 7, :], 0.01, tf[:, 1, :], ALU.mult, ALU.add))
            link(nc.vector.tensor_scalar(tf[:, 3, :], tf[:, 2, :], 4000.0, None, ALU.mult))
            nc.vector.tensor_copy(ang[:, 0:2 * TILES], toks[:])
            link(nc.vector.tensor_scalar(ang[:, 2 * TILES:], tf[:, 3, :], const[:, C_FREQ:C_FREQ + 1], None, ALU.mult))
            link(nc.vector.tensor_scalar(ang_k[:, 0, :], ang[:], 1.0 / TWO_PI, ROUND, ALU.mult, ALU.add))
            link(nc.vector.tensor_scalar(ang_k[:, 1, :], ang_k[:, 0, :], -ROUND, None, ALU.add))
            link(nc.vector.scalar_tensor_tensor(ang_r[:, 0, :], ang_k[:, 1, :], -PI_A, ang[:], ALU.mult, ALU.add))
            link(nc.vector.scalar_tensor_tensor(ang_r[:, 1, :], ang_k[:, 1, :], -PI_B, ang_r[:, 0, :], ALU.mult, ALU.add))
            link(nc.vector.scalar_tensor_tensor(ang_r[:, 2, :], ang_k[:, 1, :], -PI_C, ang_r[:, 1, :], ALU.mult, ALU.add))
            link(nc.vector.tensor_scalar(ang_r[:, 3, :], ang_r[:, 2, :], -PI_MAX, PI_MAX, ALU.max, ALU.min))
            nc.vector.tensor_scalar(arg[:, 0:2 * TILES], ang_r[:, 3, 0:2 * TILES], 1.0, None, ALU.mult)
            link(nc.vector.scalar_tensor_tensor(ang_r[:, 0, :], ang_r[:, 3, :], -1.0, ang_r[:, 3, :], ALU.mult, ALU.max))
            nc.vector.tensor_scalar(arg[:, 2 * TILES:4 * TILES], ang_r[:, 0, 0:2 * TILES], -1.0, TWO_PI / 4,
                                    ALU.mult, ALU.add)
            link(nc.vector.tensor_scalar(emb_abs[:], ang_r[:, 0, 2 * TILES:], const[:, C_COSM:C_COSM + 1],
                                         const[:, C_COSA:C_COSA + 1], ALU.mult, ALU.add))
            nc.vector.scalar_tensor_tensor(arg[:, 4 * TILES:], ang_r[:, 3, 2 * TILES:], const[:, C_SIN:C_SIN + 1],
                                           emb_abs[:], ALU.mult, ALU.add).then_inc(arg_done, 1)
            link(nc.vector.tensor_copy(idf[:, 0, :], ids[:, 0:TILES]))
            link(nc.vector.tensor_scalar(idf[:, 1, :], idf[:, 0, :], 0.0, float(E - 1), ALU.max, ALU.min))
            nc.vector.tensor_scalar(idx[:], idf[:, 1, :], float(A), const[:, C_OUT:C_OUT + 1],
                                    ALU.mult, ALU.add).then_inc(idx_done, 1)
            link(nc.vector.tensor_tensor(idf[:, 2, :], idf[:, 1, :], idf[:, 0, :], ALU.is_equal))
            link(nc.vector.tensor_scalar(idf[:, 3, :], idf[:, 2, :], -1.0, 1.0, ALU.mult, ALU.add))
            dve.wait_ge(trig_done, 1)
            sines = trig[:, 0:2 * TILES].rearrange("p (w t) -> p t w", w=2)
            cosines = trig[:, 2 * TILES:4 * TILES].rearrange("p (w t o) -> p t w o", w=2, o=1)
            for c in range(CH):
                tiles = slice(c * T, (c + 1) * T)
                nc.vector.tensor_copy(tabs[:, c, T_SIN:T_SIN + 2 * T].rearrange("p (t w) -> p t w", w=2), sines[:, tiles, :])
                nc.vector.tensor_copy(
                    tabs[:, c, T_COS:T_COS + 4 * T].rearrange("p (t w e) -> p t w e", w=2, e=2),
                    cosines[:, tiles, :, :].to_broadcast([P, T, 2, 2]))
            dve.wait_ge(ld_rows, 16)
            fold_bo(blocks[0], odd.S2[0], R_BO0)
            fold_bo(blocks[1], odd.S2[1], R_BO1)
            dve.wait_ge(ada_mm, 1)
            chunks = odd.P1[:, 0:2 * B].rearrange("p (w c n) -> p w c n", w=2, c=CH)
            nc.vector.tensor_scalar(tabs[:, :, T_SCALE:T_SCALE + CB], chunks[:, 0], cols[:, K_ADA:K_ADA + 1], 1.0, ALU.add, ALU.add)
            nc.vector.tensor_scalar(tabs[:, :, T_SHIFT:T_SHIFT + CB], chunks[:, 1], cols[:, K_ADA + 1:K_ADA + 2], None,
                                    ALU.add).then_inc(ada_done, 1)
            dve.wait_ge(gathered, 16 * TILES)
            nc.vector.tensor_tensor(wsel[:, 0, :, :], got[:, :, 0:A], spread(idf[:, 2, :], TILES, A), ALU.mult)
            nc.vector.tensor_tensor(bsel[:], got[:, :, A], idf[:, 2, :], ALU.mult)
            eye = const[:, C_EYE:C_EYE + A].rearrange("p (o a) -> p o a", o=1).to_broadcast([P, TILES, A])
            link(nc.vector.tensor_tensor(wsel[:, 1, :, :], eye, spread(idf[:, 3, :], TILES, A), ALU.mult))
            nc.vector.tensor_tensor(tabs[:, :, T_BIAS:T_BIAS + T], bsel[:].rearrange("p (c t) -> p c t", c=CH),
                                    got[:, :, A + 1].rearrange("p (c t) -> p c t", c=CH), ALU.add)
            link(nc.vector.tensor_tensor(wsel[:, 0, :, :], wsel[:, 0, :, :], wsel[:, 1, :, :], ALU.add))
            for c in range(CH):
                last = nc.vector.transpose(tabs[:, c, T_W:], wsel[:, 0, c * T:(c + 1) * T, :].rearrange("p t a -> p (t a)"))
            last.then_inc(tables_done, 1)
            dve.wait_ge(tables_done, 1)
            run(joint, dve.Fori, even, odd)

        @block.gpsimd
        def _(pool):
            def norm_rstd(s, k):
                pool.wait_ge(s.mv_done, k + 1)
                nc.gpsimd.tensor_tensor(s.ve[:], s.mv[:, :, 1], eps[:], ALU.add).then_inc(s.ve_done, 1)
                pool.wait_ge(s.ve_done, k + 1)
                nc.gpsimd.tensor_tensor(s.rstd[:], s.ve[:], mhalf[:], ALU.pow).then_inc(s.rstd_done, 1)

            def probabilities(s, c, l, t):
                n = (2 * c + l) * T + t
                k = t % 2
                pool.wait_ge(s.rc_done, n + 1)
                wait(pool, s.pt_done, two_ago(n, t))
                nc.gpsimd.tensor_tensor(groups(s.Pn[:, k, :]), groups(s.Ex[:, k, :]), spread(s.rc[:, k, :], R * R, S),
                                        ALU.mult).then_inc(s.pn_done, 1)

            def subtract_max(s, c, l, t):
                if l == 0:
                    return
                k = t % 2
                pool.wait_ge(s.mx_done, (2 * c + 1) * T + t + 1)
                nc.gpsimd.tensor_tensor(groups(s.Dm[:, k, :]), groups(s.Dm[:, k, :]), spread(s.mx[:, k, :], R * R, S),
                                        ALU.subtract).then_inc(s.sub_done, 1)

            def residual(s, c, l):
                if l == 0:
                    pool.wait_ge(s.ld_x, 16 * (c + 1))
                    wait(pool, s.x1_done, 2 * c)
                    nc.gpsimd.tensor_tensor(s.xb[:], s.x, over_tiles(blocks[0].bo[:]), ALU.add).then_inc(s.xb_done, 1)

            def add_shift(s, c, l):
                if l == 1:
                    pool.wait_ge(s.tab_done, c + 1)
                    pool.wait_ge(s.xm_done, c + 1)
                    nc.gpsimd.tensor_tensor(groups(s.hT[:]), groups(s.xm[:]),
                                            spread(s.tab[:, T_SHIFT:T_SHIFT + CB], CB, S), ALU.add).then_inc(s.hT_done, 1)

            def rest(s, c, l):
                pool.wait_ge(s.x1_done, 2 * c + l + 1)
                wait(pool, s.xo_done, 2 * c + l)
                if l == 1:
                    nc.gpsimd.tensor_tensor(s.rest[:], s.x1[:], over_tiles(rows[:, R_B21:R_B21 + D]),
                                            ALU.add).then_inc(s.rest1_done, 1)
                    return
                nc.gpsimd.tensor_tensor(s.rest[:], s.x1[:], over_tiles(rows[:, R_B20:R_B20 + D]),
                                        ALU.add).then_inc(s.rest0_done, 1)
                pool.wait_ge(s.rest0_done, 4 * c + 1)
                nc.gpsimd.tensor_tensor(s.rest[:], s.rest[:], s.x, ALU.subtract).then_inc(s.rest0_done, 1)
                pool.wait_ge(s.rest0_done, 4 * c + 2)
                nc.gpsimd.tensor_tensor(s.rest[:], s.rest[:], spread(s.gate, T, D), ALU.mult).then_inc(s.rest0_done, 1)
                pool.wait_ge(s.rest0_done, 4 * c + 3)
                nc.gpsimd.tensor_tensor(s.rest[:], s.rest[:], s.x, ALU.add).then_inc(s.rest0_done, 1)

            def rotate(s, c):
                pool.wait_ge(s.xo_done, 2 * c + 2)
                v = s.xo[:].rearrange("p t (q w e) -> p t q w e", w=2, e=2)
                s2 = s.tab[:, T_SIN:T_SIN + 2 * T].rearrange("p (t o w) -> p t o w", o=1, w=2).to_broadcast([P, T, D // 4, 2])
                for e in range(2):
                    o = s.rs4[:, e, :].rearrange("p (t q w) -> p t q w", t=T, w=2)
                    nc.gpsimd.tensor_tensor(o, v[:, :, :, :, 1 - e], s2, ALU.mult).then_inc(s.rs4_done, 1)

            def residual_y(s, c):
                pool.wait_ge(s.rot_done, c + 1)
                wait(pool, s.z_done, c)
                nc.gpsimd.tensor_tensor(s.yb[:], s.y[:], over_tiles(rows[:, R_UP:R_UP + D]), ALU.add).then_inc(s.yb_done, 1)

            def expert_blocks(s, c):
                wait(pool, s.ex_mm, c)
                w = s.tab[:, T_W:T_W + T * A].rearrange("p (t o a) -> p t o a", o=1, a=A).to_broadcast([P, T, R, A])
                m = block_mask.rearrange("p (o j a) -> p o j a", o=1, a=A).to_broadcast([P, T, R, A])
                nc.gpsimd.tensor_tensor(s.wblk[:].rearrange("p t (j a) -> p t j a", a=A), w, m,
                                        ALU.mult).then_inc(s.wblk_done, 1)

            def norm3_out(s, c):
                norm_rstd(s, 5 * c + 4)
                pool.wait_ge(s.xh_done, 5 * c + 5)
                nc.gpsimd.tensor_tensor(s.og[:], s.xh[:], over_tiles(rows[:, R_LNG:R_LNG + D]), ALU.mult).then_inc(s.og_done, 1)
                pool.wait_ge(s.og_done, c + 1)
                wait(pool, s.stored, 16 * c)
                nc.gpsimd.tensor_tensor(s.ob[:], s.og[:], over_tiles(rows[:, R_LNB:R_LNB + D]), ALU.add).then_inc(s.ob_done, 1)

            def joint(att, hid):
                if att:
                    norm_rstd(att[0], 5 * att[1] + 2 * att[2])
                if hid:
                    norm_rstd(hid[0], 5 * hid[1] + 2 * hid[2] + 1)
                if att:
                    add_shift(*att)
                if hid:
                    rest(*hid)
                if att:
                    residual(*att)
                l3 = hid and hid[2] == 1
                if l3:
                    expert_blocks(*hid[:2])
                for t in range(T + 1):
                    if att and t < T:
                        subtract_max(*att, t)
                    if att and t >= 1:
                        probabilities(*att, t - 1)
                    if l3 and t == 1:
                        rotate(*hid[:2])
                    if l3 and t == 3:
                        residual_y(*hid[:2])
                if l3:
                    norm3_out(*hid[:2])

            nc.gpsimd.memset(eps[:], EPS)
            nc.gpsimd.memset(mhalf[:], -0.5).then_inc(mhalf_done, 1)
            for s in (even, odd):
                nc.gpsimd.memset(s.Km[:], 0.0)
                nc.gpsimd.memset(s.Vm[:], 0.0).then_inc(s.zeroed, 1)
            pool.wait_ge(idx_done, 1)
            for t in range(TILES):
                nc.gpsimd.indirect_dma_start(got[:, t, :], None, etab_in,
                                             bass.IndirectOffsetOnAxis(ap=idx[:, t:t + 1], axis=0)).then_inc(gathered, 16)
            pool.wait_ge(ld_mask, 16)
            nc.gpsimd.tensor_scalar(maskb[:].rearrange("p n k -> p (n k)"), mask4[:].bitcast(U8), NEG, None,
                                    ALU.mult).then_inc(maskb_done, 1)
            pool.wait_ge(mhalf_done, 1)
            pool.wait_ge(ld_rows, 16)
            run(joint, pool.Fori, even, odd)


def constants():
    c = np.zeros((P, N_CONST), np.float32)
    p = np.arange(P)
    c[:, C_IDENT:C_IDENT + P] = np.eye(P)
    c[:, C_BLOCK:C_BLOCK + P] = p[:, None] // S == p[None, :] // S
    c[:, C_CAUSAL:C_CAUSAL + S] = np.where(np.arange(S)[None, :] > (p % S)[:, None], NEG, 0.0)
    c[:, C_EYE:C_EYE + A] = (p % A)[:, None] == np.arange(A)[None, :]
    c[:, C_HEAD:C_HEAD + R] = ((p // DH % R)[:, None] == np.arange(R)[None, :]) / np.sqrt(DH)
    half = D // 2
    freq = np.exp(np.arange(half, dtype=np.float32) * np.float32(-np.log(10000.0) / (half - 1)))
    c[:, C_FREQ] = np.concatenate([freq, freq])
    c[:, C_OUT] = p % A
    c[:, C_SIN] = p < half
    c[:, C_COSM] = -(p >= half).astype(np.float32)
    c[:, C_COSA] = (p >= half) * (np.pi / 2)
    return c


def kernel(**inputs):
    import concourse.bacc as bacc
    from concourse.bass_utils import run_bass_kernel_spmd

    v = {k: np.asarray(a) for k, a in inputs.items()}

    def block_weights(n):
        w2 = v[n + "W2"].reshape(FC, P, D).transpose(1, 0, 2).reshape(P, FC * D)
        return np.concatenate([v[n + "Wq"], v[n + "Wk"], v[n + "Wv"], v[n + "Wo"], v[n + "W1"], w2], axis=1)

    def block_columns(n, g, be):
        return [v[n + "bq"], v[n + "bk"], v[n + "bv"], v[n + g], v[n + be], *v[n + "b1"].reshape(FC, P)]

    def beside(rows):
        return np.broadcast_to(np.concatenate(rows)[None, :], (P, sum(len(r) for r in rows)))

    def of_token(a):
        return np.repeat(a.reshape(TILES, R), S, axis=1).T

    arrays = {
        "x_in": np.concatenate([v["x"].reshape(CH, T, P, D).transpose(2, 0, 1, 3).reshape(P, CH, CT),
                                of_token(v["condB_gatescore"]).reshape(P, CH, T)], axis=2).reshape(P, CH * (CT + T)),
        "bias_in": v["fside_Bx16xSxS_0"].reshape(B, R, R, S, S).transpose(2, 3, 0, 1, 4).reshape(P, B * R * S),
        "mask_in": np.tile(v["mask_Bx1xSxS_bk0"].reshape(B, S, S).transpose(1, 0, 2).reshape(S, B * S),
                           (R, 1)).view(np.int32),
        "w0_in": block_weights("L0_cond_"),
        "w1_in": block_weights("L1_cond_"),
        "wx_in": np.concatenate([v["L1_cond_W_ada"], np.tile(v["L3_cond_down_W"].T, (1, R)),
                                 np.tile(v["L3_cond_up_W"].T, (R, 1))], axis=1),
        "rows_in": beside([v["L0_cond_bo"], v["L0_cond_b2"], v["L1_cond_bo"], v["L1_cond_b2"],
                           v["L3_cond_up_b"], v["L3_cond_ln_gamma"], v["L3_cond_ln_beta"]]),
        "cols_in": np.stack(block_columns("L0_cond_", "gamma2", "beta2") + block_columns("L1_cond_", "g2", "beta2")
                            + [v["L0_cond_gamma1"], v["L0_cond_beta1"], *v["L1_cond_b_ada"].reshape(2, D),
                               np.tile(v["L3_cond_down_b"], R)], axis=1),
        "toks_in": np.concatenate([of_token(v["condB_theta"]), of_token(v["condB_phi"])], axis=1),
        "ids_in": np.concatenate([of_token(v["itok_B_0_15"]),
                                  np.broadcast_to(v["itok_B_34_63"][None, :], (P, B))], axis=1),
        "etab_in": np.concatenate([v["L3_cond_expert_W"].reshape(E * A, A), v["L3_cond_expert_b"].reshape(E * A, 1),
                                   v["L3_cond_domain_emb"].reshape(E * A, 1)], axis=1),
        "const_in": constants(),
    }
    arrays = {k: np.ascontiguousarray(a) for k, a in arrays.items()}
    nc = bacc.Bacc("TRN2", target_bir_lowering=False, num_devices=1)
    args = [nc.dram_tensor(k, a.shape, mybir.dt.from_np(a.dtype), kind="ExternalInput").ap()
            for k, a in arrays.items()]
    out = nc.dram_tensor("out", (P, TILES * D), F32, kind="ExternalOutput").ap()
    cond_seq_kernel(nc, *args, out)
    r = run_bass_kernel_spmd(nc, [arrays], core_ids=[0])
    got = r.results[0]["out"].reshape(P, TILES, D).transpose(1, 0, 2).reshape(B, S, D)
    return np.ascontiguousarray(got)
```

```python
from contextlib import ExitStack

import numpy as np

import concourse.bass as bass
from concourse import mybir

F32 = mybir.dt.float32
BF16 = mybir.dt.bfloat16
I32 = mybir.dt.int32
U32 = mybir.dt.uint32
U8 = mybir.dt.uint8
ALU = mybir.AluOpType
ACT = mybir.ActivationFunctionType
AX = mybir.AxisListType.X

B, S, D = 64, 32, 128
H, DH = 16, 8
DFF = 512
E, A = 16, 32
P = 128
R = 4
TILES = B * S // P
T = 4
CH = TILES // T
CB = T * R
CT = T * P
NC = CH // 2
TW = R * P
FC = DFF // P
EPS = 1e-5
NEG = -1e30
TWO_PI = 6.283185307179586
PI_A = 6.28125
PI_B = 0.0019350051879882812
PI_C = TWO_PI - PI_A - PI_B
ROUND = 12582912.0
PI_MAX = 3.1415925

T_SCALE, T_SHIFT, T_COS, T_SIN = 0, CB, 2 * CB, 2 * CB + 4 * T
N_TAB = T_SIN + 2 * T
E_BIAS, E_W = 0, T
N_ETAB = T + T * A

C_IDENT, C_BLOCK, C_CAUSAL, C_EYE, C_HEAD, C_FREQ, C_OUT, C_SIN, C_COSM, C_COSA = (
    0, 128, 256, 288, 320, 324, 325, 326, 327, 328)
N_CONST = 329
W_Q, W_K, W_V, W_O, W_1, W_2 = 0, 128, 256, 384, 512, 1024
R_BO0, R_B20, R_BO1, R_B21, R_UP, R_LNG, R_LNB = (128 * n for n in range(7))
K_BQ, K_BK, K_BV, K_G2, K_BETA2, K_B1 = 0, 1, 2, 3, 4, 5
K_STREAM = 9
K_G1, K_BETA1, K_ADA, K_DOWN = 18, 19, 20, 22
N_COLS = 23


class Norm:

    def __init__(self, sb, sem, name):
        self.stats = sb(name + "_stats", [P, T, 6], F32)
        self.mv = sb(name + "_mv", [P, T, 2], F32)
        self.ve = sb(name + "_ve", [P, T], F32)
        self.rstd = sb(name + "_rstd", [P, T], F32)
        self.mv_done = sem(name + "_mv_done")
        self.ve_done = sem(name + "_ve_done")
        self.rstd_done = sem(name + "_rstd_done")
        self.xh_done = sem(name + "_xh_done")


class Stream:

    def __init__(self, sb, ps, sem, name, number):
        self.number = number
        self.norm = Norm(sb, sem, name + "_norm")
        self.norm3 = Norm(sb, sem, name + "_norm3")
        self.nm = sb(name + "_nm", [P, T], F32)
        self.shift = sb(name + "_shift", [P, T], F32)
        self.nm_done = sem(name + "_nm_done")
        self.shift_done = sem(name + "_shift_done")
        self.xh = sb(name + "_xh", [P, T, D], F32)
        self.xg = sb(name + "_xg", [P, CT + T], F32)
        self.x = self.xg[:, 0:CT].rearrange("p (t d) -> p t d", d=D)
        self.gate = self.xg[:, CT:]
        self.gate_kept = sb(name + "_gate_kept", [P, T], F32)
        self.xb = sb(name + "_xb", [P, T, D], F32)
        self.hT = sb(name + "_hT", [P, CT], F32)
        self.Qm = sb(name + "_Qm", [P, CB, R, S], F32)
        self.Km = sb(name + "_Km", [P, CB, R, S], F32)
        self.Vm = sb(name + "_Vm", [P, CB, D], F32)
        self.mx = sb(name + "_mx", [P, T, 16], F32)
        self.sm = sb(name + "_sm", [P, T, 16], F32)
        self.rc = sb(name + "_rc", [P, T, 16], F32)
        self.Ex = sb(name + "_Ex", [P, T, TW], F32)
        self.PT = sb(name + "_PT", [P, 2, TW], F32)
        self.ctxT = sb(name + "_ctxT", [P, CT], F32)
        self.x1 = sb(name + "_x1", [P, T, D], F32)
        self.rest = sb(name + "_rest", [P, T, D], F32)
        self.fT = sb(name + "_fT", [P, FC, CT], F32)
        self.xo = sb(name + "_xo", [P, T, D], F32)
        self.tab = sb(name + "_tab", [P, N_TAB], F32)
        self.etab = sb(name + "_etab", [P, N_ETAB], F32)
        self.xm = sb(name + "_xm", [P, CT], F32)
        self.yT = self.xm
        self.rc4 = sb(name + "_rc4", [P, T, D], F32)
        self.rs4 = sb(name + "_rs4", [P, 2, CT // 2], F32)
        self.y = self.x1
        self.yb = sb(name + "_yb", [P, T, D], F32)
        self.wblk = sb(name + "_wblk", [P, T, P], F32)
        self.hid = sb(name + "_hid", [P, CT], F32)
        self.em = sb(name + "_em", [P, T, P], F32)
        self.z = sb(name + "_z", [P, T, D], F32)
        self.og = self.yb
        self.ob = self.rs4[:].rearrange("p e n -> p (e n)").rearrange("p (t d) -> p t d", d=D)
        self.P0 = ps(name + "_P0", [P, 512], F32)[:, 0:CT]
        self.P1 = ps(name + "_P1", [P, 512], F32)[:, 0:CT]
        self.S2 = [ps(name + f"_S{n}", [P, 512], F32) for n in range(2)]

        self.ld_x = sem(name + "_ld_x")
        self.zeroed = sem(name + "_zeroed")
        self.gate_done = sem(name + "_gate_done")
        self.turned = sem(name + "_turned")
        self.xb_done = sem(name + "_xb_done")
        self.tab_done = sem(name + "_tab_done")
        self.etab_done = sem(name + "_etab_done")
        self.xm_done = sem(name + "_xm_done")
        self.hT_done = sem(name + "_hT_done")
        self.q_mm = sem(name + "_q_mm")
        self.k_mm = sem(name + "_k_mm")
        self.v_mm = sem(name + "_v_mm")
        self.qm_done = sem(name + "_qm_done")
        self.kv_act = sem(name + "_kv_act")
        self.v_dve = sem(name + "_v_dve")
        self.sc_mm = sem(name + "_sc_mm")
        self.s_free = sem(name + "_s_free")
        self.mx_done = sem(name + "_mx_done")
        self.sub_pool = sem(name + "_sub_pool")
        self.sub_dve = sem(name + "_sub_dve")
        self.ex_done = sem(name + "_ex_done")
        self.pt_done = sem(name + "_pt_done")
        self.pv_mm = sem(name + "_pv_mm")
        self.sm_done = sem(name + "_sm_done")
        self.rc_done = sem(name + "_rc_done")
        self.pn_done = sem(name + "_pn_done")
        self.ctx_done = sem(name + "_ctx_done")
        self.o_mm = sem(name + "_o_mm")
        self.x1_done = sem(name + "_x1_done")
        self.rest0_done = sem(name + "_rest0_done")
        self.rest1_done = sem(name + "_rest1_done")
        self.h2T_done = sem(name + "_h2T_done")
        self.f_mm = sem(name + "_f_mm")
        self.f_done = sem(name + "_f_done")
        self.y_mm = sem(name + "_y_mm")
        self.xo_done = sem(name + "_xo_done")
        self.rc4_done = sem(name + "_rc4_done")
        self.rs4_done = sem(name + "_rs4_done")
        self.rot_done = sem(name + "_rot_done")
        self.yb_done = sem(name + "_yb_done")
        self.y_turned = sem(name + "_y_turned")
        self.yT_done = sem(name + "_yT_done")
        self.down_mm = sem(name + "_down_mm")
        self.hid_done = sem(name + "_hid_done")
        self.wblk_done = sem(name + "_wblk_done")
        self.ex_mm = sem(name + "_ex_mm")
        self.em_done = sem(name + "_em_done")
        self.up_mm = sem(name + "_up_mm")
        self.z_done = sem(name + "_z_done")
        self.og_done = sem(name + "_og_done")
        self.ob_done = sem(name + "_ob_done")
        self.stored = sem(name + "_stored")


class Block:

    def __init__(self, sb, sem, name, col):
        self.col = col
        self.w = sb(name + "_w", [P, 4 * D + 2 * DFF], F32)
        self.bqm = sb(name + "_bqm", [P, R], F32)
        self.bvb = sb(name + "_bvb", [P, D], F32)
        self.bo = sb(name + "_bo", [P, D], F32)
        self.loaded = sem(name + "_loaded")
        self.bqm_done = sem(name + "_bqm_done")
        self.bo_mm = sem(name + "_bo_mm")
        self.bo_done = sem(name + "_bo_done")


def wait(eng, sem, value):
    if isinstance(value, int) and value <= 0:
        return
    eng.wait_ge(sem, value)


def two_ago(n, t):
    return n if t == 0 else n - 1


def run(joint, Fori, even, odd):
    joint(None, None, (even, 0, 0), None, 0)
    joint((even, 0, 0), None, (odd, 0, 0), None, 1)
    joint((odd, 0, 0), (even, 0, 0), (even, 0, 1), None, 2)
    joint((even, 0, 1), (odd, 0, 0), (odd, 0, 1), None, 3)
    with Fori(1, NC) as c:
        joint((odd, c - 1, 1), (even, c - 1, 1), (even, c, 0), None, None)
        joint((even, c, 0), (odd, c - 1, 1), (odd, c, 0), (even, c - 1), None)
        joint((odd, c, 0), (even, c, 0), (even, c, 1), (odd, c - 1), None)
        joint((even, c, 1), (odd, c, 0), (odd, c, 1), None, None)
    joint((odd, NC - 1, 1), (even, NC - 1, 1), None, None, None)
    joint(None, (odd, NC - 1, 1), None, (even, NC - 1), None)
    joint(None, None, None, (odd, NC - 1), None)


def cond_seq_kernel(nc, x_in, bias_in, mask_in, w0_in, w1_in, wx_in, rows_in, cols_in, toks_in,
                    ids_in, etab_in, const_in, out):
    with ExitStack() as ctx:
        def sb(name, shape, dt):
            return ctx.enter_context(nc.sbuf_tensor(name, shape, dt))

        def ps(name, shape, dt):
            return ctx.enter_context(nc.psum_tensor(name, shape, dt))

        def sem(name):
            return ctx.enter_context(nc.semaphore(name))

        even = Stream(sb, ps, sem, "even", 0)
        odd = Stream(sb, ps, sem, "odd", 1)
        blocks = (Block(sb, sem, "l0", 0), Block(sb, sem, "l1", K_STREAM))

        const = sb("const", [P, N_CONST], F32)
        cols = sb("cols", [P, N_COLS], F32)
        rows = sb("rows", [P, 7 * D], F32)
        wx = sb("wx", [P, 4 * D], F32)
        toks = sb("toks", [P, 2 * TILES], F32)
        ids = sb("ids", [P, TILES + B], I32)
        bias = sb("bias", [P, T, TW], F32)
        mask4 = sb("mask4", [P, B * S // 4], I32)
        maskb = sb("maskb", [P, B, S], BF16)
        identb = sb("identb", [P, P], BF16)
        causalb = sb("causalb", [P, S], BF16)
        mhalf = sb("mhalf", [P, T], F32)
        eps = sb("eps", [P, T], F32)
        zero = sb("zero", [P, T], F32)
        ident = const[:, C_IDENT:C_IDENT + P]
        block_mask = const[:, C_BLOCK:C_BLOCK + P]
        head_mask = const[:, C_HEAD:C_HEAD + R]
        NA = 2 * TILES + B
        ang = sb("ang", [P, NA], F32)
        ang_k = sb("ang_k", [P, 2, NA], F32)
        ang_r = sb("ang_r", [P, 4, NA], F32)
        arg = sb("arg", [P, 2 * 2 * TILES + B], F32)
        trig = sb("trig", [P, 2 * 2 * TILES + B], F32)
        tf = sb("tf", [P, 8, B], F32)
        emb_abs = sb("emb_abs", [P, B], F32)
        emb = sb("emb", [P, B], F32)
        tabs = sb("tabs", [P, CH, N_TAB], F32)
        etabs = sb("etabs", [P, CH, N_ETAB], F32)
        idf = sb("idf", [P, 4, TILES], F32)
        idx = sb("idx", [P, TILES], U32)
        got = sb("got", [P, TILES, A + 2], F32)
        wsel = sb("wsel", [P, 2, TILES, A], F32)
        bsel = sb("bsel", [P, TILES], F32)

        ld_const = sem("ld_const")
        ld_ids = sem("ld_ids")
        ld_rows = sem("ld_rows")
        ld_toks = sem("ld_toks")
        ld_wx = sem("ld_wx")
        ld_mask = sem("ld_mask")
        ld_bias = [sem(f"ld_bias{t}") for t in range(T)]
        consts_b = sem("consts_b")
        maskb_done = sem("maskb_done")
        mhalf_done = sem("mhalf_done")
        chain = sem("chain")
        arg_done = sem("arg_done")
        trig_done = sem("trig_done")
        emb_done = sem("emb_done")
        ada_mm = sem("ada_mm")
        ada_done = sem("ada_done")
        tables_done = sem("tables_done")
        idx_done = sem("idx_done")
        idf_done = sem("idf_done")
        gathered = sem("gathered")
        wsel_done = sem("wsel_done")
        selected = sem("selected")

        def over_tiles(row):
            return row.rearrange("p (o d) -> p o d", o=1).to_broadcast([P, T, D])

        def spread(col, n, k):
            return col.rearrange("p (n o) -> p n o", o=1).to_broadcast([P, n, k])

        def groups(ap):
            return ap.rearrange("p (n k) -> p n k", k=S)

        def tiled(ap):
            return ap.rearrange("p (t d) -> p t d", d=D)

        def pairs(buf):
            v = buf[:].rearrange("p t (q e) -> p (t q) e", e=2)
            return v[:, :, 0], v[:, :, 1]

        block = ctx.enter_context(nc.Block())

        @block.sync
        def _(sp):
            def load_x(s, c):
                wait(sp, s.rest0_done, 4 * c)
                wait(sp, s.gate_done, c)
                sp.dma_start(s.xg[:], x_in[:, bass.ds((2 * c + s.number) * (CT + T), CT + T)]).then_inc(s.ld_x, 16)

            def load_bias(s, c, first=False):
                for t in range(T):
                    if s is odd:
                        sp.wait_ge(even.s_free, (2 * c + 1) * T + t + 1)
                    elif not first:
                        sp.wait_ge(odd.s_free, (2 * c - 1) * T + t + 1)
                    at = ((2 * c + s.number) * T + t) * TW
                    sp.dma_start(bias[:, t, :], bias_in[:, bass.ds(at, TW)]).then_inc(ld_bias[t], 16)

            def store(s, c):
                sp.wait_ge(s.ob_done, c + 1)
                sp.dma_start(out[:, bass.ds((2 * c + s.number) * CT, CT)],
                             s.ob.rearrange("p t d -> p (t d)")).then_inc(s.stored, 16)

            load_x(even, 0)
            sp.dma_start(const[:], const_in).then_inc(ld_const, 16)
            sp.dma_start(blocks[0].w[:], w0_in).then_inc(blocks[0].loaded, 16)
            sp.dma_start(rows[:], rows_in).then_inc(ld_rows, 16)
            load_x(odd, 0)
            sp.dma_start(mask4[:], mask_in).then_inc(ld_mask, 16)
            sp.dma_start(blocks[1].w[:], w1_in).then_inc(blocks[1].loaded, 16)
            load_bias(even, 0, first=True)
            load_bias(odd, 0)
            with sp.Fori(1, NC) as c:
                load_x(even, c)
                load_x(odd, c)
                load_bias(even, c)
                store(even, c - 1)
                store(odd, c - 1)
                load_bias(odd, c)
            store(even, NC - 1)
            store(odd, NC - 1)
            sp.wait_ge(even.stored, 16 * NC)
            sp.wait_ge(odd.stored, 16 * NC)

        @block.tensor
        def _(pe):
            def turn(src, bank, done):
                for t in range(T):
                    last = pe.transpose(bank[:, t * P:(t + 1) * P], src[:, t, :], ident)
                last.then_inc(done, 1)

            def turn1(s, c, l):
                pe.wait_ge(s.norm.xh_done, 4 * c + 2 * l + 1)
                turn(s.xh, s.P0, s.turned)

            def project_queries(s, c, l):
                p = 2 * c + l
                wait(pe, s.f_done, p * FC)
                pe.wait_ge(s.hT_done, p + 1)
                pe.matmul(s.S2[0][:, 0:CT], blocks[l].w[:, W_Q:W_Q + D], s.hT[:], start=True, stop=True).then_inc(s.q_mm, 1)

            def project_keys(s, c, l):
                pe.matmul(s.S2[1][:, 0:CT], blocks[l].w[:, W_K:W_K + D], s.hT[:], start=True, stop=True).then_inc(s.k_mm, 1)

            def project_values(s, c, l):
                pe.wait_ge(s.qm_done, 2 * c + l + 1)
                for t in range(T):
                    last = pe.matmul(s.S2[0][:, t * P:(t + 1) * P], s.hT[:, t * P:(t + 1) * P],
                                     blocks[l].w[:, W_V:W_V + D], start=True, stop=True)
                last.then_inc(s.v_mm, 1)

            def scores(s, c, l, t):
                p = 2 * c + l
                if t == 0:
                    pe.wait_ge(s.kv_act, 2 * p + 1)
                if t == 1:
                    pe.wait_ge(s.kv_act, 2 * p + 2)
                    pe.wait_ge(s.v_dve, p + 1)
                if t >= 2:
                    pe.wait_ge(s.s_free, p * T + t - 1)
                bank = s.S2[(t + 1) % 2]
                if l == 0:
                    masks = causalb[:].rearrange("p (o k) -> p o k", o=1).to_broadcast([P, R * R, S])
                else:
                    masks = maskb[:, bass.ds((2 * c + s.number) * CB + t * R, R), :].rearrange(
                        "p (n o) k -> p n o k", o=1).to_broadcast([P, R, R, S])
                pe.matmul(bank[:], identb[:], masks, start=True, stop=False)
                for j in range(R):
                    n = t * R + j
                    last = pe.matmul(bank[:, j * P:(j + 1) * P], s.Qm[:, n, :, :], s.Km[:, n, :, :],
                                     start=False, stop=(j == R - 1))
                last.then_inc(s.sc_mm, 1)

            def values(s, c, l, t):
                p = 2 * c + l
                pe.wait_ge(s.pt_done, p * T + t + 1)
                for j in range(R):
                    n = t * R + j
                    for g in range(R):
                        last = pe.matmul(s.P0[32 * g:32 * g + 32, n * S:(n + 1) * S],
                                         s.Vm[:, n, 32 * g:32 * g + 32],
                                         s.PT[:, t % 2, (j * R + g) * S:(j * R + g + 1) * S],
                                         start=True, stop=True, tile_position=(0, 32 * g))
                last.then_inc(s.pv_mm, 1)

            def residual_in(s, c, l):
                pe.wait_ge(s.xo_done, 2 * c + 1)
                for t in range(T):
                    tile = slice(t * P, (t + 1) * P)
                    pe.matmul(s.P1[:, tile], s.hT[:, tile], ident, start=(t == 0), stop=False)

            def attention_out(s, c, l):
                pe.wait_ge(s.ctx_done, 2 * c + l + 1)
                if l == 0:
                    wait(pe, s.z_done, c)
                for t in range(T):
                    tile = slice(t * P, (t + 1) * P)
                    last = pe.matmul(s.P1[:, tile], s.ctxT[:, tile], blocks[l].w[:, W_O:W_O + D],
                                     start=(l == 0), stop=(l == 0 or t == T - 1))
                last.then_inc(s.o_mm, 1)

            def turn2(s, c, l):
                pe.wait_ge(s.norm.xh_done, 4 * c + 2 * l + 2)
                turn(s.xh, s.P0, s.turned)

            def hidden(s, c, l, k):
                p = 2 * c + l
                if k == 0:
                    pe.wait_ge(s.h2T_done, p + 1)
                if k >= 2:
                    pe.wait_ge(s.f_done, p * FC + k - 1)
                pe.matmul(s.S2[k % 2][:, 0:CT], blocks[l].w[:, W_1 + k * P:W_1 + (k + 1) * P], s.hT[:],
                          start=True, stop=True).then_inc(s.f_mm, 1)

            def hidden_out(s, c, l):
                p = 2 * c + l
                pe.wait_ge(s.f_done, (p + 1) * FC)
                pe.wait_ge(s.x1_done, p + 1)
                for t in range(T):
                    for k in range(FC):
                        last = pe.matmul(s.P1[:, t * P:(t + 1) * P], s.fT[:, k, t * P:(t + 1) * P],
                                         blocks[l].w[:, W_2 + k * D:W_2 + (k + 1) * D],
                                         start=(k == 0), stop=(k == FC - 1))
                last.then_inc(s.y_mm, 1)

            def adapter_turn(s, c, head):
                if head:
                    pe.wait_ge(s.hT_done, 2 * c + 3)
                pe.wait_ge(s.rot_done, c + 1)
                turn(s.y, s.P0, s.y_turned)

            def adapter_down(s, c):
                pe.wait_ge(s.yT_done, c + 1)
                pe.matmul(s.P1, wx[:, 2 * D:3 * D], s.yT[:], start=True, stop=True).then_inc(s.down_mm, 1)

            def adapter_expert(s, c):
                pe.wait_ge(s.hid_done, c + 1)
                pe.wait_ge(s.wblk_done, c + 1)
                for t in range(T):
                    last = pe.matmul(s.P0[:, t * P:(t + 1) * P], s.wblk[:, t, :], s.hid[:, t * P:(t + 1) * P],
                                     start=True, stop=True)
                last.then_inc(s.ex_mm, 1)

            def adapter_up(s, c):
                pe.wait_ge(s.em_done, c + 1)
                for t in range(T):
                    last = pe.matmul(s.P1[:, t * P:(t + 1) * P], s.em[:, t, :], wx[:, 3 * D:4 * D],
                                     start=True, stop=True)
                last.then_inc(s.up_mm, 1)

            def fold_bv(b, bank):
                pe.wait_ge(b.loaded, 16)
                pe.wait_ge(b.bqm_done, 2)
                pe.matmul(bank[:, 0:D], b.bvb[:], b.w[:, W_O:W_O + D], start=True, stop=True).then_inc(b.bo_mm, 1)

            def modulation():
                pe.wait_ge(ld_wx, 16)
                pe.wait_ge(emb_done, 1)
                ada = odd.P1[:, 0:2 * B]
                pe.matmul(ada[:, 0:B], wx[:, 0:D], emb[:], start=True, stop=True)
                pe.matmul(ada[:, B:2 * B], wx[:, D:2 * D], emb[:], start=True, stop=True).then_inc(ada_mm, 1)

            def joint(first, second, head, late, setup):
                early = head and head[2] == 0
                after = head and head[2] == 1
                l3 = second and second[2] == 1
                if second:
                    hidden(*second, 0)
                    hidden(*second, 1)
                if first:
                    scores(*first, 1)
                if second:
                    hidden(*second, 2)
                    hidden(*second, 3)
                if first:
                    scores(*first, 2)
                    if first[2] == 1:
                        residual_in(*first)
                if late:
                    adapter_expert(*late)
                if early:
                    if first:
                        scores(*first, 3)
                    turn1(*head)
                    if setup == 1:
                        fold_bv(blocks[1], odd.S2[1])
                        pe.wait_ge(blocks[0].bo_done, 1)
                        pe.wait_ge(blocks[1].bo_done, 1)
                    project_queries(*head)
                    project_keys(*head)
                if first and not early:
                    scores(*first, 3)
                if second:
                    hidden_out(*second)
                if early and second:
                    project_values(*head)
                if late:
                    adapter_up(*late)
                if after:
                    turn1(*head)
                if first:
                    for t in range(T):
                        values(*first, t)
                if after:
                    project_queries(*head)
                if first:
                    attention_out(*first)
                if after:
                    project_keys(*head)
                if l3:
                    adapter_turn(*second[:2], head)
                    adapter_down(*second[:2])
                if head and not (second and early):
                    project_values(*head)
                if setup == 1:
                    modulation()
                if head:
                    scores(*head, 0)
                if first:
                    turn2(*first)
                if setup == 1:
                    pe.wait_ge(ada_done, 1)

            pe.wait_ge(ld_const, 32)
            pe.wait_ge(consts_b, 1)
            fold_bv(blocks[0], odd.S2[0])
            run(joint, pe.Fori, even, odd)

        @block.scalar
        def _(act):
            act.dma_start(cols[:], cols_in).then_inc(ld_const, 16)
            act.dma_start(ids[:], ids_in).then_inc(ld_ids, 16)
            act.dma_start(toks[:], toks_in).then_inc(ld_toks, 16)
            act.dma_start(wx[:], wx_in).then_inc(ld_wx, 16)

            def apply3(s, c):
                norm = s.norm3
                act.wait_ge(s.shift_done, c + 1)
                for t in range(T):
                    last = nc.scalar.activation(s.z[:, t, :], s.z[:, t, :], ACT.Identity,
                                                bias=s.shift[:, t:t + 1], scale=norm.rstd[:, t:t + 1])
                last.then_inc(norm.xh_done, 1)


            def norm_out(s, c, l):
                act.wait_ge(s.turned, 4 * c + 1)
                nc.scalar.activation(s.hT[:], s.P0, ACT.Identity, bias=cols[:, K_BETA1:K_BETA1 + 1],
                                     scale=cols[:, K_G1:K_G1 + 1]).then_inc(s.hT_done, 1)

            def queries(s, c, l):
                p = 2 * c + l
                act.wait_ge(s.q_mm, p + 1)
                for r in range(R):
                    last = nc.scalar.activation(s.Qm[:, :, r, :], groups(s.S2[0][:, 0:CT]), ACT.Identity,
                                                bias=blocks[l].bqm[:, r:r + 1], scale=head_mask[:, r:r + 1])
                last.then_inc(s.qm_done, 1)

            def keys(s, c, l):
                k = blocks[l].col + K_BK
                act.wait_ge(s.k_mm, 2 * c + l + 1)
                for g in range(R):
                    q = slice(32 * g, 32 * g + 32)
                    last = nc.scalar.activation(s.Km[q, :, g, :], groups(s.S2[1][q, 0:CT]), ACT.Identity,
                                                bias=cols[q, k:k + 1])
                last.then_inc(s.kv_act, 1)

            def values_spread(s, c, l):
                act.wait_ge(s.v_mm, 2 * c + l + 1)
                for j in range(2):
                    src = s.S2[0][32 * j:32 * j + 32, 0:CT].rearrange("p (t g r d) -> p t g r d", t=T, g=R, r=R)
                    for r in range(R):
                        dst = s.Vm[32 * r:32 * r + 32, :, :].rearrange(
                            "p (t j) (g r d) -> p t j g r d", j=R, g=R, r=R)
                        last = nc.scalar.activation(dst[:, :, j, :, r, :], src[:, :, :, r, :], ACT.Copy)
                last.then_inc(s.kv_act, 1)

            def exps(s, c, l, t):
                n = (2 * c + l) * T + t
                if l == 0:
                    act.wait_ge(s.s_free, n + 1)
                else:
                    act.wait_ge(s.sub_pool if t < 2 else s.sub_dve, 2 * c + t % 2 + 1)
                nc.scalar.activation(s.Ex[:, t, :], s.Ex[:, t, :], ACT.Exp).then_inc(s.ex_done, 1)

            def context(s, c, l):
                p = 2 * c + l
                act.wait_ge(s.pv_mm, (p + 1) * T)
                nc.scalar.activation(s.ctxT[:], s.P0, ACT.Copy).then_inc(s.ctx_done, 1)

            def norm2_out(s, c, l):
                col = blocks[l].col
                act.wait_ge(s.turned, 4 * c + 2 * l + 2)
                nc.scalar.activation(s.hT[:], s.P0, ACT.Identity, bias=cols[:, col + K_BETA2:col + K_BETA2 + 1],
                                     scale=cols[:, col + K_G2:col + K_G2 + 1]).then_inc(s.h2T_done, 1)

            def gelu(s, c, l, k):
                at = blocks[l].col + K_B1 + k
                act.wait_ge(s.f_mm, (2 * c + l) * FC + k + 1)
                nc.scalar.activation(s.fT[:, k, :], s.S2[k % 2][:, 0:CT], ACT.Gelu if l == 0 else ACT.Gelu_apprx_sigmoid,
                                     bias=cols[:, at:at + 1]).then_inc(s.f_done, 1)

            def adapter_in(s, c):
                act.wait_ge(s.y_turned, c + 1)
                nc.scalar.activation(s.yT[:], s.P0, ACT.Copy).then_inc(s.yT_done, 1)

            def adapter_gelu(s, c):
                act.wait_ge(s.down_mm, c + 1)
                nc.scalar.activation(s.hid[:], s.P1, ACT.Gelu, bias=cols[:, K_DOWN:K_DOWN + 1]).then_inc(s.hid_done, 1)

            def joint(first, second, head, late, setup):
                early = head and head[2] == 0
                if second:
                    norm2_out(*second)
                    for k in range(FC):
                        gelu(*second, k)
                if setup == 1:
                    mask()
                if first:
                    exps(*first, 0)
                    exps(*first, 1)
                if early and second:
                    norm_out(*head)
                if first:
                    exps(*first, 2)
                    exps(*first, 3)
                if early and not second:
                    norm_out(*head)
                    if setup == 1:
                        sines()
                if early:
                    queries(*head)
                    act.wait_ge(head[0].zeroed, 1)
                    keys(*head)
                if early and (second or not first):
                    values_spread(*head)
                if first:
                    context(*first)
                if late:
                    apply3(*late)
                if second and second[2] == 1:
                    adapter_in(*second[:2])
                    adapter_gelu(*second[:2])
                if early and first and not second:
                    values_spread(*head)
                if head and head[2] == 1:
                    queries(*head)
                    keys(*head)
                    values_spread(*head)

            def sines():
                act.wait_ge(arg_done, 1)
                nc.scalar.activation(trig[:], arg[:], ACT.Sin).then_inc(trig_done, 1)
                act.wait_ge(trig_done, 1)
                nc.scalar.activation(emb[:], trig[:, 4 * TILES:], ACT.Silu).then_inc(emb_done, 1)

            def mask():
                act.wait_ge(ld_mask, 16)
                nc.scalar.activation(maskb[:].rearrange("p n k -> p (n k)"), mask4[:].bitcast(U8), ACT.Copy,
                                     scale=NEG).then_inc(maskb_done, 1)

            act.wait_ge(ld_const, 32)
            for b in blocks:
                act.wait_ge(b.bqm_done, 1)
            run(joint, act.Fori, even, odd)

        @block.vector
        def _(dve):
            steps = [0]

            def link(ins):
                steps[0] += 1
                ins.then_inc(chain, 1)
                dve.wait_ge(chain, steps[0])

            def norm_stats(norm, src, k):
                for t in range(T):
                    nc.vector.bn_stats(norm.stats[:, t, :], src[:, t, :])
                wait(dve, norm.xh_done, k)
                dve.drain()
                for t in range(T):
                    last = nc.vector.bn_aggr(norm.mv[:, t, :], norm.stats[:, t, :])
                last.then_inc(norm.mv_done, 1)

            def norm_apply(s, src, k):
                dve.wait_ge(s.norm.rstd_done, k + 1)
                wait(dve, s.turned, k)
                for t in range(T):
                    last = nc.vector.tensor_scalar(s.xh[:, t, :], src[:, t, :], s.norm.mv[:, t, 0:1],
                                                   s.norm.rstd[:, t:t + 1], ALU.subtract, ALU.mult)
                last.then_inc(s.norm.xh_done, 1)

            def apply1(s, c, l):
                norm_apply(s, s.xo if l else s.x, 4 * c + 2 * l)

            def apply2(s, c, l):
                norm_apply(s, s.x1, 4 * c + 2 * l + 1)

            def stats1(s, c, l):
                if l == 0:
                    dve.wait_ge(s.ld_x, 16 * (c + 1))
                    nc.vector.tensor_copy(s.gate_kept[:], s.gate).then_inc(s.gate_done, 1)
                    norm_stats(s.norm, s.x, 4 * c)
                else:
                    dve.wait_ge(s.xo_done, 2 * c + 1)
                    norm_stats(s.norm, s.xo, 4 * c + 2)

            def modulate(s, c):
                wait(dve, s.rs4_done, 2 * c)
                nc.vector.tensor_copy(s.tab[:], tabs[:, bass.ds(2 * c + s.number, 1), :].rearrange(
                    "p o n -> p (o n)")).then_inc(s.tab_done, 1)
                dve.wait_ge(s.tab_done, c + 1)
                dve.wait_ge(s.turned, 4 * c + 3)
                nc.vector.tensor_tensor(groups(s.xm[:]), groups(s.P0), spread(s.tab[:, T_SCALE:T_SCALE + CB], CB, S),
                                        ALU.mult).then_inc(s.xm_done, 1)
                dve.wait_ge(s.xm_done, c + 1)
                nc.vector.tensor_tensor(groups(s.hT[:]), groups(s.xm[:]), spread(s.tab[:, T_SHIFT:T_SHIFT + CB], CB, S),
                                        ALU.add).then_inc(s.hT_done, 1)

            def values_spread(s, c, l):
                dve.wait_ge(s.v_mm, 2 * c + l + 1)
                for j in range(2, R):
                    src = s.S2[0][32 * j:32 * j + 32, 0:CT].rearrange("p (t g r d) -> p t g r d", t=T, g=R, r=R)
                    for r in range(R):
                        dst = s.Vm[32 * r:32 * r + 32, :, :].rearrange(
                            "p (t j) (g r d) -> p t j g r d", j=R, g=R, r=R)
                        last = nc.vector.tensor_copy(dst[:, :, j, :, r, :], src[:, :, :, r, :])
                last.then_inc(s.v_dve, 1)

            def row_max(s, c, l, t):
                n = (2 * c + l) * T + t
                bank = s.S2[(t + 1) % 2]
                dve.wait_ge(s.sc_mm, n + 1)
                if l == 0:
                    nc.vector.tensor_reduce(s.mx[:, t, :], groups(bank[:]), AX, ALU.max).then_inc(s.mx_done, 1)
                    dve.wait_ge(s.mx_done, n + 1)
                    nc.vector.tensor_tensor(groups(s.Ex[:, t, :]), groups(bank[:]), spread(s.mx[:, t, :], R * R, S),
                                            ALU.subtract).then_inc(s.s_free, 1)
                else:
                    dve.wait_ge(ld_bias[t], (2 * c + s.number + 1) * 16)
                    nc.vector.tensor_tensor(s.Ex[:, t, :], bank[:], bias[:, t, :], ALU.add).then_inc(s.s_free, 1)
                    dve.wait_ge(s.s_free, n + 1)
                    nc.vector.tensor_reduce(s.mx[:, t, :], groups(s.Ex[:, t, :]), AX, ALU.max).then_inc(s.mx_done, 1)
                    if t >= 2:
                        dve.wait_ge(s.mx_done, n + 1)
                        nc.vector.tensor_tensor(groups(s.Ex[:, t, :]), groups(s.Ex[:, t, :]),
                                                spread(s.mx[:, t, :], R * R, S), ALU.subtract).then_inc(s.sub_dve, 1)

            def row_sum(s, c, l, t):
                n = (2 * c + l) * T + t
                dve.wait_ge(s.ex_done, n + 1)
                nc.vector.tensor_reduce(s.sm[:, t, :], groups(s.Ex[:, t, :]), AX, ALU.add).then_inc(s.sm_done, 1)
                dve.wait_ge(s.sm_done, n + 1)
                nc.vector.reciprocal(s.rc[:, t, :], s.sm[:, t, :]).then_inc(s.rc_done, 1)

            def turn_probs(s, c, l, t):
                n = (2 * c + l) * T + t
                dve.wait_ge(s.pn_done, n + 1)
                wait(dve, s.pv_mm, two_ago(n, t))
                nc.vector.transpose(s.PT[:, t % 2, :], s.Ex[:, t, :]).then_inc(s.pt_done, 1)

            def after_attention(s, c, l):
                dve.wait_ge(s.o_mm, 2 * c + l + 1)
                if l == 0:
                    dve.wait_ge(s.xb_done, c + 1)
                    wait(dve, s.rest1_done, c)
                    nc.vector.tensor_tensor(s.x1[:], tiled(s.P1), s.xb[:], ALU.add).then_inc(s.x1_done, 1)
                else:
                    dve.wait_ge(s.rest0_done, 4 * c + 4)
                    nc.vector.tensor_tensor(s.x1[:], tiled(s.P1), over_tiles(blocks[1].bo[:]),
                                            ALU.add).then_inc(s.x1_done, 1)
                dve.wait_ge(s.x1_done, 2 * c + l + 1)
                norm_stats(s.norm, s.x1, 4 * c + 2 * l + 1)

            def block_out(s, c, l):
                dve.wait_ge(s.y_mm, 2 * c + l + 1)
                if l == 0:
                    dve.wait_ge(s.gate_done, c + 1)
                    dve.wait_ge(s.rest0_done, 4 * c + 4)
                    wait(dve, s.rs4_done, 2 * c)
                    for t in range(T):
                        last = nc.vector.scalar_tensor_tensor(
                            s.xo[:, t, :], s.P1[:, t * P:(t + 1) * P], s.gate_kept[:, t:t + 1],
                            s.rest[:, t, :], ALU.mult, ALU.add)
                    last.then_inc(s.xo_done, 1)
                else:
                    dve.wait_ge(s.rest1_done, c + 1)
                    nc.vector.tensor_tensor(s.xo[:], tiled(s.P1), s.rest[:], ALU.add).then_inc(s.xo_done, 1)
                    dve.wait_ge(s.xo_done, 2 * c + 2)
                    c4 = s.tab[:, T_COS:T_COS + 4 * T].rearrange("p (t o w) -> p t o w", o=1, w=4)
                    nc.vector.tensor_tensor(quads(s.rc4), quads(s.xo), c4.to_broadcast([P, T, D // 4, 4]),
                                            ALU.mult).then_inc(s.rc4_done, 1)

            def quads(buf):
                return buf[:].rearrange("p t (q w) -> p t q w", w=4)

            def rotate(s, c):
                dve.wait_ge(s.rc4_done, c + 1)
                dve.wait_ge(s.rs4_done, 2 * c + 2)
                wait(dve, s.yb_done, c)
                y_even, y_odd = pairs(s.y)
                c_even, c_odd = pairs(s.rc4)
                nc.vector.tensor_tensor(y_even, c_even, s.rs4[:, 0, :], ALU.add)
                nc.vector.tensor_tensor(y_odd, c_odd, s.rs4[:, 1, :], ALU.subtract).then_inc(s.rot_done, 1)

            def expert_tables(s, c):
                wait(dve, s.wblk_done, c)
                nc.vector.tensor_copy(s.etab[:], etabs[:, bass.ds(2 * c + s.number, 1), :].rearrange(
                    "p o n -> p (o n)")).then_inc(s.etab_done, 1)

            def expert_bias(s, c):
                dve.wait_ge(s.ex_mm, c + 1)
                for t in range(T):
                    last = nc.vector.scalar_tensor_tensor(
                        s.em[:, t, :], s.P0[:, t * P:(t + 1) * P], s.etab[:, E_BIAS + t:E_BIAS + t + 1],
                        block_mask, ALU.add, ALU.mult)
                last.then_inc(s.em_done, 1)

            def adapter_out(s, c):
                dve.wait_ge(s.up_mm, c + 1)
                dve.wait_ge(s.yb_done, c + 1)
                nc.vector.tensor_tensor(s.z[:], tiled(s.P1), s.yb[:], ALU.add).then_inc(s.z_done, 1)
                dve.wait_ge(s.z_done, c + 1)
                norm_stats(s.norm3, s.z, c)

            def last_out(s, c):
                dve.wait_ge(s.norm3.xh_done, c + 1)
                nc.vector.tensor_tensor(s.og[:], s.z[:], over_tiles(rows[:, R_LNG:R_LNG + D]), ALU.mult).then_inc(s.og_done, 1)
                dve.wait_ge(s.og_done, c + 1)
                nc.vector.tensor_tensor(s.ob, s.og[:], over_tiles(rows[:, R_LNB:R_LNB + D]), ALU.add).then_inc(s.ob_done, 1)

            def fold_bo(b, bank, row):
                dve.wait_ge(ld_rows, 16)
                dve.wait_ge(b.bo_mm, 1)
                nc.vector.tensor_tensor(b.bo[:], bank[:, 0:D], rows[:, row:row + D], ALU.add).then_inc(b.bo_done, 1)

            def joint(first, second, head, late, setup):
                l3 = second and second[2] == 1
                early = head and head[2] == 0
                after = head and head[2] == 1
                if early:
                    stats1(*head)
                if first:
                    row_max(*first, 1)
                if early:
                    apply1(*head)
                if setup == 0:
                    angles()
                    fold_bo(blocks[0], odd.S2[0], R_BO0)
                if first:
                    row_max(*first, 2)
                if late:
                    expert_bias(*late)
                if first:
                    row_max(*first, 3)
                if first:
                    row_sum(*first, 0)
                    row_sum(*first, 1)
                if first and not after:
                    row_sum(*first, 2)
                if setup == 1:
                    fold_bo(blocks[1], odd.S2[1], R_BO1)
                if second and after:
                    block_out(*second)
                if after:
                    stats1(*head)
                    row_sum(*first, 2)
                    apply1(*head)
                if first and not after:
                    row_sum(*first, 3)
                if first:
                    turn_probs(*first, 0)
                    turn_probs(*first, 1)
                if after:
                    row_sum(*first, 3)
                if second and not after:
                    block_out(*second)
                    if l3:
                        expert_tables(*second[:2])
                if late:
                    adapter_out(*late)
                if first:
                    turn_probs(*first, 2)
                    turn_probs(*first, 3)
                if l3:
                    rotate(*second[:2])
                if early and (second or not first):
                    dve.wait_ge(head[0].zeroed, 1)
                    values_spread(*head)
                if after:
                    modulate(*head[:2])
                if first:
                    after_attention(*first)
                if setup == 1:
                    tables()
                if first:
                    apply2(*first)
                if early and first and not second:
                    dve.wait_ge(head[0].zeroed, 1)
                    values_spread(*head)
                if after:
                    values_spread(*head)
                if head:
                    row_max(*head, 0)
                if setup == 3:
                    expert_weights()
                if late and not first and not second:
                    last_out(*late)

            def angles():
                dve.wait_ge(ld_ids, 16)
                dve.wait_ge(ld_toks, 16)
                link(nc.vector.tensor_copy(tf[:, 0, :], ids[:, TILES:]))
                link(nc.vector.tensor_scalar(tf[:, 1, :], tf[:, 0, :], 0.01, None, ALU.mult))
                link(nc.vector.tensor_scalar(tf[:, 2, :], tf[:, 1, :], 4097.0, None, ALU.mult))
                link(nc.vector.tensor_tensor(tf[:, 3, :], tf[:, 2, :], tf[:, 1, :], ALU.subtract))
                link(nc.vector.tensor_tensor(tf[:, 4, :], tf[:, 2, :], tf[:, 3, :], ALU.subtract))
                link(nc.vector.tensor_tensor(tf[:, 5, :], tf[:, 1, :], tf[:, 4, :], ALU.subtract))
                link(nc.vector.scalar_tensor_tensor(tf[:, 6, :], tf[:, 4, :], -100.0, tf[:, 0, :], ALU.mult, ALU.add))
                link(nc.vector.scalar_tensor_tensor(tf[:, 7, :], tf[:, 5, :], -100.0, tf[:, 6, :], ALU.mult, ALU.add))
                link(nc.vector.scalar_tensor_tensor(tf[:, 2, :], tf[:, 7, :], 0.01, tf[:, 1, :], ALU.mult, ALU.add))
                link(nc.vector.tensor_scalar(tf[:, 3, :], tf[:, 2, :], 4000.0, None, ALU.mult))
                nc.vector.tensor_copy(ang[:, 0:2 * TILES], toks[:])
                link(nc.vector.tensor_scalar(ang[:, 2 * TILES:], tf[:, 3, :], const[:, C_FREQ:C_FREQ + 1], None, ALU.mult))
                link(nc.vector.tensor_scalar(ang_k[:, 0, :], ang[:], 1.0 / TWO_PI, ROUND, ALU.mult, ALU.add))
                link(nc.vector.tensor_scalar(ang_k[:, 1, :], ang_k[:, 0, :], -ROUND, None, ALU.add))
                link(nc.vector.scalar_tensor_tensor(ang_r[:, 0, :], ang_k[:, 1, :], -PI_A, ang[:], ALU.mult, ALU.add))
                link(nc.vector.scalar_tensor_tensor(ang_r[:, 1, :], ang_k[:, 1, :], -PI_B, ang_r[:, 0, :], ALU.mult, ALU.add))
                link(nc.vector.scalar_tensor_tensor(ang_r[:, 2, :], ang_k[:, 1, :], -PI_C, ang_r[:, 1, :], ALU.mult, ALU.add))
                link(nc.vector.tensor_scalar(ang_r[:, 3, :], ang_r[:, 2, :], -PI_MAX, PI_MAX, ALU.max, ALU.min))
                nc.vector.tensor_scalar(arg[:, 0:2 * TILES], ang_r[:, 3, 0:2 * TILES], 1.0, None, ALU.mult)
                link(nc.vector.scalar_tensor_tensor(ang_r[:, 0, :], ang_r[:, 3, :], -1.0, ang_r[:, 3, :], ALU.mult, ALU.max))
                nc.vector.tensor_scalar(arg[:, 2 * TILES:4 * TILES], ang_r[:, 0, 0:2 * TILES], -1.0, TWO_PI / 4,
                                        ALU.mult, ALU.add)
                link(nc.vector.tensor_scalar(emb_abs[:], ang_r[:, 0, 2 * TILES:], const[:, C_COSM:C_COSM + 1],
                                             const[:, C_COSA:C_COSA + 1], ALU.mult, ALU.add))
                nc.vector.scalar_tensor_tensor(arg[:, 4 * TILES:], ang_r[:, 3, 2 * TILES:], const[:, C_SIN:C_SIN + 1],
                                               emb_abs[:], ALU.mult, ALU.add).then_inc(arg_done, 1)
                link(nc.vector.tensor_copy(idf[:, 0, :], ids[:, 0:TILES]))
                link(nc.vector.tensor_scalar(idf[:, 1, :], idf[:, 0, :], 0.0, float(E - 1), ALU.max, ALU.min))
                nc.vector.tensor_scalar(idx[:], idf[:, 1, :], float(A), const[:, C_OUT:C_OUT + 1],
                                        ALU.mult, ALU.add).then_inc(idx_done, 1)
                link(nc.vector.tensor_tensor(idf[:, 2, :], idf[:, 1, :], idf[:, 0, :], ALU.is_equal))
                nc.vector.tensor_scalar(idf[:, 3, :], idf[:, 2, :], -1.0, 1.0, ALU.mult, ALU.add).then_inc(idf_done, 1)

            def tables():
                dve.wait_ge(trig_done, 1)
                sines = trig[:, 0:2 * TILES].rearrange("p (w t) -> p t w", w=2)
                cosines = trig[:, 2 * TILES:4 * TILES].rearrange("p (w t o) -> p t w o", w=2, o=1)
                for c in range(CH):
                    tiles = slice(c * T, (c + 1) * T)
                    nc.vector.tensor_copy(tabs[:, c, T_SIN:T_SIN + 2 * T].rearrange("p (t w) -> p t w", w=2), sines[:, tiles, :])
                    nc.vector.tensor_copy(
                        tabs[:, c, T_COS:T_COS + 4 * T].rearrange("p (t w e) -> p t w e", w=2, e=2),
                        cosines[:, tiles, :, :].to_broadcast([P, T, 2, 2]))
                dve.wait_ge(ada_mm, 1)
                chunks = odd.P1[:, 0:2 * B].rearrange("p (w c n) -> p w c n", w=2, c=CH)
                nc.vector.tensor_scalar(tabs[:, :, T_SCALE:T_SCALE + CB], chunks[:, 0], cols[:, K_ADA:K_ADA + 1], 1.0, ALU.add, ALU.add)
                nc.vector.tensor_scalar(tabs[:, :, T_SHIFT:T_SHIFT + CB], chunks[:, 1], cols[:, K_ADA + 1:K_ADA + 2], None,
                                        ALU.add).then_inc(ada_done, 1)

            def expert_weights():
                dve.wait_ge(selected, 1)
                nc.vector.tensor_tensor(etabs[:, :, E_BIAS:E_BIAS + T], bsel[:].rearrange("p (c t) -> p c t", c=CH),
                                        got[:, :, A + 1].rearrange("p (c t) -> p c t", c=CH), ALU.add)
                for c in range(CH):
                    last = nc.vector.transpose(etabs[:, c, E_W:], wsel[:, 0, c * T:(c + 1) * T, :].rearrange("p t a -> p (t a)"))
                last.then_inc(tables_done, 1)
                dve.wait_ge(tables_done, 1)

            dve.wait_ge(ld_const, 32)
            nc.vector.tensor_copy(identb[:], ident)
            nc.vector.tensor_copy(causalb[:], const[:, C_CAUSAL:C_CAUSAL + S]).then_inc(consts_b, 1)
            for b in blocks:
                nc.vector.tensor_scalar(b.bqm[:], head_mask, cols[:, b.col + K_BQ:b.col + K_BQ + 1], None,
                                        ALU.mult).then_inc(b.bqm_done, 1)
                nc.vector.tensor_scalar(b.bvb[:], ident, 0.0, cols[:, b.col + K_BV:b.col + K_BV + 1],
                                        ALU.mult, ALU.add).then_inc(b.bqm_done, 1)
            run(joint, dve.Fori, even, odd)

        @block.gpsimd
        def _(pool):
            def norm_rstd(norm, k):
                pool.wait_ge(norm.mv_done, k + 1)
                wait(pool, norm.xh_done, k)
                nc.gpsimd.tensor_tensor(norm.ve[:], norm.mv[:, :, 1], eps[:], ALU.add).then_inc(norm.ve_done, 1)
                pool.wait_ge(norm.ve_done, k + 1)
                nc.gpsimd.tensor_tensor(norm.rstd[:], norm.ve[:], mhalf[:], ALU.pow).then_inc(norm.rstd_done, 1)

            def norm3_shift(s, c):
                norm_rstd(s.norm3, c)
                nc.gpsimd.tensor_tensor(s.nm[:], zero[:], s.norm3.mv[:, :, 0], ALU.subtract).then_inc(s.nm_done, 1)
                pool.wait_ge(s.nm_done, c + 1)
                pool.wait_ge(s.norm3.rstd_done, c + 1)
                nc.gpsimd.tensor_tensor(s.shift[:], s.nm[:], s.norm3.rstd[:], ALU.mult).then_inc(s.shift_done, 1)

            def subtract_max(s, c, l, t):
                pool.wait_ge(s.mx_done, (2 * c + 1) * T + t + 1)
                nc.gpsimd.tensor_tensor(groups(s.Ex[:, t, :]), groups(s.Ex[:, t, :]), spread(s.mx[:, t, :], R * R, S),
                                        ALU.subtract).then_inc(s.sub_pool, 1)

            def probabilities(s, c, l, t):
                n = (2 * c + l) * T + t
                pool.wait_ge(s.rc_done, n + 1)
                nc.gpsimd.tensor_tensor(groups(s.Ex[:, t, :]), groups(s.Ex[:, t, :]), spread(s.rc[:, t, :], R * R, S),
                                        ALU.mult).then_inc(s.pn_done, 1)

            def residual(s, c):
                pool.wait_ge(s.ld_x, 16 * (c + 1))
                pool.wait_ge(blocks[0].bo_done, 1)
                wait(pool, s.x1_done, 2 * c)
                nc.gpsimd.tensor_tensor(s.xb[:], s.x, over_tiles(blocks[0].bo[:]), ALU.add).then_inc(s.xb_done, 1)

            def rest(s, c, l, step):
                if l == 1:
                    if step == 0:
                        pool.wait_ge(s.x1_done, 2 * c + 2)
                        pool.wait_ge(s.xo_done, 2 * c + 1)
                        nc.gpsimd.tensor_tensor(s.rest[:], s.x1[:], over_tiles(rows[:, R_B21:R_B21 + D]),
                                                ALU.add).then_inc(s.rest1_done, 1)
                    return
                if step == 0:
                    pool.wait_ge(s.x1_done, 2 * c + 1)
                    wait(pool, s.xo_done, 2 * c)
                    nc.gpsimd.tensor_tensor(s.rest[:], s.x1[:], over_tiles(rows[:, R_B20:R_B20 + D]),
                                            ALU.add).then_inc(s.rest0_done, 1)
                else:
                    pool.wait_ge(s.rest0_done, 4 * c + step)
                if step == 1:
                    nc.gpsimd.tensor_tensor(s.rest[:], s.rest[:], s.x, ALU.subtract).then_inc(s.rest0_done, 1)
                if step == 2:
                    nc.gpsimd.tensor_tensor(s.rest[:], s.rest[:], spread(s.gate, T, D), ALU.mult).then_inc(s.rest0_done, 1)
                if step == 3:
                    nc.gpsimd.tensor_tensor(s.rest[:], s.rest[:], s.x, ALU.add).then_inc(s.rest0_done, 1)

            def rotate(s, c):
                pool.wait_ge(s.xo_done, 2 * c + 2)
                wait(pool, s.stored, 16 * c)
                v = s.xo[:].rearrange("p t (q w e) -> p t q w e", w=2, e=2)
                s2 = s.tab[:, T_SIN:T_SIN + 2 * T].rearrange("p (t o w) -> p t o w", o=1, w=2).to_broadcast([P, T, D // 4, 2])
                for e in range(2):
                    o = s.rs4[:, e, :].rearrange("p (t q w) -> p t q w", t=T, w=2)
                    nc.gpsimd.tensor_tensor(o, v[:, :, :, :, 1 - e], s2, ALU.mult).then_inc(s.rs4_done, 1)

            def residual_y(s, c):
                pool.wait_ge(s.rot_done, c + 1)
                wait(pool, s.z_done, c)
                nc.gpsimd.tensor_tensor(s.yb[:], s.y[:], over_tiles(rows[:, R_UP:R_UP + D]), ALU.add).then_inc(s.yb_done, 1)

            def expert_blocks(s, c):
                pool.wait_ge(s.etab_done, c + 1)
                wait(pool, s.ex_mm, c)
                w = s.etab[:, E_W:E_W + T * A].rearrange("p (t o a) -> p t o a", o=1, a=A).to_broadcast([P, T, R, A])
                m = block_mask.rearrange("p (o j a) -> p o j a", o=1, a=A).to_broadcast([P, T, R, A])
                nc.gpsimd.tensor_tensor(s.wblk[:].rearrange("p t (j a) -> p t j a", a=A), w, m,
                                        ALU.mult).then_inc(s.wblk_done, 1)

            def norm3_out(s, c):
                pool.wait_ge(s.norm3.xh_done, c + 1)
                nc.gpsimd.tensor_tensor(s.og[:], s.z[:], over_tiles(rows[:, R_LNG:R_LNG + D]), ALU.mult).then_inc(s.og_done, 1)
                pool.wait_ge(s.og_done, c + 1)
                nc.gpsimd.tensor_tensor(s.ob, s.og[:], over_tiles(rows[:, R_LNB:R_LNB + D]), ALU.add).then_inc(s.ob_done, 1)

            def expert_weights():
                pool.wait_ge(idf_done, 1)
                pool.wait_ge(gathered, 16 * TILES)
                eye = const[:, C_EYE:C_EYE + A].rearrange("p (o a) -> p o a", o=1).to_broadcast([P, TILES, A])
                nc.gpsimd.tensor_tensor(wsel[:, 0, :, :], got[:, :, 0:A], spread(idf[:, 2, :], TILES, A), ALU.mult)
                nc.gpsimd.tensor_tensor(wsel[:, 1, :, :], eye, spread(idf[:, 3, :], TILES, A), ALU.mult).then_inc(wsel_done, 1)
                nc.gpsimd.tensor_tensor(bsel[:], got[:, :, A], idf[:, 2, :], ALU.mult)
                pool.wait_ge(wsel_done, 1)
                nc.gpsimd.tensor_tensor(wsel[:, 0, :, :], wsel[:, 0, :, :], wsel[:, 1, :, :], ALU.add).then_inc(selected, 1)

            def gather(lo, hi):
                for t in range(lo, hi):
                    nc.gpsimd.indirect_dma_start(got[:, t, :], None, etab_in,
                                                 bass.IndirectOffsetOnAxis(ap=idx[:, t:t + 1], axis=0)).then_inc(gathered, 16)

            def joint(first, second, head, late, setup):
                l3 = second and second[2] == 1
                early = head and head[2] == 0
                if setup == 0:
                    norm_rstd(head[0].norm, 0)
                    gpsimd_zero(odd)
                    residual(*head[:2])
                    pool.wait_ge(ld_rows, 16)
                    pool.wait_ge(idx_done, 1)
                    gather(0, 2)
                    return
                if early and not second:
                    norm_rstd(head[0].norm, 4 * head[1])
                if first and first[2] == 1:
                    subtract_max(*first, 0)
                if second:
                    for step in range(4):
                        rest(*second, step)
                if early and second:
                    norm_rstd(head[0].norm, 4 * head[1])
                if first and first[2] == 1:
                    subtract_max(*first, 1)
                if setup == 1:
                    gather(2, 4)
                if setup == 2:
                    gather(9, TILES)
                if setup == 3:
                    expert_weights()
                for t in range(T):
                    if first:
                        probabilities(*first, t)
                    if head and head[2] == 1 and t == 1:
                        norm_rstd(head[0].norm, 4 * head[1] + 2)
                if l3:
                    rotate(*second[:2])
                if late:
                    norm3_shift(*late)
                if setup == 1:
                    gather(4, 9)
                if early:
                    residual(*head[:2])
                if l3:
                    residual_y(*second[:2])
                    expert_blocks(*second[:2])
                if first:
                    norm_rstd(first[0].norm, 4 * first[1] + 2 * first[2] + 1)
                if late and (first or second):
                    norm3_out(*late)

            def gpsimd_zero(s):
                nc.gpsimd.memset(s.Km[:], 0.0)
                nc.gpsimd.memset(s.Vm[:], 0.0).then_inc(s.zeroed, 1)

            nc.gpsimd.memset(eps[:], EPS)
            nc.gpsimd.memset(zero[:], 0.0)
            nc.gpsimd.memset(mhalf[:], -0.5).then_inc(mhalf_done, 1)
            gpsimd_zero(even)
            pool.wait_ge(mhalf_done, 1)
            run(joint, pool.Fori, even, odd)


def constants():
    c = np.zeros((P, N_CONST), np.float32)
    p = np.arange(P)
    c[:, C_IDENT:C_IDENT + P] = np.eye(P)
    c[:, C_BLOCK:C_BLOCK + P] = p[:, None] // S == p[None, :] // S
    c[:, C_CAUSAL:C_CAUSAL + S] = np.where(np.arange(S)[None, :] > (p % S)[:, None], NEG, 0.0)
    c[:, C_EYE:C_EYE + A] = (p % A)[:, None] == np.arange(A)[None, :]
    c[:, C_HEAD:C_HEAD + R] = ((p // DH % R)[:, None] == np.arange(R)[None, :]) / np.sqrt(DH)
    half = D // 2
    freq = np.exp(np.arange(half, dtype=np.float32) * np.float32(-np.log(10000.0) / (half - 1)))
    c[:, C_FREQ] = np.concatenate([freq, freq])
    c[:, C_OUT] = p % A
    c[:, C_SIN] = p < half
    c[:, C_COSM] = -(p >= half).astype(np.float32)
    c[:, C_COSA] = (p >= half) * (np.pi / 2)
    return c


def kernel(**inputs):
    import concourse.bacc as bacc
    from concourse.bass_utils import run_bass_kernel_spmd

    v = {k: np.asarray(a) for k, a in inputs.items()}

    def block_weights(n):
        w2 = v[n + "W2"].reshape(FC, P, D).transpose(1, 0, 2).reshape(P, FC * D)
        return np.concatenate([v[n + "Wq"], v[n + "Wk"], v[n + "Wv"], v[n + "Wo"], v[n + "W1"], w2], axis=1)

    def block_columns(n, g, be):
        return [v[n + "bq"], v[n + "bk"], v[n + "bv"], v[n + g], v[n + be], *v[n + "b1"].reshape(FC, P)]

    def beside(rows):
        return np.broadcast_to(np.concatenate(rows)[None, :], (P, sum(len(r) for r in rows)))

    def of_token(a):
        return np.repeat(a.reshape(TILES, R), S, axis=1).T

    arrays = {
        "x_in": np.concatenate([v["x"].reshape(CH, T, P, D).transpose(2, 0, 1, 3).reshape(P, CH, CT),
                                of_token(v["condB_gatescore"]).reshape(P, CH, T)], axis=2).reshape(P, CH * (CT + T)),
        "bias_in": v["fside_Bx16xSxS_0"].reshape(B, R, R, S, S).transpose(2, 3, 0, 1, 4).reshape(P, B * R * S),
        "mask_in": np.tile(v["mask_Bx1xSxS_bk0"].reshape(B, S, S).transpose(1, 0, 2).reshape(S, B * S),
                           (R, 1)).view(np.int32),
        "w0_in": block_weights("L0_cond_"),
        "w1_in": block_weights("L1_cond_"),
        "wx_in": np.concatenate([v["L1_cond_W_ada"], np.tile(v["L3_cond_down_W"].T, (1, R)),
                                 np.tile(v["L3_cond_up_W"].T, (R, 1))], axis=1),
        "rows_in": beside([v["L0_cond_bo"], v["L0_cond_b2"], v["L1_cond_bo"], v["L1_cond_b2"],
                           v["L3_cond_up_b"], v["L3_cond_ln_gamma"], v["L3_cond_ln_beta"]]),
        "cols_in": np.stack(block_columns("L0_cond_", "gamma2", "beta2") + block_columns("L1_cond_", "g2", "beta2")
                            + [v["L0_cond_gamma1"], v["L0_cond_beta1"], *v["L1_cond_b_ada"].reshape(2, D),
                               np.tile(v["L3_cond_down_b"], R)], axis=1),
        "toks_in": np.concatenate([of_token(v["condB_theta"]), of_token(v["condB_phi"])], axis=1),
        "ids_in": np.concatenate([of_token(v["itok_B_0_15"]),
                                  np.broadcast_to(v["itok_B_34_63"][None, :], (P, B))], axis=1),
        "etab_in": np.concatenate([v["L3_cond_expert_W"].reshape(E * A, A), v["L3_cond_expert_b"].reshape(E * A, 1),
                                   v["L3_cond_domain_emb"].reshape(E * A, 1)], axis=1),
        "const_in": constants(),
    }
    arrays = {k: np.ascontiguousarray(a) for k, a in arrays.items()}
    nc = bacc.Bacc("TRN2", target_bir_lowering=False, num_devices=1)
    args = [nc.dram_tensor(k, a.shape, mybir.dt.from_np(a.dtype), kind="ExternalInput").ap()
            for k, a in arrays.items()]
    out = nc.dram_tensor("out", (P, TILES * D), F32, kind="ExternalOutput").ap()
    cond_seq_kernel(nc, *args, out)
    r = run_bass_kernel_spmd(nc, [arrays], core_ids=[0])
    got = r.results[0]["out"].reshape(P, TILES, D).transpose(1, 0, 2).reshape(B, S, D)
    return np.ascontiguousarray(got)
```
